# Optimizing a Trainium2 kernel written in Bass

```python
import numpy as np
import jax
import jax.numpy as jnp

def _softmax(x, axis=-1):
    return jax.nn.softmax(x, axis=axis)

def _gelu(x):
    return jax.nn.gelu(x, approximate=True)

def _silu(x):
    return jax.nn.silu(x)

def _sigmoid(x):
    return jax.nn.sigmoid(x)

def _layernorm(x, axis=-1, eps=1e-05):
    m = jnp.mean(x, axis=axis, keepdims=True)
    v = jnp.var(x, axis=axis, keepdims=True)
    return (x - m) / jnp.sqrt(v + eps)

def _scatter_add(tgt, idx, src, axis=0):
    return tgt.at[idx].add(src)

def _segment_sum(src, seg, n):
    return jax.ops.segment_sum(src, seg, n)
kernel_name = 'mk_gnn_preln_d2_gnn_r8_6e089a'

def setup_inputs(seed: int=0):
    np.random.seed(seed)
    _w = jnp.asarray

    def _rec_inputs():
        import jax
        import jax.numpy as jnp
        _gk = jax.random.key(seed)
        x = -0.0007083 + 1.001 * jax.random.normal(jax.random.fold_in(_gk, 1), (6250, 48), jnp.float32)
        src = jax.random.randint(jax.random.fold_in(_gk, 2), (200000,), 0, 6250, jnp.int32)
        dst = jax.random.randint(jax.random.fold_in(_gk, 3), (200000,), 0, 6250, jnp.int32)
        _o = jnp.argsort(dst, stable=True)
        src = src[_o]
        dst = dst[_o]
        edge_attr_40 = jax.random.uniform(jax.random.fold_in(_gk, 12), (200000, 40), jnp.float32, 0.0, 1)
        edge_weight = jax.random.uniform(jax.random.fold_in(_gk, 14), (200000,), jnp.float32, 0.0, 6.99999)
        node_type_119 = jax.random.randint(jax.random.fold_in(_gk, 15), (6250,), 0, 119, jnp.int32)
        node_vec = jax.random.uniform(jax.random.fold_in(_gk, 16), (6250,), jnp.float32, 0.0, 1.49999)
        return (x, src, dst, edge_attr_40, edge_weight, node_type_119, node_vec)
    x, src, dst, edge_attr_40, edge_weight, node_type_119, node_vec = _rec_inputs()

    def _L0_gnn_setup():
        import jax, jax.numpy as jnp
        import numpy as np
        CUTOFF = 6.0
        LN_EPS = 1e-05
        key = jax.random.key(seed)
        ks = jax.random.split(key, 16)
        N, E, H, R, NEL, G = (6250, 100000, 48, 40, 119, 32)
        inp = {'h': jax.random.normal(ks[0], (N, H), jnp.float32), 'edge_index': jax.random.randint(ks[1], (2, E), 0, N, jnp.int64), 'edge_attr': jax.random.uniform(ks[2], (E, R), jnp.float32), 'distances': jax.random.uniform(ks[3], (E,), jnp.float32) * 7.0, 'atom_z': jax.random.randint(ks[4], (N,), 0, NEL, jnp.int64), 'node_mult': jax.random.uniform(ks[5], (N,), jnp.float32) + 0.5, 'batch': jnp.zeros((N,), jnp.int64), 'W1': jax.random.normal(ks[6], (H, R), jnp.float32) / np.sqrt(R), 'b1': jax.random.normal(ks[7], (H,), jnp.float32) * 0.01, 'W2': jax.random.normal(ks[8], (H, H), jnp.float32) / np.sqrt(H), 'b2': jax.random.normal(ks[9], (H,), jnp.float32) * 0.01, 'emb': jax.random.normal(ks[10], (NEL, G), jnp.float32) * 0.01, 'adaptW': jax.random.normal(ks[11], (G, G), jnp.float32) * 0.01, 'gamma': jnp.ones((H,), jnp.float32), 'beta': jnp.zeros((H,), jnp.float32)}
        return inp
    _L0_gnn_all = _L0_gnn_setup()
    _L0_gnn_in = {k: v for k, v in _L0_gnn_all.items() if k in ('W1', 'b1', 'W2', 'b2', 'emb', 'adaptW', 'gamma', 'beta')}
    del _L0_gnn_all

    def _L1_gnn_setup():
        import jax, jax.numpy as jnp
        import numpy as np
        N = 12500
        E = 200000
        D = 48
        K = 5
        ALPHA = 0.8
        key = jax.random.key(seed)
        k1, k2 = jax.random.split(key)
        x = jax.random.normal(k1, (N, D), dtype=jnp.float32)
        edge_index = jax.random.randint(k2, (2, E), 0, N, dtype=jnp.int32)
        return {'x': x, 'edge_index': edge_index}
    _L1_gnn_all = _L1_gnn_setup()
    _L1_gnn_in = {k: v for k, v in _L1_gnn_all.items() if k in ()}
    del _L1_gnn_all
    return {'x': x, 'src': src, 'dst': dst, 'edge_attr_40': edge_attr_40, 'edge_weight': edge_weight, 'node_type_119': node_type_119, 'node_vec': node_vec, 'L0_gnn_W1': _L0_gnn_in['W1'], 'L0_gnn_b1': _L0_gnn_in['b1'], 'L0_gnn_W2': _L0_gnn_in['W2'], 'L0_gnn_b2': _L0_gnn_in['b2'], 'L0_gnn_emb': _L0_gnn_in['emb'], 'L0_gnn_adaptW': _L0_gnn_in['adaptW'], 'L0_gnn_gamma': _L0_gnn_in['gamma'], 'L0_gnn_beta': _L0_gnn_in['beta']}

def reference(x, src, dst, edge_attr_40, edge_weight, node_type_119, node_vec, L0_gnn_W1, L0_gnn_b1, L0_gnn_W2, L0_gnn_b2, L0_gnn_emb, L0_gnn_adaptW, L0_gnn_gamma, L0_gnn_beta):
    import jax
    import jax.numpy as jnp

    def _L0_gnn_ref(h, edge_index, edge_attr, distances, atom_z, node_mult, batch, W1, b1, W2, b2, emb, adaptW, gamma, beta):
        import jax, jax.numpy as jnp
        import numpy as np
        CUTOFF = 6.0
        LN_EPS = 1e-05
        src, dst = (edge_index[0], edge_index[1])
        N = h.shape[0]
        gate = jax.nn.silu(edge_attr @ W1.T + b1) @ W2.T + b2
        ei = emb[atom_z[src]]
        ej = emb[atom_z[dst]]
        adapt_logit = jnp.sum(ei * (ej @ adaptW.T), axis=-1, keepdims=True)
        gate = gate + adapt_logit
        cw = jnp.where(distances < CUTOFF, 0.5 * (jnp.cos(jnp.pi * distances / CUTOFF) + 1.0), 0.0)
        mj = node_mult[dst]
        msg = gate * h[dst] * (cw * mj)[:, None]
        agg = jax.ops.segment_sum(msg, src, num_segments=N)
        tot = jax.ops.segment_sum(mj, src, num_segments=N)
        agg = agg / jnp.clip(tot, 1e-08, None)[:, None]
        x = h + agg
        mu = jnp.mean(x, axis=-1, keepdims=True)
        var = jnp.mean(jnp.square(x - mu), axis=-1, keepdims=True)
        return (x - mu) / jnp.sqrt(var + LN_EPS) * gamma + beta

    def _L1_gnn_ref(x, edge_index):
        import jax, jax.numpy as jnp
        import numpy as np
        N = 12500
        E = 200000
        D = 48
        K = 5
        ALPHA = 0.8
        n = x.shape[0]
        loops = jnp.arange(n, dtype=edge_index.dtype)
        row = jnp.concatenate([edge_index[0], loops])
        col = jnp.concatenate([edge_index[1], loops])
        deg = jax.ops.segment_sum(jnp.ones(row.shape, x.dtype), col, num_segments=n)
        dinv = jnp.where(deg > 0, jax.lax.rsqrt(deg), jnp.zeros((), x.dtype))
        w = dinv[row] * dinv[col]

        def step(h, _):
            m = jax.ops.segment_sum(w[:, None] * h[row], col, num_segments=n)
            h = (1.0 - ALPHA) * m + ALPHA * x
            return (h, None)
        h, _ = jax.lax.scan(step, x, None, length=K)
        return h
    edge_index = jnp.stack([src, dst])
    batch0 = jnp.zeros((6250,), jnp.int32)
    h = jnp.maximum(_layernorm(x, axis=-1), 0.0)
    x = x + _L0_gnn_ref(h, edge_index, edge_attr_40, edge_weight, node_type_119, node_vec, batch0, L0_gnn_W1, L0_gnn_b1, L0_gnn_W2, L0_gnn_b2, L0_gnn_emb, L0_gnn_adaptW, L0_gnn_gamma, L0_gnn_beta)
    h = jnp.maximum(_layernorm(x, axis=-1), 0.0)
    x = x + _L1_gnn_ref(h, edge_index)
    return x

_drawn_inputs = setup_inputs


def setup_inputs(seed=0):
    import zlib

    import numpy as np

    out = dict(_drawn_inputs(seed))
    spreads = {'L0_gnn_gamma': (1.0, 0.2), 'L0_gnn_beta': (0.0, 0.1)}
    factors = {'edge_attr_40': 5.164,
     'edge_weight': 4.252,
     'node_vec': 5.912,
     'L0_gnn_b1': 185.517,
     'L0_gnn_b2': 64.0,
     'L0_gnn_emb': 64.0,
     'L0_gnn_adaptW': 64.0}
    for name, (base, spread) in spreads.items():
        noise = np.random.default_rng([zlib.crc32(name.encode()), seed]).standard_normal(out[name].shape)
        drawn = base * np.exp(spread * noise) if base else spread * noise
        out[name] = jnp.asarray(drawn.astype(out[name].dtype))
    for name, factor in factors.items():
        out[name] = (out[name] * factor).astype(out[name].dtype)
    return out
```

```python
from contextlib import ExitStack

import concourse.bass as bass
from concourse import mybir

F32 = mybir.dt.float32
BF16 = mybir.dt.bfloat16
I32 = mybir.dt.int32
I16 = mybir.dt.int16
ALU = mybir.AluOpType
ACT = mybir.ActivationFunctionType
AX = mybir.AxisListType

P = 128
N = 6250
E = 200000
H = 48
R = 40
NEL = 119
G = 32
TE = 125
LO = N // TE
HT = 8
HE = HT * TE
BT = 2 * HT
NB = E // (BT * TE)
T = E // TE
GW = H + 1 + NEL
ACC_ROWS = 6400
NTAB = HT
K = 5
ALPHA = 0.8
CUTOFF = 6.0
LN_EPS = 1e-5
PI = 3.141592653589793
ROUND = 12582912.0


def build(nc, x, src, dst, edge_attr, edge_weight, node_type, node_vec, W1, b1, W2, b2, emb, adaptW,
          gamma, beta, out):
    node_tab = nc.dram_tensor("node_tab", (N, GW), F32).ap()
    y_tab = nc.dram_tensor("y_tab", (N, H), F32).ap()
    logit_tab = nc.dram_tensor("logit_tab", (NEL, NEL), F32).ap()
    msg_acc = [nc.dram_tensor(f"msg_acc{i}", (ACC_ROWS, H + 1), F32).ap() for i in range(NTAB)]
    prop_acc = [nc.dram_tensor(f"prop_acc{i}", (ACC_ROWS, H), F32).ap() for i in range(NTAB)]
    src_rows = nc.dram_tensor("src_rows", (T, TE), I16).ap()
    dst_rows = nc.dram_tensor("dst_rows", (T, TE), I16).ap()
    hi_rows = nc.dram_tensor("hi_rows", (T, TE), BF16).ap()

    with ExitStack() as ctx:
        def sb(name, shape, dt=F32):
            return ctx.enter_context(nc.sbuf_tensor(name, shape, dt))

        def sem(name):
            return ctx.enter_context(nc.semaphore(name))

        part_idx = sb("part_idx", [P, 1])
        free_idx = sb("free_idx", [P, P])
        ident = sb("ident", [P, P])
        tri = sb("tri", [P, TE])
        trash = sb("trash", [P, 1])
        zeros = sb("zeros", [P, ACC_ROWS // P * (H + 1)])
        half_pi = sb("half_pi", [P, 1])
        eps = sb("eps", [P, 1])
        w1_pair = sb("w1_pair", [2 * R, 2 * H])
        w2_pair = sb("w2_pair", [2 * H + 1, 2 * H])
        b1_pair = sb("b1_pair", [2 * H, 1])
        emb_t = sb("emb_t", [G, NEL])
        adapt_t = sb("adapt_t", [G, G])
        gamma_b = sb("gamma_b", [P, H])
        beta_b = sb("beta_b", [P, H])
        q_t = sb("q_t", [G, NEL])
        logits = sb("logits", [NEL, NEL])
        xn = sb("xn", [TE, LO, H])
        hn = sb("hn", [TE, LO, H])
        mult = sb("mult", [TE, LO])
        ntype = sb("ntype", [P, LO], I32)
        ntype_bf = sb("ntype_bf", [TE, LO], BF16)
        stat = sb("stat", [TE, 4, LO])
        dinv = sb("dinv", [TE, LO])
        src_i = sb("src_i", [P, T], I32)
        dst_i = sb("dst_i", [P, T], I32)
        src_c = sb("src_c", [TE, T])
        dst_c = sb("dst_c", [TE, T])
        lo_c = sb("lo_c", [TE, T])
        cw_c = sb("cw_c", [TE, T])

        dve_step = sem("dve_step")
        steps = [0]

        def link(ins):
            steps[0] += 1
            ins.then_inc(dve_step, 1)
            nc.vector.wait_ge(dve_step, steps[0])

        def layer_norm(v, xin, y, sq):
            def bc(a):
                return a.unsqueeze(2).to_broadcast([TE, LO, H])
            link(v.tensor_reduce(stat[:, 0, :], xin, AX.X, ALU.add))
            link(v.tensor_scalar(stat[:, 1, :], stat[:, 0, :], 1.0 / H, None, ALU.mult))
            link(v.tensor_tensor(y, xin, bc(stat[:, 1, :]), ALU.subtract))
            link(v.tensor_tensor(sq, y, y, ALU.mult))
            link(v.tensor_reduce(stat[:, 2, :], sq, AX.X, ALU.add))
            link(v.tensor_scalar(stat[:, 0, :], stat[:, 2, :], 1.0 / H, LN_EPS, ALU.mult, ALU.add))
            v.sem_inc(root_asked, 1)
            roots[0] += 1
            v.wait_ge(root_done, roots[0])
            link(v.reciprocal(stat[:, 3, :], stat[:, 1, :]))
            link(v.tensor_tensor(y, y, bc(stat[:, 3, :]), ALU.mult))

        root_asked, root_done, roots = sem("root_asked"), sem("root_done"), [0]

        def root(a, n):
            a.wait_ge(root_asked, n)
            a.activation(stat[:, 1, :], stat[:, 0, :], ACT.Sqrt).then_inc(root_done, 1)

        with ExitStack() as setup:
            def ssb(name, shape, dt=F32):
                return setup.enter_context(nc.sbuf_tensor(name, shape, dt))

            sq = ssb("sq", [TE, LO, H])
            rows = ssb("rows", [TE, LO, GW])
            hi_c = ssb("hi_c", [TE, T])
            near = ssb("near", [TE, T])
            wt_c = ssb("wt_c", [TE, T])
            row_out = [ssb("src_out", [100, 16, TE], I16), ssb("dst_out", [100, 16, TE], I16),
                       ssb("hi_out", [100, 16, TE], BF16)]
            ps_row = setup.enter_context(nc.psum_tensor("ps_row", [P, 2, 4, P], F32))
            ps_q = setup.enter_context(nc.psum_tensor("ps_q", [P, 512], F32))
            ps_l = setup.enter_context(nc.psum_tensor("ps_l", [P, 512], F32))
            loaded_nodes, loaded_edges, loaded_weights = sem("loaded_nodes"), sem("loaded_edges"), sem("loaded_weights")
            consts, padded, qt_mm, qt_sb, logit_mm, logit_sb = (sem("consts"), sem("padded"), sem("qt_mm"), sem("qt_sb"),
                                                                sem("logit_mm"), sem("logit_sb"))
            logit_out, logit_rows, rows_ready, tables = sem("logit_out"), sem("logit_rows"), sem("rows_ready"), sem("tables")
            cols_ready, row_mm, row_copied, angle, sined = (sem("cols_ready"), sem("row_mm"), sem("row_copied"), sem("angle"),
                                                            sem("sined"))
            zeroed = sem("zeroed")
            rows_of = (src_c, dst_c, hi_c)
            WEIGHTS = 12
            with nc.allow_non_contiguous_dma(reason="weights of a few KB, transposed once"), nc.Block() as block:

                @block.sync
                def _(sp):
                    by_tile = "(b p i) -> p b i"
                    sp.wait_ge(padded, 3)
                    for a, t in ((dst, dst_i), (src, src_i)):
                        sp.dma_start(t[0:TE, :].rearrange("p (b i) -> p b i", i=BT),
                                     a.rearrange(by_tile, p=TE, i=BT)).then_inc(loaded_edges, 16)
                    sp.dma_start(wt_c[:, :].rearrange("p (b i) -> p b i", i=BT),
                                 edge_weight.rearrange(by_tile, p=TE, i=BT)).then_inc(loaded_edges, 16)
                    for c in range(16):
                        sp.wait_ge(row_copied, 3 * (c + 1))
                        for d, t in zip((src_rows, dst_rows, hi_rows), row_out):
                            sp.dma_start(d[100 * c:100 * c + 100, :], t[:, c, :]).then_inc(tables, 16)
                    sp.wait_ge(rows_ready, 1)
                    sp.wait_ge(logit_rows, 16 * LO)
                    sp.dma_start(node_tab.rearrange("(p j) f -> p j f", j=LO), rows[:, :, :]).then_inc(tables, 16)
                    sp.wait_ge(tables, 16 * 49)
                    sp.wait_ge(zeroed, 16 * 2 * NTAB)

                @block.gpsimd
                def _(p):
                    p.memset(src_i[:, :], 0).then_inc(padded, 1)
                    p.memset(dst_i[:, :], 0).then_inc(padded, 1)
                    p.memset(ntype[:, :], 0).then_inc(padded, 1)
                    p.iota(part_idx[:, :], [[0, 1]], 0, 1, allow_small_or_imprecise_dtypes=True)
                    p.iota(trash[:, :], [[0, 1]], N, 1, allow_small_or_imprecise_dtypes=True)
                    p.iota(free_idx[:, :], [[1, P]], 0, 0, allow_small_or_imprecise_dtypes=True).then_inc(consts, 1)
                    p.wait_ge(logit_out, 16)
                    p.wait_ge(loaded_nodes, 16 * 3)
                    for j in range(LO):
                        p.indirect_dma_start(rows[:, j, H + 1:GW], None, logit_tab,
                                             bass.IndirectOffsetOnAxis(ap=ntype[0:TE, j:j + 1], axis=0)
                                             ).then_inc(logit_rows, 16)

                @block.scalar
                def _(a):
                    a.wait_ge(padded, 3)
                    a.dma_start(xn[:, :, :], x.rearrange("(p j) f -> p j f", j=LO)).then_inc(loaded_nodes, 16)
                    a.dma_start(mult[:, :], node_vec.rearrange("(p j) -> p j", j=LO)).then_inc(loaded_nodes, 16)
                    a.dma_start(ntype[0:TE, :], node_type.rearrange("(p j) -> p j", j=LO)).then_inc(loaded_nodes, 16)
                    a.dma_start(emb_t[:, :], emb.rearrange("n g -> g n")).then_inc(loaded_weights, 16)
                    a.dma_start(adapt_t[:, :], adaptW.rearrange("i k -> k i")).then_inc(loaded_weights, 16)
                    a.wait_ge(consts, 2)
                    for s in range(2):
                        a.dma_start(w1_pair[R * s:R * s + R, H * s:H * s + H], W1.rearrange("h r -> r h")
                                    ).then_inc(loaded_weights, 16)
                        a.dma_start(w2_pair[H * s:H * s + H, H * s:H * s + H], W2.rearrange("o i -> i o")
                                    ).then_inc(loaded_weights, 16)
                        a.dma_start(w2_pair[2 * H:2 * H + 1, H * s:H * s + H], b2.unsqueeze(0)
                                    ).then_inc(loaded_weights, 16)
                        a.dma_start(b1_pair[H * s:H * s + H, :], b1.unsqueeze(1)).then_inc(loaded_weights, 16)
                    a.dma_start(gamma_b[:, :], gamma.partition_broadcast(P)).then_inc(loaded_weights, 16)
                    a.dma_start(beta_b[:, :], beta.partition_broadcast(P)).then_inc(loaded_weights, 16)
                    for t in msg_acc + prop_acc:
                        w = t.shape[1] * ACC_ROWS // P
                        a.dma_start(t.rearrange("(p r) f -> p (r f)", p=P), zeros[:, 0:w]).then_inc(zeroed, 16)
                    a.wait_ge(logit_sb, 1)
                    a.dma_start(logit_tab, logits[:, :]).then_inc(logit_out, 16)
                    a.wait_ge(angle, 1)
                    a.activation(near[:, :], wt_c[:, :], ACT.Sin, bias=half_pi[0:TE, :],
                                 scale=-PI / CUTOFF).then_inc(sined, 1)
                    root(a, 1)
                    a.wait_ge(loaded_weights, 16 * WEIGHTS)
                    a.wait_ge(logit_out, 16)

                @block.tensor
                def _(t):
                    t.wait_ge(loaded_weights, 16 * WEIGHTS)
                    t.matmul(ps_q[0:G, 0:NEL], adapt_t[:, :], emb_t[:, :], start=True, stop=True).then_inc(qt_mm, 1)
                    t.wait_ge(qt_sb, 1)
                    t.matmul(ps_l[0:NEL, 0:NEL], q_t[:, :], emb_t[:, :], start=True, stop=True).then_inc(logit_mm, 1)
                    t.wait_ge(cols_ready, 1)
                    for c in range(16):
                        if c >= 2:
                            t.wait_ge(row_copied, 3 * (c - 1))
                        for n, cols in enumerate(rows_of):
                            m = t.transpose(ps_row[0:100, c % 2, n, 0:TE], cols[:, 100 * c:100 * c + 100],
                                            ident[0:TE, 0:TE])
                        m.then_inc(row_mm, 1)

                @block.vector
                def _(v):
                    v.memset(zeros[:, :], 0.0)
                    v.memset(w1_pair[:, :], 0.0)
                    v.memset(w2_pair[:, :], 0.0)
                    v.memset(half_pi[:, :], PI / 2)
                    v.memset(eps[:, :], LN_EPS).then_inc(consts, 1)
                    v.wait_ge(consts, 2)
                    v.tensor_scalar(ident[:, :], free_idx[:, :], part_idx[:, 0:1], None, ALU.is_equal)
                    link(v.tensor_scalar(tri[:, :], free_idx[:, 0:TE], part_idx[:, 0:1], None, ALU.is_le))
                    v.wait_ge(loaded_edges, 16 * 3)
                    v.tensor_copy(src_c[:, :], src_i[0:TE, :])
                    link(v.tensor_copy(dst_c[:, :], dst_i[0:TE, :]))
                    link(v.tensor_scalar(near[:, :], src_c[:, :], (LO - 1) / 2, 1.0 / LO, ALU.subtract, ALU.mult))
                    link(v.tensor_scalar(hi_c[:, :], near[:, :], ROUND, ROUND, ALU.add, ALU.subtract))
                    link(v.scalar_tensor_tensor(lo_c[:, :], hi_c[:, :], -float(LO), src_c[:, :], ALU.mult, ALU.add))
                    v.sem_inc(cols_ready, 1)
                    link(v.tensor_scalar(cw_c[:, :], wt_c[:, :], CUTOFF, 0.5, ALU.is_lt, ALU.mult))
                    link(v.tensor_scalar(wt_c[:, :], wt_c[:, :], CUTOFF, None, ALU.min))
                    v.sem_inc(angle, 1)
                    v.wait_ge(qt_mm, 1)
                    v.tensor_copy(q_t[:, :], ps_q[0:G, 0:NEL]).then_inc(qt_sb, 1)
                    v.wait_ge(logit_mm, 1)
                    v.tensor_copy(logits[:, :], ps_l[0:NEL, 0:NEL]).then_inc(logit_sb, 1)
                    for c in range(16):
                        v.wait_ge(row_mm, c + 1)
                        for n, t in enumerate(row_out):
                            v.tensor_copy(t[:, c, :], ps_row[0:100, c % 2, n, 0:TE]).then_inc(row_copied, 1)
                    v.wait_ge(sined, 1)
                    link(v.scalar_tensor_tensor(cw_c[:, :], near[:, :], 1.0, cw_c[:, :], ALU.add, ALU.mult))
                    v.wait_ge(loaded_nodes, 16 * 3)
                    v.tensor_copy(ntype_bf[:, :], ntype[0:TE, :])
                    layer_norm(v, xn[:, :, :], hn[:, :, :], sq[:, :, :])
                    link(v.tensor_scalar(hn[:, :, :], hn[:, :, :], 0.0, None, ALU.max))
                    v.tensor_copy(rows[:, :, H:H + 1], mult[:, :].unsqueeze(2))
                    link(v.tensor_tensor(rows[:, :, 0:H], hn[:, :, :], mult[:, :].unsqueeze(2).to_broadcast([TE, LO, H]),
                                         ALU.mult))
                    v.sem_inc(rows_ready, 1)

        stage = ExitStack()

        def esb(name, shape, dt=F32):
            return stage.enter_context(nc.sbuf_tensor(name, shape, dt))

        attr = esb("attr", [TE, 2, HT, R])
        key_rows = esb("key_rows", [TE, 2, HE], I16)
        hib = esb("hib", [TE, 2, HE], BF16)
        hi_t = esb("hi_t", [TE, 2, HE], BF16)
        attr_t = esb("attr_t", [2 * R, HT // 2 * TE])
        hid = esb("hid", [2 * H + 1, 2, HT // 2 * TE])
        gat = esb("gat", [P, 2, HT, GW])
        gat_y = esb("gat_y", [P, 2, HT, H])
        gat_idx = esb("gat_idx", [P, 2, HT], I32)
        same = esb("same", [TE, 2, HT, TE])
        junk_lo = esb("junk_lo", [TE, HT, LO], BF16)
        junk_z = esb("junk_z", [TE, HT, NEL], BF16)
        count = esb("count", [TE, 2, HT])
        sel = esb("sel", [TE, 2, HT])
        firsts = esb("firsts", [TE, 2, HT])
        target = esb("target", [P, 2, HT], I32)
        ztype = esb("ztype", [TE, 2, HT])
        adapt = esb("adapt", [TE, 2, HT])
        raw = esb("raw", [TE, HT, H])
        msg = esb("msg", [TE, 2, HT, H + 1])
        sums = esb("sums", [P, 2, HT, H + 1])
        sums_y = esb("sums_y", [P, 2, HT, H])
        src_less = esb("src_less", [TE, T])
        dst_less = esb("dst_less", [TE, T])

        ps_attr = stage.enter_context(nc.psum_tensor("ps_attr", [P, 512], F32))
        ps_hid = stage.enter_context(nc.psum_tensor("ps_hid", [P, 512], F32))
        ps_gate = stage.enter_context(nc.psum_tensor("ps_gate", [P, 2, 512], F32))
        ps_z = stage.enter_context(nc.psum_tensor("ps_z", [P, 2, 512], F32))
        ps_sum = stage.enter_context(nc.psum_tensor("ps_sum", [P, 2, 512], F32))

        def cols(a, h, parts=TE):
            return a[0:parts, bass.ds(h * HT, HT)]

        loads = [sem("loads_even"), sem("loads_odd")]
        attr_read, attr_sb, hid_mm, hid_sb = sem("attr_read"), sem("attr_sb"), sem("hid_mm"), sem("hid_sb")
        hi_onehot, z_mm, z_read, gate_mm, gate_read = (sem("hi_onehot"), sem("z_mm"), sem("z_read"), sem("gate_mm"),
                                                       sem("gate_read"))
        same_ready, msg_ready, sum_mm, sum_sb = sem("same_ready"), sem("msg_ready"), sem("sum_mm"), sem("sum_sb")
        gathered = [sem("gathered_even"), sem("gathered_odd")]
        idx_copied, target_ready = sem("idx_copied"), sem("target_ready")
        added = [sem("added_low"), sem("added_high")]
        pool_passed, sp_passed = sem("pool_passed"), sem("sp_passed")
        dve_half = sem("dve_half")
        NH = 2 * NB
        ADDS = 16 * HT // 2
        LINKS = 3

        with nc.Block() as block:

            @block.sync
            def _(sp):
                def load(h, par, first):
                    if not first:
                        sp.wait_ge(attr_read, h - 1)
                        sp.wait_ge(same_ready, h - 1)
                        sp.wait_ge(hi_onehot, h - 1)
                        sp.sem_inc(sp_passed, 1)
                    sp.dma_start(attr[:, par, :, :],
                                 edge_attr[bass.ds((h - par) * HE, 2 * HE), :].rearrange("(p i) r -> p i r", i=BT)
                                 [:, HT * par:HT * par + HT, :]).then_inc(loads[par], 16)
                    for rows_sb, rows_dram in ((key_rows, src_rows), (hib, hi_rows)):
                        sp.dma_start(rows_sb[:, par, :], rows_dram[bass.ds(h * HT, HT), :].rearrange("t e -> (t e)")
                                     .partition_broadcast(TE)).then_inc(loads[par], 16)
                load(0, 0, True)
                load(1, 1, True)
                with sp.Fori(1, NB) as b:
                    load(2 * b, 0, False)
                    load(2 * b + 1, 1, False)

            @block.gpsimd
            def _(p):
                def gather(h, par, first):
                    if not first:
                        p.wait_ge(msg_ready, h - 1)
                    p.sem_inc(pool_passed, 1)
                    p.tensor_copy(gat_idx[:, par, :], cols(dst_i, h, P)).then_inc(idx_copied, 1)
                    p.wait_ge(idx_copied, h + 1)
                    p.sem_inc(pool_passed, 1)
                    for i in range(HT):
                        p.indirect_dma_start(gat[:, par, i, :], None, node_tab,
                                             bass.IndirectOffsetOnAxis(ap=gat_idx[:, par, i:i + 1], axis=0)
                                             ).then_inc(gathered[par], 16)

                def scatter(h, par, first):
                    p.wait_ge(sum_sb, h + 2)
                    p.wait_ge(target_ready, h + 1)
                    for g in range(2):
                        if not first:
                            p.wait_ge(added[g], h * ADDS)
                        p.sem_inc(pool_passed, 1)
                        for i in range(HT // 2 * g, HT // 2 * (g + 1)):
                            p.indirect_dma_start(msg_acc[i], bass.IndirectOffsetOnAxis(ap=target[:, par, i:i + 1], axis=0),
                                                 sums[:, par, i, :], None, compute_op=ALU.add
                                                 ).then_inc(added[g], 16)
                gather(0, 0, True)
                gather(1, 1, True)
                scatter(0, 0, True)
                with p.Fori(1, NB) as b:
                    gather(2 * b, 0, False)
                    scatter(2 * b - 1, 1, False)
                    gather(2 * b + 1, 1, False)
                    scatter(2 * b, 0, False)
                scatter(NH - 1, 1, False)
                for g in range(2):
                    p.wait_ge(added[g], NH * ADDS)

            @block.tensor
            def _(t):
                def front(h, par, first, b):
                    t.wait_ge(loads[par], 48 * b + 48)
                    if not (first and par == 0):
                        t.wait_ge(attr_sb, h)
                    for k in range(HT // 2):
                        m = t.transpose(ps_attr[0:2 * R, TE * k:TE * k + TE],
                                        attr[:, par, 2 * k:2 * k + 2, :].rearrange("p a r -> p (a r)"), ident[0:TE, 0:TE])
                    m.then_inc(attr_read, 1)
                    t.wait_ge(attr_sb, h + 1)
                    if not (first and par == 0):
                        t.wait_ge(hid_sb, h)
                    t.matmul(ps_hid[0:2 * H, 0:HE // 2], w1_pair[:, :], attr_t[:, :], start=True, stop=True
                             ).then_inc(hid_mm, 1)
                    t.wait_ge(hi_onehot, h + 1)
                    if not first:
                        t.wait_ge(z_read, h - 1)
                    for i in range(HT):
                        m = t.matmul(ps_z[0:TE, par, LO * i:LO * i + LO], hi_t[:, par, TE * i:TE * i + TE], ntype_bf[:, :],
                                     start=True, stop=True)
                    m.then_inc(z_mm, 1)
                    t.wait_ge(hid_sb, h + 1)
                    if not first:
                        t.wait_ge(gate_read, h - 1)
                    for k in range(HT // 2):
                        m = t.matmul(ps_gate[0:TE, par, 2 * H * k:2 * H * k + 2 * H], hid[:, par, TE * k:TE * k + TE],
                                     w2_pair[:, :], start=True, stop=True)
                    m.then_inc(gate_mm, 1)

                def combine(h, par, first):
                    t.wait_ge(same_ready, h + 1)
                    t.wait_ge(msg_ready, h + 1)
                    if not first:
                        t.wait_ge(sum_sb, h)
                    for i in range(HT):
                        m = t.matmul(ps_sum[0:TE, par, (H + 1) * i:(H + 1) * (i + 1)], same[:, par, i, :],
                                     msg[:, par, i, :], start=True, stop=True)
                    m.then_inc(sum_mm, 1)
                t.sem_inc(sum_sb, 1)
                front(0, 0, True, 0)
                front(1, 1, True, 0)
                combine(0, 0, True)
                with t.Fori(1, NB) as b:
                    front(2 * b, 0, False, b)
                    combine(2 * b - 1, 1, False)
                    front(2 * b + 1, 1, False, b)
                    combine(2 * b, 0, False)
                combine(NH - 1, 1, False)

            @block.scalar
            def _(a):
                def front(h, par, first):
                    a.wait_ge(attr_read, h + 1)
                    if not (first and par == 0):
                        a.wait_ge(hid_mm, h)
                    a.activation(attr_t[:, :], ps_attr[0:2 * R, 0:HE // 2], ACT.Copy).then_inc(attr_sb, 1)
                    a.wait_ge(hid_mm, h + 1)
                    if not first:
                        a.wait_ge(gate_mm, h - 1)
                    a.activation(hid[0:2 * H, par, :], ps_hid[0:2 * H, 0:HE // 2], ACT.Silu, bias=b1_pair[:, :]
                                 ).then_inc(hid_sb, 1)

                def back(h, par):
                    a.wait_ge(sum_mm, h + 1)
                    a.wait_ge(target_ready, h + 1)
                    a.activation(sums[0:TE, par, :, :], ps_sum[0:TE, par, 0:HT * (H + 1)]
                                 .rearrange("p (i f) -> p i f", f=H + 1), ACT.Copy).then_inc(sum_sb, 1)
                front(0, 0, True)
                front(1, 1, True)
                back(0, 0)
                with a.Fori(1, NB) as b:
                    front(2 * b, 0, False)
                    back(2 * b - 1, 1)
                    front(2 * b + 1, 1, False)
                    back(2 * b, 0)
                back(NH - 1, 1)

            @block.vector
            def _(v):
                v.memset(hid[2 * H:2 * H + 1, :, :], 1.0)
                v.memset(sums[:, :, :, :], 0.0)
                v.memset(sums_y[:, :, :, :], 0.0)
                link(v.tensor_scalar(target[:, :, :].rearrange("p a i -> p (a i)"), zeros[:, 0:2 * HT], trash[:, :], None, ALU.add))
                v.tensor_scalar(dst_less[:, :], dst_c[:, :], trash[0:TE, :], None, ALU.subtract)
                link(v.tensor_scalar(src_less[:, :], src_c[:, :], trash[0:TE, :], None, ALU.subtract))

                def half(h, par, first, b):
                    n = [0]

                    def inner(ins):
                        n[0] += 1
                        ins.then_inc(dve_half, 1)
                        v.wait_ge(dve_half, h * LINKS + n[0])
                    v.wait_ge(loads[par], 48 * b + 48)
                    if not first:
                        v.wait_ge(z_mm, h - 1)
                    v.tensor_scalar(hi_t[:, par, :], hib[:, par, :], part_idx[0:TE, :], None, ALU.is_equal
                                    ).then_inc(hi_onehot, 1)
                    if not first:
                        v.wait_ge(sum_mm, h - 1)
                    for i in range(HT):
                        m = v.scalar_tensor_tensor(same[:, par, i, :], key_rows[:, par, TE * i:TE * i + TE],
                                                   src_c[:, bass.ds(h * HT + i, 1)], tri[0:TE, :], ALU.is_equal,
                                                   ALU.mult, accum_out=count[:, par, i:i + 1])
                    m.then_inc(same_ready, 1)
                    v.wait_ge(same_ready, h + 1)
                    inner(v.scalar_tensor_tensor(firsts[:, par, :], count[:, par, :], 1.0, cols(src_less, h), ALU.is_equal,
                                                 ALU.mult))
                    if not first:
                        for g in range(2):
                            v.wait_ge(added[g], (h - 1) * ADDS)
                    v.tensor_scalar(target[0:TE, par, :], firsts[:, par, :], trash[0:TE, :], None, ALU.add
                                    ).then_inc(target_ready, 1)
                    v.wait_ge(z_mm, h + 1)
                    for i in range(HT):
                        m = v.scalar_tensor_tensor(junk_lo[:, i, :], free_idx[0:TE, 0:LO], lo_c[:, bass.ds(h * HT + i, 1)],
                                                   ps_z[0:TE, par, LO * i:LO * i + LO], ALU.is_equal, ALU.mult,
                                                   accum_out=ztype[:, par, i:i + 1])
                    m.then_inc(z_read, 1)
                    v.wait_ge(z_read, h + 1)
                    v.wait_ge(gathered[par], 16 * HT * b + 16 * HT)
                    for i in range(HT):
                        m = v.scalar_tensor_tensor(junk_z[:, i, :], free_idx[0:TE, 0:NEL], ztype[:, par, i:i + 1],
                                                   gat[0:TE, par, i, H + 1:GW], ALU.is_equal, ALU.mult,
                                                   accum_out=adapt[:, par, i:i + 1])
                    inner(m)
                    v.wait_ge(gate_mm, h + 1)
                    for i in range(HT):
                        m = v.scalar_tensor_tensor(raw[:, i, :], ps_gate[0:TE, par, H * i:H * i + H], adapt[:, par, i:i + 1],
                                                   gat[0:TE, par, i, 0:H], ALU.add, ALU.mult)
                    m.then_inc(gate_read, 1)
                    v.wait_ge(gate_read, h + 1)
                    v.tensor_copy(msg[:, par, :, H:H + 1], gat[0:TE, par, :, H:H + 1])
                    inner(v.tensor_tensor(msg[:, par, :, 0:H], raw[:, :, :],
                                          cols(cw_c, h).unsqueeze(2).to_broadcast([TE, HT, H]), ALU.mult))
                    v.sem_inc(msg_ready, 1)
                    assert n[0] == LINKS
                half(0, 0, True, 0)
                half(1, 1, True, 0)
                with v.Fori(1, NB) as b:
                    half(2 * b, 0, False, b)
                    half(2 * b + 1, 1, False, b)

        def bc(a):
            return a.unsqueeze(2).to_broadcast([TE, LO, H])

        with ExitStack() as nodes:
            tabs = nodes.enter_context(nc.sbuf_tensor("tabs1", [TE, 3, LO, H + 1], F32))
            tabs_in = [sem("tabs_in0"), sem("tabs_in1")]
            tab_read, tot_ready = sem("tab_read"), sem("tot_ready")
            with nc.Block() as block:

                @block.sync
                def _(sp):
                    for i in range(NTAB):
                        if i >= 2:
                            sp.wait_ge(tab_read, i - 1)
                        sp.dma_start(tabs[:, i % 2, :, :], msg_acc[i][0:N, :].rearrange("(p j) f -> p j f", j=LO)
                                     ).then_inc(tabs_in[i % 2], 16)

                @block.scalar
                def _(a):
                    root(a, 2)
                    root(a, 3)

                @block.vector
                def _(v):
                    agg = tabs[:, 2, :, :]
                    for i in range(NTAB):
                        v.wait_ge(tabs_in[i % 2], 16 * (i // 2 + 1))
                        if i >= 1:
                            v.wait_ge(tab_read, i)
                            m = v.tensor_tensor(agg, agg, tabs[:, i % 2, :, :], ALU.add)
                        else:
                            m = v.tensor_copy(agg, tabs[:, 0, :, :])
                        m.then_inc(tab_read, 1)
                    v.wait_ge(tab_read, NTAB)
                    work, sq = tabs[:, 0, :, 0:H], tabs[:, 1, :, 0:H]
                    link(v.tensor_scalar(stat[:, 0, :].unsqueeze(2), agg[:, :, H:H + 1], 1e-8, None, ALU.max))
                    link(v.reciprocal(stat[:, 1, :], stat[:, 0, :]))
                    link(v.tensor_tensor(work, agg[:, :, 0:H], bc(stat[:, 1, :]), ALU.mult))
                    link(v.tensor_tensor(hn[:, :, :], hn[:, :, :], work, ALU.add))
                    layer_norm(v, hn[:, :, :], work, sq)
                    link(v.tensor_tensor(work, work, gamma_b[0:TE, :].unsqueeze(1).to_broadcast([TE, LO, H]), ALU.mult))
                    link(v.tensor_tensor(work, work, beta_b[0:TE, :].unsqueeze(1).to_broadcast([TE, LO, H]), ALU.add))
                    link(v.tensor_tensor(xn[:, :, :], xn[:, :, :], work, ALU.add))
                    layer_norm(v, xn[:, :, :], hn[:, :, :], sq)
                    link(v.tensor_scalar(hn[:, :, :], hn[:, :, :], 0.0, None, ALU.max))

        propagate(nc, ctx, locals())
        stage.close()


def propagate(nc, ctx, env):
    (sem, root, link, bc, cols, stage) = (env[k] for k in ("sem", "root", "link", "bc", "cols", "stage"))
    (key_rows, same, count, firsts, target, gat_idx, gat_y, sums_y, ps_sum) = (
        env[k] for k in ("key_rows", "same", "count", "firsts", "target", "gat_idx", "gat_y", "sums_y", "ps_sum"))
    (dst_c, dst_less, dst_rows, src_i, prop_acc, y_tab, zeros, tri, trash, xn, hn, dinv, stat, out) = (
        env[k] for k in ("dst_c", "dst_less", "dst_rows", "src_i", "prop_acc", "y_tab", "zeros", "tri", "trash", "xn",
                         "hn", "dinv", "stat", "out"))
    NH = env["NH"]
    QT = HT // 4
    yn = stage.enter_context(nc.sbuf_tensor("yn", [TE, LO, H], F32))
    acc = stage.enter_context(nc.sbuf_tensor("acc", [TE, LO, H], F32))
    tabs = stage.enter_context(nc.sbuf_tensor("tabs2", [TE, 2, LO, H], F32))
    keys = [sem("keys_even"), sem("keys_odd")]
    same_ready, sum_mm, sum_sb = sem("p_same_ready"), sem("p_sum_mm"), sem("p_sum_sb")
    gathered = [[sem(f"p_gathered_{x}{q}") for q in range(4)] for x in ("even", "odd")]
    idx_copied, target_ready, pool_passed = sem("p_idx_copied"), sem("p_target_ready"), sem("p_pool_passed")
    added = [sem(f"p_added{q}") for q in range(4)]
    tabs_in, tab_read = [sem("p_tabs_even"), sem("p_tabs_odd")], sem("p_tab_read")
    y_ready, y_stored, rezeroed, node_step, first_ready, stored, out_ready = (
        sem("y_ready"), sem("y_stored"), sem("rezeroed"), sem("node_step"), sem("first_ready"), sem("stored"),
        sem("out_ready"))
    NODE = 5

    with nc.Block() as block:

        @block.sync
        def _(sp):
            def edges(s):
                def load(h, par, first):
                    if not first:
                        sp.wait_ge(same_ready, s * NH + h - 1)
                        sp.sem_inc(env["sp_passed"], 1)
                    sp.dma_start(key_rows[:, par, :], dst_rows[bass.ds(h * HT, HT), :].rearrange("t e -> (t e)")
                                 .partition_broadcast(TE)).then_inc(keys[par], 16)
                load(0, 0, True)
                load(1, 1, True)
                with sp.Fori(1, NB) as b:
                    load(2 * b, 0, False)
                    load(2 * b + 1, 1, False)

            def between(s):
                for q in range(4):
                    sp.wait_ge(added[q], (s + 1) * (NH * 16 * QT))
                    sp.sem_inc(env["sp_passed"], 1)
                for i in range(NTAB):
                    if i >= 2:
                        sp.wait_ge(tab_read, s * NTAB + i - 1)
                        sp.sem_inc(env["sp_passed"], 1)
                    sp.dma_start(tabs[:, i % 2, :, :], prop_acc[i][0:N, :].rearrange("(p j) f -> p j f", j=LO)
                                 ).then_inc(tabs_in[i % 2], 16)
                for i in range(2):
                    sp.wait_ge(tabs_in[i], (s + 1) * (16 * NTAB // 2))
                    sp.sem_inc(env["sp_passed"], 1)
                for t in prop_acc:
                    sp.dma_start(t.rearrange("(p r) f -> p (r f)", p=P), zeros[:, 0:ACC_ROWS // P * H]
                                 ).then_inc(rezeroed, 16)
                sp.wait_ge(y_ready, s + 2)
                sp.sem_inc(env["sp_passed"], 1)
                sp.dma_start(y_tab.rearrange("(p j) f -> p j f", j=LO), yn[:, :, :]).then_inc(y_stored, 16)
                sp.wait_ge(rezeroed, (s + 1) * (16 * NTAB))
                sp.wait_ge(y_stored, s * 16 + 32)
                sp.sem_inc(env["sp_passed"], 1)
            sp.wait_ge(y_ready, 1)
            sp.dma_start(y_tab.rearrange("(p j) f -> p j f", j=LO), yn[:, :, :]).then_inc(y_stored, 16)
            edges(0)
            between(0)
            with sp.Fori(1, K + 1) as s:
                edges(s)
                between(s)
            sp.wait_ge(out_ready, 1)
            sp.dma_start(out.rearrange("(p j) f -> p j f", j=LO), xn[:, :, :]).then_inc(stored, 16)
            sp.wait_ge(stored, 16)

        @block.gpsimd
        def _(p):
            def edges(s):
                p.wait_ge(y_stored, s * 16 + 16)
                if not isinstance(s, int):
                    p.wait_ge(rezeroed, s * (16 * NTAB))

                def gather(h, par, first):
                    g = s * NH + h
                    if not first:
                        p.wait_ge(sum_mm, g - 1)
                    p.sem_inc(pool_passed, 1)
                    p.tensor_copy(gat_idx[:, par, :], cols(src_i, h, P)).then_inc(idx_copied, 1)
                    p.wait_ge(idx_copied, g + 1)
                    p.sem_inc(pool_passed, 1)
                    for i in range(HT):
                        p.indirect_dma_start(gat_y[:, par, i, :], None, y_tab,
                                             bass.IndirectOffsetOnAxis(ap=gat_idx[:, par, i:i + 1], axis=0)
                                             ).then_inc(gathered[par][i // QT], 16)

                def scatter(h, par, first):
                    g = s * NH + h
                    p.wait_ge(sum_sb, g + 2)
                    p.wait_ge(target_ready, g + 1)
                    for q in range(4):
                        if not first:
                            p.wait_ge(added[q], g * (16 * QT))
                        p.sem_inc(pool_passed, 1)
                        for i in range(QT * q, QT * (q + 1)):
                            p.indirect_dma_start(prop_acc[i], bass.IndirectOffsetOnAxis(ap=target[:, par, i:i + 1], axis=0),
                                                 sums_y[:, par, i, :], None, compute_op=ALU.add
                                                 ).then_inc(added[q], 16)
                gather(0, 0, True)
                gather(1, 1, True)
                scatter(0, 0, True)
                with p.Fori(1, NB) as b:
                    gather(2 * b, 0, False)
                    scatter(2 * b - 1, 1, False)
                    gather(2 * b + 1, 1, False)
                    scatter(2 * b, 0, False)
                scatter(NH - 1, 1, False)
            edges(0)
            with p.Fori(1, K + 1) as s:
                edges(s)

        @block.tensor
        def _(t):
            def edges(s):
                def combine(h, par, b, first):
                    g = s * NH + h
                    t.wait_ge(same_ready, g + 1)
                    for q in range(4):
                        t.wait_ge(gathered[par][q], (s * NB + b + 1) * (16 * QT))
                    if not first:
                        t.wait_ge(sum_sb, g)
                    for i in range(HT):
                        m = t.matmul(ps_sum[0:TE, par, H * i:H * (i + 1)], same[:, par, i, :], gat_y[0:TE, par, i, :],
                                     start=True, stop=True)
                    m.then_inc(sum_mm, 1)
                combine(0, 0, 0, True)
                combine(1, 1, 0, True)
                with t.Fori(1, NB) as b:
                    combine(2 * b, 0, b, False)
                    combine(2 * b + 1, 1, b, False)
            t.sem_inc(sum_sb, 1)
            edges(0)
            with t.Fori(1, K + 1) as s:
                edges(s)

        @block.scalar
        def _(a):
            def edges(s):
                def back(h, par):
                    a.wait_ge(sum_mm, s * NH + h + 1)
                    a.wait_ge(target_ready, s * NH + h + 1)
                    a.activation(sums_y[0:TE, par, :, :], ps_sum[0:TE, par, 0:HT * H]
                                 .rearrange("p (i f) -> p i f", f=H), ACT.Copy).then_inc(sum_sb, 1)
                with a.Fori(0, NB) as b:
                    back(2 * b, 0)
                    back(2 * b + 1, 1)
            edges(0)
            root(a, 4)
            with a.Fori(1, K + 1) as s:
                edges(s)

        @block.vector
        def _(v):
            def edges(s):
                def half(h, par, first):
                    g = s * NH + h
                    v.wait_ge(keys[par], (s * NH + (h - par)) * 8 + 16)
                    if not first:
                        v.wait_ge(sum_mm, g - 1)
                    for i in range(HT):
                        m = v.scalar_tensor_tensor(same[:, par, i, :], key_rows[:, par, TE * i:TE * i + TE],
                                                   dst_c[:, bass.ds(h * HT + i, 1)], tri[0:TE, :], ALU.is_equal,
                                                   ALU.mult, accum_out=count[:, par, i:i + 1])
                    m.then_inc(same_ready, 1)
                    v.wait_ge(same_ready, g + 1)
                    v.scalar_tensor_tensor(firsts[:, par, :], count[:, par, :], 1.0, cols(dst_less, h), ALU.is_equal,
                                           ALU.mult).then_inc(first_ready, 1)
                    v.wait_ge(first_ready, g + 1)
                    if not first:
                        for q in range(4):
                            v.wait_ge(added[q], (g - 1) * (16 * QT))
                    v.tensor_scalar(target[0:TE, par, :], firsts[:, par, :], trash[0:TE, :], None, ALU.add
                                    ).then_inc(target_ready, 1)
                half(0, 0, True)
                half(1, 1, True)
                with v.Fori(1, NB) as b:
                    half(2 * b, 0, False)
                    half(2 * b + 1, 1, False)

            def collect(s):
                for i in range(NTAB):
                    v.wait_ge(tabs_in[i % 2], s * (16 * NTAB // 2) + 16 * (i // 2 + 1))
                    if i == 0:
                        m = v.tensor_copy(acc[:, :, :], tabs[:, 0, :, :])
                    else:
                        v.wait_ge(tab_read, s * NTAB + i)
                        m = v.tensor_tensor(acc[:, :, :], acc[:, :, :], tabs[:, i % 2, :, :], ALU.add)
                    m.then_inc(tab_read, 1)
                v.wait_ge(tab_read, s * NTAB + NTAB)

            v.memset(yn[:, :, :], 1.0).then_inc(y_ready, 1)
            edges(0)
            collect(0)
            link(v.tensor_scalar(stat[:, 0, :].unsqueeze(2), acc[:, :, 0:1], 1.0, None, ALU.add))
            v.sem_inc(env["root_asked"], 1)
            v.wait_ge(env["root_done"], 4)
            link(v.reciprocal(dinv[:, :], stat[:, 1, :]))
            v.wait_ge(y_stored, 16)
            v.tensor_tensor(yn[:, :, :], hn[:, :, :], bc(dinv[:, :]), ALU.mult).then_inc(y_ready, 1)
            with v.Fori(1, K + 1) as s:
                edges(s)
                collect(s)
                n = [0]

                def step(ins):
                    n[0] += 1
                    ins.then_inc(node_step, 1)
                    v.wait_ge(node_step, (s - 1) * NODE + n[0])
                step(v.tensor_tensor(acc[:, :, :], acc[:, :, :], yn[:, :, :], ALU.add))
                step(v.tensor_tensor(acc[:, :, :], acc[:, :, :], bc(dinv[:, :]), ALU.mult))
                step(v.tensor_scalar(acc[:, :, :], acc[:, :, :], 1.0 - ALPHA, None, ALU.mult))
                step(v.scalar_tensor_tensor(acc[:, :, :], hn[:, :, :], ALPHA, acc[:, :, :], ALU.mult, ALU.add))
                v.wait_ge(y_stored, s * 16 + 16)
                step(v.tensor_tensor(yn[:, :, :], acc[:, :, :], bc(dinv[:, :]), ALU.mult))
                v.sem_inc(y_ready, 1)
                assert n[0] == NODE
            v.tensor_tensor(xn[:, :, :], xn[:, :, :], acc[:, :, :], ALU.add).then_inc(out_ready, 1)


_INS = ['x', 'src', 'dst', 'edge_attr_40', 'edge_weight', 'node_type_119', 'node_vec', 'L0_gnn_W1', 'L0_gnn_b1',
        'L0_gnn_W2', 'L0_gnn_b2', 'L0_gnn_emb', 'L0_gnn_adaptW', 'L0_gnn_gamma', 'L0_gnn_beta']
_OUTS = [((N, H), 'float32')]


def kernel(**inputs):
    import numpy as _np
    import concourse.bacc as _bacc
    from concourse import mybir as _mybir
    from concourse.bass_utils import run_bass_kernel_spmd as _run

    nc = _bacc.Bacc("TRN2", target_bir_lowering=False, num_devices=1)
    arrays, args = {}, []
    for name in _INS:
        a = _np.ascontiguousarray(inputs[name])
        arrays[f"in_{name}_dram"] = a
        args.append(nc.dram_tensor(f"in_{name}_dram", a.shape, _mybir.dt.from_np(a.dtype), kind="ExternalInput").ap())
    for i, (shape, dtype) in enumerate(_OUTS):
        dt = _mybir.dt.from_np(_np.dtype(dtype))
        args.append(nc.dram_tensor(f"out_{i}_dram", shape, dt, kind="ExternalOutput").ap())
    build(nc, *args)
    r = _run(nc, [arrays], core_ids=[0])
    got = tuple(r.results[0][f"out_{i}_dram"] for i in range(len(_OUTS)))
    return got[0]
```

```python
from contextlib import ExitStack

import concourse.bass as bass
from concourse import mybir

F32 = mybir.dt.float32
BF16 = mybir.dt.bfloat16
I32 = mybir.dt.int32
I16 = mybir.dt.int16
F16 = mybir.dt.float16
F8 = mybir.dt.float8e4
ALU = mybir.AluOpType
ACT = mybir.ActivationFunctionType
AX = mybir.AxisListType

P = 128
N = 6250
E = 200000
H = 48
R = 40
NEL = 119
G = 32
TE = 125
LO = N // TE
HT = 8
HE = HT * TE
BT = 2 * HT
NB = E // (BT * TE)
T = E // TE
GW = H + 1 + NEL
ACC_ROWS = 6400
NTAB = HT
K = 5
GN = 8
GT = 3
HG = 4
NG = HG * E // HE
QG = 7
FINE = 16
ALPHA = 0.8
CUTOFF = 6.0
LN_EPS = 1e-5
PI = 3.141592653589793
ROUND = 12582912.0


def build(nc, x, src, dst, edge_attr, edge_weight, node_type, node_vec, W1, b1, W2, b2, emb, adaptW,
          gamma, beta, out):
    node_tab = nc.dram_tensor("node_tab", (N, GW), F32).ap()
    y_tab = nc.dram_tensor("y_tab", (N, H), F32).ap()
    logit_tab = nc.dram_tensor("logit_tab", (NEL, NEL), F32).ap()
    msg_acc = [nc.dram_tensor(f"msg_acc{i}", (ACC_ROWS, H + 1), F32).ap() for i in range(NTAB)]
    prop_acc = [nc.dram_tensor(f"prop_acc{i}", (ACC_ROWS, H), F32).ap() for i in range(NTAB)]
    src_rows = nc.dram_tensor("src_rows", (T, TE), I16).ap()
    dst_rows = nc.dram_tensor("dst_rows", (T, TE), I16).ap()
    hi_rows = nc.dram_tensor("hi_rows", (T, TE), BF16).ap()
    code_pairs = nc.dram_tensor("code_pairs", (E + GT * P, 2), F32).ap()
    first_edges = nc.dram_tensor("first_edges", (QG * P,), I32).ap()
    counts = nc.dram_tensor("counts", (TE + 1, NG * GN * LO // 2), I16).ap()
    sum_tab = nc.dram_tensor("sum_tab", (N, H + 1), F32).ap()

    with ExitStack() as ctx:
        def sb(name, shape, dt=F32):
            return ctx.enter_context(nc.sbuf_tensor(name, shape, dt))

        def sem(name):
            return ctx.enter_context(nc.semaphore(name))

        part_idx = sb("part_idx", [P, 1])
        free_idx = sb("free_idx", [P, P])
        ident = sb("ident", [P, P])
        tri = sb("tri", [P, TE])
        trash = sb("trash", [P, 1])
        zeros = sb("zeros", [P, ACC_ROWS // P * (H + 1)])
        half_pi = sb("half_pi", [P, 1])
        flags = sb("flags", [P, 3])
        flag_i = sb("flag_i", [1, 1], I32)
        first_row = sb("first_row", [1, QG * P], I32)
        indeg = sb("indeg", [TE, LO])
        eps = sb("eps", [P, 1])
        w1_pair = sb("w1_pair", [2 * R, 2 * H])
        w2_pair = sb("w2_pair", [2 * H + 1, 2 * H])
        b1_pair = sb("b1_pair", [2 * H, 1])
        emb_t = sb("emb_t", [G, NEL])
        adapt_t = sb("adapt_t", [G, G])
        gamma_b = sb("gamma_b", [P, H])
        beta_b = sb("beta_b", [P, H])
        q_t = sb("q_t", [G, NEL])
        logits = sb("logits", [NEL, NEL])
        xn = sb("xn", [TE, LO, H])
        hn = sb("hn", [TE, LO, H])
        mult = sb("mult", [TE, LO])
        ntype = sb("ntype", [P, LO], I32)
        ntype_bf = sb("ntype_bf", [TE, LO], BF16)
        stat = sb("stat", [TE, 4, LO])
        dinv = sb("dinv", [TE, LO])
        src_i = sb("src_i", [P, T], I32)
        dst_i = sb("dst_i", [P, T], I32)
        src_c = sb("src_c", [TE, T])
        dst_c = sb("dst_c", [TE, T])
        lo_c = sb("lo_c", [TE, T])
        cw_c = sb("cw_c", [TE, T])

        dve_step = sem("dve_step")
        steps = [0]

        def link(ins):
            steps[0] += 1
            ins.then_inc(dve_step, 1)
            nc.vector.wait_ge(dve_step, steps[0])

        def layer_norm(v, xin, y, sq):
            def bc(a):
                return a.unsqueeze(2).to_broadcast([TE, LO, H])
            link(v.tensor_reduce(stat[:, 0, :], xin, AX.X, ALU.add))
            link(v.tensor_scalar(stat[:, 1, :], stat[:, 0, :], 1.0 / H, None, ALU.mult))
            link(v.tensor_tensor(y, xin, bc(stat[:, 1, :]), ALU.subtract))
            link(v.tensor_tensor(sq, y, y, ALU.mult))
            link(v.tensor_reduce(stat[:, 2, :], sq, AX.X, ALU.add))
            link(v.tensor_scalar(stat[:, 0, :], stat[:, 2, :], 1.0 / H, LN_EPS, ALU.mult, ALU.add))
            v.sem_inc(root_asked, 1)
            roots[0] += 1
            v.wait_ge(root_done, roots[0])
            link(v.reciprocal(stat[:, 3, :], stat[:, 1, :]))
            link(v.tensor_tensor(y, y, bc(stat[:, 3, :]), ALU.mult))

        root_asked, root_done, roots = sem("root_asked"), sem("root_done"), [0]

        def root(a, n):
            a.wait_ge(root_asked, n)
            a.activation(stat[:, 1, :], stat[:, 0, :], ACT.Sqrt).then_inc(root_done, 1)

        with ExitStack() as setup:
            def ssb(name, shape, dt=F32):
                return setup.enter_context(nc.sbuf_tensor(name, shape, dt))

            sq = ssb("sq", [TE, LO, H])
            rows = ssb("rows", [TE, LO, GW])
            hi_c = ssb("hi_c", [TE, T])
            pair = ssb("pair", [TE, T, 2])
            no_pair = ssb("no_pair", [P, 2 * GT])
            tile_first_i = ssb("tile_first_i", [1, T], I32)
            tile_first = ssb("tile_first", [1, T])
            ones_row = ssb("ones_row", [1, P])
            dst_flat = ssb("dst_flat", [TE, T], I32)
            dst_next = ssb("dst_next", [TE, T], I32)
            falls = ssb("falls", [TE, T], BF16)
            below = ssb("below", [P, T], BF16)
            group_node = ssb("group_node", [P, QG + 1])
            tiles_below, tile_at = ssb("tiles_below", [P, QG + 1]), ssb("tile_at", [P, QG + 1])
            tile_at_i = ssb("tile_at_i", [P, QG + 1], I32)
            found = ssb("found", [P, QG + 1, TE], I32)
            edges_below, first_at = ssb("edges_below", [P, QG + 1]), ssb("first_at", [P, QG + 1])
            first_at_i = ssb("first_at_i", [P, QG + 1], I32)
            loaded_order, pair_ready, firsts_ready, firsts_mm = (sem("loaded_order"), sem("pair_ready"), sem("firsts_ready"),
                                                                 sem("firsts_mm"))
            tile_known, tile_found, first_known, first_out = (sem("tile_known"), sem("tile_found"), sem("first_known"),
                                                              sem("first_out"))
            near = ssb("near", [TE, T])
            wt_c = ssb("wt_c", [TE, T])
            row_out = [ssb("src_out", [100, 16, TE], I16), ssb("dst_out", [100, 16, TE], I16),
                       ssb("hi_out", [100, 16, TE], BF16)]
            ps_row = setup.enter_context(nc.psum_tensor("ps_row", [P, 2, 4, P], F32))
            ps_q = setup.enter_context(nc.psum_tensor("ps_q", [P, 512], F32))
            ps_l = setup.enter_context(nc.psum_tensor("ps_l", [P, 512], F32))
            ps_first = setup.enter_context(nc.psum_tensor("ps_first", [P, 4, 512], F32))
            loaded_nodes, loaded_edges, loaded_weights = sem("loaded_nodes"), sem("loaded_edges"), sem("loaded_weights")
            consts, padded, qt_mm, qt_sb, logit_mm, logit_sb = (sem("consts"), sem("padded"), sem("qt_mm"), sem("qt_sb"),
                                                                sem("logit_mm"), sem("logit_sb"))
            logit_out, logit_rows, rows_ready, tables = sem("logit_out"), sem("logit_rows"), sem("rows_ready"), sem("tables")
            cols_ready, row_mm, row_copied, angle, sined = (sem("cols_ready"), sem("row_mm"), sem("row_copied"), sem("angle"),
                                                            sem("sined"))
            zeroed = sem("zeroed")
            rows_of = (src_c, dst_c, hi_c)
            WEIGHTS = 12
            with nc.allow_non_contiguous_dma(reason="weights of a few KB, transposed once"), nc.Block() as block:

                @block.sync
                def _(sp):
                    by_tile = "(b p i) -> p b i"
                    sp.wait_ge(padded, 3)
                    for a, t in ((dst, dst_i), (src, src_i)):
                        sp.dma_start(t[0:TE, :].rearrange("p (b i) -> p b i", i=BT),
                                     a.rearrange(by_tile, p=TE, i=BT)).then_inc(loaded_edges, 16)
                    sp.dma_start(wt_c[:, :].rearrange("p (b i) -> p b i", i=BT),
                                 edge_weight.rearrange(by_tile, p=TE, i=BT)).then_inc(loaded_edges, 16)
                    sp.wait_ge(padded, 4)
                    sp.dma_start(tile_first_i[:, :], dst.rearrange("(o t e) -> o t e", o=1, e=TE)[:, :, 0]
                                 ).then_inc(loaded_order, 16)
                    sp.dma_start(dst_flat[:, :], dst.rearrange("(p t) -> p t", t=T)).then_inc(loaded_order, 16)
                    sp.dma_start(dst_next[0:TE - 1, :], dst[1:1 + (TE - 1) * T].rearrange("(p t) -> p t", t=T)
                                 ).then_inc(loaded_order, 16)
                    sp.dma_start(dst_next[TE - 1:TE, 0:T - 1], dst[1 + (TE - 1) * T:E].unsqueeze(0)
                                 ).then_inc(loaded_order, 16)
                    sp.wait_ge(pair_ready, 1)
                    sp.dma_start(code_pairs[0:E, :].rearrange("(b p i) c -> p b (i c)", p=TE, i=BT),
                                 pair[:, :, :].rearrange("p (b i) c -> p b (i c)", i=BT)).then_inc(tables, 16)
                    sp.wait_ge(consts, 2)
                    sp.dma_start(code_pairs[E:E + GT * P, :].rearrange("(p i) c -> p (i c)", p=P), no_pair[:, :]
                                 ).then_inc(tables, 16)
                    sp.wait_ge(first_known, 1)
                    sp.dma_start(first_edges.rearrange("(p c) -> p c", c=QG), first_at_i[:, 0:QG]).then_inc(first_out, 16)
                    sp.wait_ge(first_out, 16)
                    sp.dma_start(first_row[:, :], first_edges.unsqueeze(0)).then_inc(tables, 16)
                    for c in range(16):
                        sp.wait_ge(row_copied, 3 * (c + 1))
                        for d, t in zip((src_rows, dst_rows, hi_rows), row_out):
                            sp.dma_start(d[100 * c:100 * c + 100, :], t[:, c, :]).then_inc(tables, 16)
                    sp.wait_ge(rows_ready, 1)
                    sp.wait_ge(logit_rows, 16 * LO)
                    sp.dma_start(node_tab.rearrange("(j p) f -> p j f", p=TE), rows[:, :, :]).then_inc(tables, 16)
                    sp.wait_ge(tables, 16 * 52)
                    sp.wait_ge(zeroed, 16 * 2 * NTAB)

                @block.gpsimd
                def _(p):
                    p.memset(src_i[:, :], 0).then_inc(padded, 1)
                    p.memset(dst_i[:, :], 0).then_inc(padded, 1)
                    p.memset(ntype[:, :], 0).then_inc(padded, 1)
                    p.memset(dst_next[:, :], N).then_inc(padded, 1)
                    p.iota(group_node[:, :], [[GN, QG + 1]], 0, GN * QG, allow_small_or_imprecise_dtypes=True)
                    p.iota(part_idx[:, :], [[0, 1]], 0, 1, allow_small_or_imprecise_dtypes=True)
                    p.iota(trash[:, :], [[0, 1]], N, 1, allow_small_or_imprecise_dtypes=True)
                    p.iota(free_idx[:, :], [[1, P]], 0, 0, allow_small_or_imprecise_dtypes=True).then_inc(consts, 1)
                    p.wait_ge(tile_known, 1)
                    for c in range(QG + 1):
                        p.indirect_dma_start(found[:, c, :], None, dst.rearrange("(t e) -> t e", e=TE),
                                             bass.IndirectOffsetOnAxis(ap=tile_at_i[:, c:c + 1], axis=0)
                                             ).then_inc(tile_found, 16)
                    p.wait_ge(logit_out, 16)
                    p.wait_ge(loaded_nodes, 16 * 3)
                    for j in range(LO):
                        p.indirect_dma_start(rows[:, j, H + 1:GW], None, logit_tab,
                                             bass.IndirectOffsetOnAxis(ap=ntype[0:TE, j:j + 1], axis=0)
                                             ).then_inc(logit_rows, 16)

                @block.scalar
                def _(a):
                    a.wait_ge(padded, 3)
                    a.dma_start(xn[:, :, :], x.rearrange("(j p) f -> p j f", p=TE)).then_inc(loaded_nodes, 16)
                    a.dma_start(mult[:, :], node_vec.rearrange("(j p) -> p j", p=TE)).then_inc(loaded_nodes, 16)
                    a.dma_start(ntype[0:TE, :], node_type.rearrange("(j p) -> p j", p=TE)).then_inc(loaded_nodes, 16)
                    a.dma_start(emb_t[:, :], emb.rearrange("n g -> g n")).then_inc(loaded_weights, 16)
                    a.dma_start(adapt_t[:, :], adaptW.rearrange("i k -> k i")).then_inc(loaded_weights, 16)
                    a.wait_ge(consts, 2)
                    for s in range(2):
                        a.dma_start(w1_pair[R * s:R * s + R, H * s:H * s + H], W1.rearrange("h r -> r h")
                                    ).then_inc(loaded_weights, 16)
                        a.dma_start(w2_pair[H * s:H * s + H, H * s:H * s + H], W2.rearrange("o i -> i o")
                                    ).then_inc(loaded_weights, 16)
                        a.dma_start(w2_pair[2 * H:2 * H + 1, H * s:H * s + H], b2.unsqueeze(0)
                                    ).then_inc(loaded_weights, 16)
                        a.dma_start(b1_pair[H * s:H * s + H, :], b1.unsqueeze(1)).then_inc(loaded_weights, 16)
                    a.dma_start(gamma_b[:, :], gamma.partition_broadcast(P)).then_inc(loaded_weights, 16)
                    a.dma_start(beta_b[:, :], beta.partition_broadcast(P)).then_inc(loaded_weights, 16)
                    for t in msg_acc + prop_acc:
                        w = t.shape[1] * ACC_ROWS // P
                        a.dma_start(t.rearrange("(p r) f -> p (r f)", p=P), zeros[:, 0:w]).then_inc(zeroed, 16)
                    a.wait_ge(logit_sb, 1)
                    a.dma_start(logit_tab, logits[:, :]).then_inc(logit_out, 16)
                    a.wait_ge(angle, 1)
                    a.activation(near[:, :], wt_c[:, :], ACT.Sin, bias=half_pi[0:TE, :],
                                 scale=-PI / CUTOFF).then_inc(sined, 1)
                    root(a, 1)
                    a.wait_ge(loaded_weights, 16 * WEIGHTS)
                    a.wait_ge(logit_out, 16)

                @block.tensor
                def _(t):
                    t.wait_ge(loaded_weights, 16 * WEIGHTS)
                    t.matmul(ps_q[0:G, 0:NEL], adapt_t[:, :], emb_t[:, :], start=True, stop=True).then_inc(qt_mm, 1)
                    t.wait_ge(qt_sb, 1)
                    t.matmul(ps_l[0:NEL, 0:NEL], q_t[:, :], emb_t[:, :], start=True, stop=True).then_inc(logit_mm, 1)
                    t.wait_ge(firsts_ready, 1)
                    for c in range(4):
                        m = t.matmul(ps_first[:, c, 0:T // 4], ones_row[:, :], tile_first[:, T // 4 * c:T // 4 * (c + 1)],
                                     start=True, stop=True)
                    m.then_inc(firsts_mm, 1)
                    t.wait_ge(cols_ready, 1)
                    for c in range(16):
                        if c >= 2:
                            t.wait_ge(row_copied, 3 * (c - 1))
                        for n, cols in enumerate(rows_of):
                            m = t.transpose(ps_row[0:100, c % 2, n, 0:TE], cols[:, 100 * c:100 * c + 100],
                                            ident[0:TE, 0:TE])
                        m.then_inc(row_mm, 1)

                @block.vector
                def _(v):
                    v.memset(zeros[:, :], 0.0)
                    v.memset(flags[:, :], 0.0)
                    v.memset(ones_row[:, :], 1.0)
                    v.memset(no_pair[:, :], -1.0)
                    v.memset(w1_pair[:, :], 0.0)
                    v.memset(w2_pair[:, :], 0.0)
                    v.memset(half_pi[:, :], PI / 2)
                    v.memset(eps[:, :], LN_EPS).then_inc(consts, 1)
                    v.wait_ge(consts, 2)
                    v.tensor_scalar(ident[:, :], free_idx[:, :], part_idx[:, 0:1], None, ALU.is_equal)
                    link(v.tensor_scalar(tri[:, :], free_idx[:, 0:TE], part_idx[:, 0:1], None, ALU.is_le))
                    v.wait_ge(qt_mm, 1)
                    v.tensor_copy(q_t[:, :], ps_q[0:G, 0:NEL]).then_inc(qt_sb, 1)
                    v.wait_ge(logit_mm, 1)
                    v.tensor_copy(logits[:, :], ps_l[0:NEL, 0:NEL]).then_inc(logit_sb, 1)
                    v.wait_ge(loaded_edges, 16 * 3)
                    v.tensor_copy(src_c[:, :], src_i[0:TE, :])
                    link(v.tensor_copy(dst_c[:, :], dst_i[0:TE, :]))
                    link(v.tensor_scalar(near[:, :], src_c[:, :], (TE - 1) / 2, 1.0 / TE, ALU.subtract, ALU.mult))
                    link(v.tensor_scalar(lo_c[:, :], near[:, :], ROUND, ROUND, ALU.add, ALU.subtract))
                    link(v.scalar_tensor_tensor(hi_c[:, :], lo_c[:, :], -float(TE), src_c[:, :], ALU.mult, ALU.add))
                    v.sem_inc(cols_ready, 1)
                    v.tensor_copy(pair[:, :, 1], hi_c[:, :])
                    link(v.scalar_tensor_tensor(pair[:, :, 0], dst_c[:, :], float(LO), lo_c[:, :], ALU.mult, ALU.add))
                    v.sem_inc(pair_ready, 1)
                    v.wait_ge(loaded_order, 16 * 4)
                    link(v.tensor_copy(tile_first[:, :], tile_first_i[:, :]))
                    v.sem_inc(firsts_ready, 1)
                    v.tensor_tensor(falls[:, :], dst_flat[:, :], dst_next[:, :], ALU.is_gt).then_inc(dve_step, 1)
                    steps[0] += 1
                    v.wait_ge(dve_step, steps[0])
                    link(v.tensor_reduce(flags[0:TE, 0:1], falls[:, :], AX.X, ALU.max))
                    v.wait_ge(firsts_mm, 1)
                    for c in range(QG + 1):
                        link(v.tensor_scalar(below[:, :].rearrange("p (a b) -> p a b", a=4), ps_first[:, :, 0:T // 4],
                                             group_node[:, c:c + 1], 0.0, ALU.is_lt, ALU.add,
                                             accum_out=tiles_below[:, c:c + 1]))
                    link(v.tensor_scalar(tile_at[:, :], tiles_below[:, :], 1.0, 0.0, ALU.subtract, ALU.max))
                    link(v.tensor_copy(tile_at_i[:, :], tile_at[:, :]))
                    v.sem_inc(tile_known, 1)
                    link(v.tensor_scalar(cw_c[:, :], wt_c[:, :], CUTOFF, 0.5, ALU.is_lt, ALU.mult))
                    link(v.tensor_scalar(wt_c[:, :], wt_c[:, :], CUTOFF, None, ALU.min))
                    v.sem_inc(angle, 1)
                    v.wait_ge(tile_found, 16 * (QG + 1))
                    for c in range(QG + 1):
                        link(v.tensor_scalar(below[:, 0:TE], found[:, c, :], group_node[:, c:c + 1], 0.0, ALU.is_lt,
                                             ALU.add, accum_out=edges_below[:, c:c + 1]))
                    link(v.scalar_tensor_tensor(first_at[:, :], tile_at[:, :], float(TE), edges_below[:, :], ALU.mult,
                                                ALU.add))
                    link(v.tensor_copy(first_at_i[:, :], first_at[:, :]))
                    v.sem_inc(first_known, 1)
                    link(v.tensor_tensor(below[:, 0:QG], first_at[:, 1:QG + 1], first_at[:, 0:QG], ALU.subtract))
                    link(v.tensor_reduce(tiles_below[:, 0:1], below[:, 0:QG], AX.X, ALU.max))
                    link(v.tensor_scalar(flags[:, 1:2], tiles_below[:, 0:1], float(GT * P), None, ALU.is_gt))
                    for c in range(16):
                        v.wait_ge(row_mm, c + 1)
                        for n, t in enumerate(row_out):
                            v.tensor_copy(t[:, c, :], ps_row[0:100, c % 2, n, 0:TE]).then_inc(row_copied, 1)
                    v.wait_ge(sined, 1)
                    link(v.scalar_tensor_tensor(cw_c[:, :], near[:, :], 1.0, cw_c[:, :], ALU.add, ALU.mult))
                    v.wait_ge(loaded_nodes, 16 * 3)
                    v.tensor_copy(ntype_bf[:, :], ntype[0:TE, :])
                    layer_norm(v, xn[:, :, :], hn[:, :, :], sq[:, :, :])
                    link(v.tensor_scalar(hn[:, :, :], hn[:, :, :], 0.0, None, ALU.max))
                    v.tensor_copy(rows[:, :, H:H + 1], mult[:, :].unsqueeze(2))
                    link(v.tensor_tensor(rows[:, :, 0:H], hn[:, :, :], mult[:, :].unsqueeze(2).to_broadcast([TE, LO, H]),
                                         ALU.mult))
                    v.sem_inc(rows_ready, 1)

        stage = ExitStack()

        def esb(name, shape, dt=F32):
            return stage.enter_context(nc.sbuf_tensor(name, shape, dt))

        attr = esb("attr", [TE, 2, HT, R])
        key_rows = esb("key_rows", [TE, 2, HE], I16)
        hib = esb("hib", [TE, 2, HE], BF16)
        hi_t = esb("hi_t", [TE, 2, HE], BF16)
        attr_t = esb("attr_t", [2 * R, HT // 2 * TE])
        hid = esb("hid", [2 * H + 1, 2, HT // 2 * TE])
        gat = esb("gat", [P, 2, HT, GW])
        gat_y = esb("gat_y", [P, 2, HT, H])
        gat_idx = esb("gat_idx", [P, 2, HT], I32)
        same = esb("same", [TE, 2, HT, TE])
        junk_lo = esb("junk_lo", [TE, HT, LO], BF16)
        junk_z = esb("junk_z", [TE, HT, NEL], BF16)
        count = esb("count", [TE, 2, HT])
        sel = esb("sel", [TE, 2, HT])
        firsts = esb("firsts", [TE, 2, HT])
        target = esb("target", [P, 2, HT], I32)
        ztype = esb("ztype", [TE, 2, HT])
        adapt = esb("adapt", [TE, 2, HT])
        raw = esb("raw", [TE, HT, H])
        msg = esb("msg", [TE, 2, HT, H + 1])
        sums = esb("sums", [P, 2, HT, H + 1])
        sums_y = esb("sums_y", [P, 2, HT, H])
        src_less = esb("src_less", [TE, T])
        dst_less = esb("dst_less", [TE, T])
        pair_in = esb("pair_in", [P, 2, HG, GT, 2])
        group_code = esb("group_code", [P, NG])
        code_in = esb("code_in", [P, 2, HG, GT])
        hi_in = esb("hi_in", [P, 2, HG, GT], BF16)
        hi_iota = esb("hi_iota", [P, TE, HG * GT], BF16)
        code_iota = esb("code_iota", [P, GN * LO], F16)
        hi_hot = esb("hi_hot", [P, 2, TE + 1, HG * GT], BF16)
        code_hot = esb("code_hot", [P, 2, HG * GT, GN * LO], BF16)
        slab = esb("slab", [TE + 1, 2, HG, GN * LO], F8)

        ps_attr = stage.enter_context(nc.psum_tensor("ps_attr", [P, 512], F32))
        ps_hid = stage.enter_context(nc.psum_tensor("ps_hid", [P, 512], F32))
        ps_gate = stage.enter_context(nc.psum_tensor("ps_gate", [P, 2, 512], F32))
        ps_z = stage.enter_context(nc.psum_tensor("ps_z", [P, 512], F32))
        ps_sum = stage.enter_context(nc.psum_tensor("ps_sum", [P, 512], F32))
        ps_count = stage.enter_context(nc.psum_tensor("ps_count", [P, 2, 512], F32))

        def cols(a, h, parts=TE):
            return a[0:parts, bass.ds(h * HT, HT)]

        loads = [sem("loads_even"), sem("loads_odd")]
        attr_read, attr_sb, hid_mm, hid_sb = sem("attr_read"), sem("attr_sb"), sem("hid_mm"), sem("hid_sb")
        hi_onehot, z_mm, z_read, gate_mm, gate_read = (sem("hi_onehot"), sem("z_mm"), sem("z_read"), sem("gate_mm"),
                                                       sem("gate_read"))
        same_ready, msg_ready, sum_mm, sum_sb = sem("same_ready"), sem("msg_ready"), sem("sum_mm"), sem("sum_sb")
        gathered = [sem("gathered_even"), sem("gathered_odd")]
        idx_copied, target_ready = sem("idx_copied"), sem("target_ready")
        added = [sem("added_low"), sem("added_high")]
        pool_passed, sp_passed = sem("pool_passed"), sem("sp_passed")
        dve_half = sem("dve_half")
        NH = 2 * NB
        ADDS = 16 * HT // 2
        pairs_in = [sem("pairs_in_even"), sem("pairs_in_odd")]
        code_ready, hot_ready, count_mm, slab_sb = sem("code_ready"), sem("hot_ready"), sem("count_mm"), sem("slab_sb")
        slab_out = [sem("slab_out_even"), sem("slab_out_odd")]
        iotas, act_passed, pe_passed = sem("iotas"), sem("act_passed"), sem("pe_passed")
        LINKS = 3

        with nc.Block() as block:

            @block.sync
            def _(sp):
                def load(h, par, first):
                    if not first:
                        sp.wait_ge(attr_read, h - 1)
                        sp.wait_ge(same_ready, h - 1)
                        sp.wait_ge(hi_onehot, h - 1)
                        sp.sem_inc(sp_passed, 1)
                    sp.dma_start(attr[:, par, :, :],
                                 edge_attr[bass.ds((h - par) * HE, 2 * HE), :].rearrange("(p i) r -> p i r", i=BT)
                                 [:, HT * par:HT * par + HT, :]).then_inc(loads[par], 16)
                    for rows_sb, rows_dram in ((key_rows, src_rows), (hib, hi_rows)):
                        sp.dma_start(rows_sb[:, par, :], rows_dram[bass.ds(h * HT, HT), :].rearrange("t e -> (t e)")
                                     .partition_broadcast(TE)).then_inc(loads[par], 16)
                    if not first:
                        sp.wait_ge(code_ready, h - 1)
                        sp.sem_inc(sp_passed, 1)
                    for k in range(HG):
                        at = sp.value_load(first_row[0:1, bass.ds(h * HG + k, 1)], min_val=0, max_val=E)
                        sp.dma_start(pair_in[:, par, k, :, :].rearrange("p i c -> p (i c)"),
                                     code_pairs[bass.ds(at, GT * P), :].rearrange("(p i) c -> p (i c)", p=P)
                                     ).then_inc(pairs_in[par], 16)

                def store(h, par):
                    sp.wait_ge(slab_sb, h * HG + HG)
                    sp.sem_inc(sp_passed, 1)
                    sp.dma_start(counts[:, bass.ds(h * (HG * GN * LO // 2), HG * GN * LO // 2)],
                                 slab[:, par, :, :].rearrange("p k c -> p (k c)").bitcast(I16)
                                 ).then_inc(slab_out[par], 16)
                load(0, 0, True)
                load(1, 1, True)
                with sp.Fori(1, NB) as b:
                    store(2 * b - 2, 0)
                    load(2 * b, 0, False)
                    store(2 * b - 1, 1)
                    load(2 * b + 1, 1, False)
                store(NH - 2, 0)
                store(NH - 1, 1)
                for par in range(2):
                    sp.wait_ge(slab_out[par], 16 * NB)

            @block.gpsimd
            def _(p):
                def gather(h, par, first):
                    if not first:
                        p.wait_ge(msg_ready, h - 1)
                    p.sem_inc(pool_passed, 1)
                    p.tensor_copy(gat_idx[:, par, :], cols(dst_i, h, P)).then_inc(idx_copied, 1)
                    p.wait_ge(idx_copied, h + 1)
                    p.sem_inc(pool_passed, 1)
                    for i in range(HT):
                        p.indirect_dma_start(gat[:, par, i, :], None, node_tab,
                                             bass.IndirectOffsetOnAxis(ap=gat_idx[:, par, i:i + 1], axis=0)
                                             ).then_inc(gathered[par], 16)

                def scatter(h, par, first):
                    p.wait_ge(sum_sb, h + 2)
                    p.wait_ge(target_ready, h + 1)
                    for g in range(2):
                        if not first:
                            p.wait_ge(added[g], h * ADDS)
                        p.sem_inc(pool_passed, 1)
                        for i in range(HT // 2 * g, HT // 2 * (g + 1)):
                            p.indirect_dma_start(msg_acc[i], bass.IndirectOffsetOnAxis(ap=target[:, par, i:i + 1], axis=0),
                                                 sums[:, par, i, :], None, compute_op=ALU.add
                                                 ).then_inc(added[g], 16)
                p.iota(group_code[:, :], [[GN * LO, NG]], 0, 0, allow_small_or_imprecise_dtypes=True)
                p.iota(code_iota[:, :], [[1, GN * LO]], 0, 0, allow_small_or_imprecise_dtypes=True)
                p.iota(hi_iota[:, :, :], [[1, TE], [0, HG * GT]], 0, 0, allow_small_or_imprecise_dtypes=True
                       ).then_inc(iotas, 1)
                gather(0, 0, True)
                gather(1, 1, True)
                scatter(0, 0, True)
                with p.Fori(1, NB) as b:
                    gather(2 * b, 0, False)
                    scatter(2 * b - 1, 1, False)
                    gather(2 * b + 1, 1, False)
                    scatter(2 * b, 0, False)
                scatter(NH - 1, 1, False)
                for g in range(2):
                    p.wait_ge(added[g], NH * ADDS)

            @block.tensor
            def _(t):
                def front(h, par, first, b):
                    t.wait_ge(loads[par], 48 * b + 48)
                    if not (first and par == 0):
                        t.wait_ge(attr_sb, h)
                    for k in range(HT // 2):
                        m = t.transpose(ps_attr[0:2 * R, TE * k:TE * k + TE],
                                        attr[:, par, 2 * k:2 * k + 2, :].rearrange("p a r -> p (a r)"), ident[0:TE, 0:TE])
                    m.then_inc(attr_read, 1)
                    t.wait_ge(attr_sb, h + 1)
                    if not (first and par == 0):
                        t.wait_ge(hid_sb, h)
                    t.matmul(ps_hid[0:2 * H, 0:HE // 2], w1_pair[:, :], attr_t[:, :], start=True, stop=True
                             ).then_inc(hid_mm, 1)
                    t.wait_ge(hi_onehot, h + 1)
                    if not (first and par == 0):
                        t.wait_ge(z_read, h)
                    for i in range(HT):
                        m = t.matmul(ps_z[0:TE, LO * i:LO * i + LO], hi_t[:, par, TE * i:TE * i + TE], ntype_bf[:, :],
                                     start=True, stop=True)
                    m.then_inc(z_mm, 1)
                    t.wait_ge(hid_sb, h + 1)
                    if not first:
                        t.wait_ge(gate_read, h - 1)
                    for k in range(HT // 2):
                        m = t.matmul(ps_gate[0:TE, par, 2 * H * k:2 * H * k + 2 * H], hid[:, par, TE * k:TE * k + TE],
                                     w2_pair[:, :], start=True, stop=True)
                    m.then_inc(gate_mm, 1)

                def combine(h, par, first):
                    t.wait_ge(same_ready, h + 1)
                    t.wait_ge(msg_ready, h + 1)
                    if not first:
                        t.wait_ge(sum_sb, h + 1)
                    for i in range(HT):
                        m = t.matmul(ps_sum[0:TE, (H + 1) * i:(H + 1) * (i + 1)], same[:, par, i, :],
                                     msg[:, par, i, :], start=True, stop=True)
                    m.then_inc(sum_mm, 1)

                def count(h, par, first):
                    t.wait_ge(hot_ready, h + 1)
                    for k in range(HG):
                        if not (first and par == 0 and k < 2):
                            t.wait_ge(slab_sb, h * HG + k - 1)
                        for i in range(GT * k, GT * k + GT):
                            m = t.matmul(ps_count[0:TE + 1, k % 2, 0:GN * LO], hi_hot[:, par, :, i],
                                         code_hot[:, par, i, :], start=(i % GT == 0), stop=(i % GT == GT - 1))
                        m.then_inc(count_mm, 1)
                t.sem_inc(sum_sb, 1)
                front(0, 0, True, 0)
                count(0, 0, True)
                front(1, 1, True, 0)
                count(1, 1, True)
                combine(0, 0, True)
                with t.Fori(1, NB) as b:
                    front(2 * b, 0, False, b)
                    combine(2 * b - 1, 1, False)
                    count(2 * b, 0, False)
                    front(2 * b + 1, 1, False, b)
                    combine(2 * b, 0, False)
                    count(2 * b + 1, 1, False)
                combine(NH - 1, 1, False)

            @block.scalar
            def _(a):
                def front(h, par, first):
                    a.wait_ge(attr_read, h + 1)
                    if not (first and par == 0):
                        a.wait_ge(hid_mm, h)
                    a.activation(attr_t[:, :], ps_attr[0:2 * R, 0:HE // 2], ACT.Copy).then_inc(attr_sb, 1)
                    a.wait_ge(hid_mm, h + 1)
                    if not first:
                        a.wait_ge(gate_mm, h - 1)
                    a.activation(hid[0:2 * H, par, :], ps_hid[0:2 * H, 0:HE // 2], ACT.Silu, bias=b1_pair[:, :]
                                 ).then_inc(hid_sb, 1)

                def back(h, par):
                    a.wait_ge(sum_mm, h + 1)
                    a.wait_ge(target_ready, h + 1)
                    a.activation(sums[0:TE, par, :, :], ps_sum[0:TE, 0:HT * (H + 1)]
                                 .rearrange("p (i f) -> p i f", f=H + 1), ACT.Copy).then_inc(sum_sb, 1)

                def counted(h, par, b):
                    if b is not None:
                        a.wait_ge(slab_out[par], 16 * b)
                    for k in range(HG):
                        a.wait_ge(count_mm, h * HG + k + 1)
                        a.sem_inc(act_passed, 1)
                        a.activation(slab[:, par, k, :], ps_count[0:TE + 1, k % 2, 0:GN * LO], ACT.Copy, saturate=True
                                     ).then_inc(slab_sb, 1)
                front(0, 0, True)
                counted(0, 0, None)
                front(1, 1, True)
                counted(1, 1, None)
                back(0, 0)
                with a.Fori(1, NB) as b:
                    front(2 * b, 0, False)
                    back(2 * b - 1, 1)
                    counted(2 * b, 0, b)
                    front(2 * b + 1, 1, False)
                    back(2 * b, 0)
                    counted(2 * b + 1, 1, b)
                back(NH - 1, 1)

            @block.vector
            def _(v):
                v.memset(hid[2 * H:2 * H + 1, :, :], 1.0)
                v.memset(hi_hot[:, :, TE, :], 1.0)
                v.wait_ge(iotas, 1)
                v.memset(sums[:, :, :, :], 0.0)
                v.memset(sums_y[:, :, :, :], 0.0)
                link(v.tensor_scalar(target[:, :, :].rearrange("p a i -> p (a i)"), zeros[:, 0:2 * HT], trash[:, :], None, ALU.add))
                v.tensor_scalar(dst_less[:, :], dst_c[:, :], trash[0:TE, :], None, ALU.subtract)
                link(v.tensor_scalar(src_less[:, :], src_c[:, :], trash[0:TE, :], None, ALU.subtract))

                def half(h, par, first, b):
                    n = [0]

                    def inner(ins):
                        n[0] += 1
                        ins.then_inc(dve_half, 1)
                        v.wait_ge(dve_half, h * LINKS + n[0])
                    v.wait_ge(loads[par], 48 * b + 48)
                    if not first:
                        v.wait_ge(z_mm, h - 1)
                    v.tensor_scalar(hi_t[:, par, :], hib[:, par, :], part_idx[0:TE, :], None, ALU.is_equal
                                    ).then_inc(hi_onehot, 1)
                    if not first:
                        v.wait_ge(sum_mm, h - 1)
                    for i in range(HT):
                        m = v.scalar_tensor_tensor(same[:, par, i, :], key_rows[:, par, TE * i:TE * i + TE],
                                                   src_c[:, bass.ds(h * HT + i, 1)], tri[0:TE, :], ALU.is_equal,
                                                   ALU.mult, accum_out=count[:, par, i:i + 1])
                    m.then_inc(same_ready, 1)
                    v.wait_ge(same_ready, h + 1)
                    inner(v.scalar_tensor_tensor(firsts[:, par, :], count[:, par, :], 1.0, cols(src_less, h), ALU.is_equal,
                                                 ALU.mult))
                    if not first:
                        for g in range(2):
                            v.wait_ge(added[g], (h - 1) * ADDS)
                    v.tensor_scalar(target[0:TE, par, :], firsts[:, par, :], trash[0:TE, :], None, ALU.add
                                    ).then_inc(target_ready, 1)
                    v.wait_ge(pairs_in[par], 16 * HG * b + 16 * HG)
                    v.tensor_tensor(code_in[:, par, :, :], pair_in[:, par, :, :, 0],
                                    group_code[:, bass.ds(h * HG, HG)].unsqueeze(2).to_broadcast([P, HG, GT]),
                                    ALU.subtract)
                    v.tensor_copy(hi_in[:, par, :, :], pair_in[:, par, :, :, 1]).then_inc(code_ready, 1)
                    v.wait_ge(code_ready, h + 1)
                    if not first:
                        v.wait_ge(count_mm, (h - 1) * HG)
                    v.tensor_tensor(hi_hot[:, par, 0:TE, :], hi_iota[:, :, :],
                                    hi_in[:, par, :, :].rearrange("p k i -> p (k i)").unsqueeze(1)
                                    .to_broadcast([P, TE, HG * GT]), ALU.is_equal)
                    for i in range(HG * GT):
                        m = v.tensor_scalar(code_hot[:, par, i, :], code_iota[:, :],
                                            code_in[:, par, i // GT, i % GT:i % GT + 1], None, ALU.is_equal)
                    m.then_inc(hot_ready, 1)
                    v.wait_ge(z_mm, h + 1)
                    for i in range(HT):
                        m = v.scalar_tensor_tensor(junk_lo[:, i, :], free_idx[0:TE, 0:LO], lo_c[:, bass.ds(h * HT + i, 1)],
                                                   ps_z[0:TE, LO * i:LO * i + LO], ALU.is_equal, ALU.mult,
                                                   accum_out=ztype[:, par, i:i + 1])
                    m.then_inc(z_read, 1)
                    v.wait_ge(z_read, h + 1)
                    v.wait_ge(gathered[par], 16 * HT * b + 16 * HT)
                    for i in range(HT):
                        m = v.scalar_tensor_tensor(junk_z[:, i, :], free_idx[0:TE, 0:NEL], ztype[:, par, i:i + 1],
                                                   gat[0:TE, par, i, H + 1:GW], ALU.is_equal, ALU.mult,
                                                   accum_out=adapt[:, par, i:i + 1])
                    inner(m)
                    v.wait_ge(gate_mm, h + 1)
                    for i in range(HT):
                        m = v.scalar_tensor_tensor(raw[:, i, :], ps_gate[0:TE, par, H * i:H * i + H], adapt[:, par, i:i + 1],
                                                   gat[0:TE, par, i, 0:H], ALU.add, ALU.mult)
                    m.then_inc(gate_read, 1)
                    v.wait_ge(gate_read, h + 1)
                    v.tensor_copy(msg[:, par, :, H:H + 1], gat[0:TE, par, :, H:H + 1])
                    inner(v.tensor_tensor(msg[:, par, :, 0:H], raw[:, :, :],
                                          cols(cw_c, h).unsqueeze(2).to_broadcast([TE, HT, H]), ALU.mult))
                    v.sem_inc(msg_ready, 1)
                    assert n[0] == LINKS
                half(0, 0, True, 0)
                half(1, 1, True, 0)
                with v.Fori(1, NB) as b:
                    half(2 * b, 0, False, b)
                    half(2 * b + 1, 1, False, b)

        def bc(a):
            return a.unsqueeze(2).to_broadcast([TE, LO, H])

        stage.close()
        with ExitStack() as nodes:
            tabs = nodes.enter_context(nc.sbuf_tensor("tabs", [TE, 2, LO * (H + 1)], F32))
            summed = nodes.enter_context(nc.sbuf_tensor("summed", [TE, LO * (H + 1)], F32))
            agg = nodes.enter_context(nc.sbuf_tensor("agg", [TE, LO, H + 1], F32))
            work = nodes.enter_context(nc.sbuf_tensor("work", [TE, LO, H], F32))
            sq1 = nodes.enter_context(nc.sbuf_tensor("sq1", [TE, LO, H], F32))
            last_row = nodes.enter_context(nc.sbuf_tensor("last_row", [TE, LO, LO], F8))
            last_row_f = nodes.enter_context(nc.sbuf_tensor("last_row_f", [TE, LO, LO], F32))
            ones_col = nodes.enter_context(nc.sbuf_tensor("ones_col", [P, 1], F32))
            flag_sum = nodes.enter_context(nc.sbuf_tensor("flag_sum", [1, 1], F32))
            biggest = nodes.enter_context(nc.sbuf_tensor("biggest", [TE, 1], F32))
            ps_flag = nodes.enter_context(nc.psum_tensor("ps_flag", [P, 512], F32))
            tabs_in = [sem("tabs_in0"), sem("tabs_in1")]
            tab_read, row_in, turned, flags_ready, flag_mm = (sem("tab_read"), sem("row_in"), sem("turned"),
                                                              sem("flags_ready"), sem("flag_mm"))
            with nc.Block() as block:

                @block.sync
                def _(sp):
                    sp.dma_start(last_row[:, :, :].rearrange("p q j -> p (q j)").bitcast(I16)
                                 .rearrange("p (q j) -> p q j", q=LO),
                                 counts[TE, 0:N * LO // 2].rearrange("(q m j) -> m q j", m=TE, j=LO // 2)
                                 ).then_inc(row_in, 16)
                    for i in range(NTAB):
                        if i >= 2:
                            sp.wait_ge(tab_read, i - 1)
                        sp.dma_start(tabs[:, i % 2, :], msg_acc[i][0:N, :].rearrange("(p j) f -> p (j f)", j=LO)
                                     ).then_inc(tabs_in[i % 2], 16)
                    sp.wait_ge(tab_read, NTAB)
                    sp.dma_start(sum_tab.rearrange("(p j) f -> p (j f)", j=LO), summed[:, :]).then_inc(turned, 16)
                    sp.wait_ge(turned, 16)
                    sp.dma_start(agg[:, :, :], sum_tab.rearrange("(j p) f -> p j f", p=TE)).then_inc(turned, 16)

                @block.scalar
                def _(a):
                    root(a, 2)
                    root(a, 3)
                    root(a, 4)

                @block.tensor
                def _(t):
                    t.wait_ge(flags_ready, 1)
                    t.matmul(ps_flag[0:1, 0:3], ones_col[:, :], flags[:, :], start=True, stop=True).then_inc(flag_mm, 1)

                @block.vector
                def _(v):
                    v.memset(ones_col[:, :], 1.0)
                    v.wait_ge(row_in, 16)
                    link(v.tensor_copy(last_row_f[:, :, :], last_row[:, :, :]))
                    link(v.tensor_reduce(indeg[:, :], last_row_f[:, :, :], AX.X, ALU.add))
                    link(v.tensor_reduce(biggest[:, :], last_row_f[:, :, :], AX.XY, ALU.max))
                    link(v.tensor_scalar(flags[0:TE, 2:3], biggest[:, :], float(FINE), None, ALU.is_ge))
                    v.sem_inc(flags_ready, 1)
                    v.wait_ge(flag_mm, 1)
                    link(v.tensor_reduce(flag_sum[:, :], ps_flag[0:1, 0:3], AX.X, ALU.add))
                    link(v.tensor_copy(flag_i[:, :], flag_sum[:, :]))
                    link(v.tensor_scalar(stat[:, 0, :], indeg[:, :], 1.0, None, ALU.add))
                    v.sem_inc(root_asked, 1)
                    roots[0] += 1
                    v.wait_ge(root_done, roots[0])
                    link(v.reciprocal(dinv[:, :], stat[:, 1, :]))
                    for i in range(NTAB):
                        v.wait_ge(tabs_in[i % 2], 16 * (i // 2 + 1))
                        if i >= 1:
                            v.wait_ge(tab_read, i)
                            m = v.tensor_tensor(summed[:, :], summed[:, :], tabs[:, i % 2, :], ALU.add)
                        else:
                            m = v.tensor_copy(summed[:, :], tabs[:, 0, :])
                        m.then_inc(tab_read, 1)
                    v.wait_ge(turned, 32)
                    link(v.tensor_scalar(stat[:, 0, :].unsqueeze(2), agg[:, :, H:H + 1], 1e-8, None, ALU.max))
                    link(v.reciprocal(stat[:, 1, :], stat[:, 0, :]))
                    link(v.tensor_tensor(work[:, :, :], agg[:, :, 0:H], bc(stat[:, 1, :]), ALU.mult))
                    link(v.tensor_tensor(hn[:, :, :], hn[:, :, :], work[:, :, :], ALU.add))
                    layer_norm(v, hn[:, :, :], work[:, :, :], sq1[:, :, :])
                    link(v.tensor_tensor(work[:, :, :], work[:, :, :], gamma_b[0:TE, :].unsqueeze(1)
                                         .to_broadcast([TE, LO, H]), ALU.mult))
                    link(v.tensor_tensor(work[:, :, :], work[:, :, :], beta_b[0:TE, :].unsqueeze(1)
                                         .to_broadcast([TE, LO, H]), ALU.add))
                    link(v.tensor_tensor(xn[:, :, :], xn[:, :, :], work[:, :, :], ALU.add))
                    layer_norm(v, xn[:, :, :], hn[:, :, :], sq1[:, :, :])
                    link(v.tensor_scalar(hn[:, :, :], hn[:, :, :], 0.0, None, ALU.max))

        env = locals()
        over_edges = propagate_edges(nc, env)
        over_counts = propagate_counts(nc, env)
        with nc.Block() as block:
            for name in ("sync", "gpsimd", "tensor", "scalar", "vector"):
                def program(eng, name=name):
                    flag = eng.value_load(flag_i[0:1, 0:1], min_val=0, max_val=3 * P)
                    before = steps[0]
                    with eng.If(flag == 0):
                        over_counts[name](eng)
                    steps[0] = before
                    with eng.Else():
                        over_edges[name](eng)
                block_part(block, name)(program)


def block_part(block, name):
    return {"sync": block.sync, "gpsimd": block.gpsimd, "tensor": block.tensor, "scalar": block.scalar,
            "vector": block.vector}[name]


def propagate_edges(nc, env):
    (sem, root, link, bc, cols) = (env[k] for k in ("sem", "root", "link", "bc", "cols"))
    (dst_c, dst_rows, src_i, prop_acc, y_tab, zeros, tri, trash, xn, hn, dinv, stat, out) = (
        env[k] for k in ("dst_c", "dst_rows", "src_i", "prop_acc", "y_tab", "zeros", "tri", "trash", "xn",
                         "hn", "dinv", "stat", "out"))
    NH = env["NH"]
    QT = HT // 4
    mine = ExitStack()

    def sb(name, shape, dt=F32):
        return mine.enter_context(nc.sbuf_tensor(name, shape, dt))
    key_rows = sb("e_key_rows", [TE, 2, HE], I16)
    same = sb("e_same", [TE, 2, HT, TE])
    count, firsts = sb("e_count", [TE, 2, HT]), sb("e_firsts", [TE, 2, HT])
    target, gat_idx = sb("e_target", [P, 2, HT], I32), sb("e_gat_idx", [P, 2, HT], I32)
    gat_y, sums_y = sb("e_gat_y", [P, 2, HT, H]), sb("e_sums_y", [P, 2, HT, H])
    dst_less = sb("e_dst_less", [TE, T])
    ps_sum = mine.enter_context(nc.psum_tensor("e_ps_sum", [P, 2, 512], F32))
    yn = mine.enter_context(nc.sbuf_tensor("yn_e", [TE, LO, H], F32))
    acc = mine.enter_context(nc.sbuf_tensor("acc_e", [TE, LO, H], F32))
    tabs = mine.enter_context(nc.sbuf_tensor("tabs_e", [TE, 2, LO, H], F32))
    keys = [sem("keys_even"), sem("keys_odd")]
    same_ready, sum_mm, sum_sb = sem("p_same_ready"), sem("p_sum_mm"), sem("p_sum_sb")
    gathered = [[sem(f"p_gathered_{x}{q}") for q in range(4)] for x in ("even", "odd")]
    idx_copied, target_ready, pool_passed = sem("p_idx_copied"), sem("p_target_ready"), sem("p_pool_passed")
    added = [sem(f"p_added{q}") for q in range(4)]
    tabs_in, tab_read = [sem("p_tabs_even"), sem("p_tabs_odd")], sem("p_tab_read")
    y_ready, y_stored, rezeroed, node_step, first_ready, stored, out_ready = (
        sem("y_ready"), sem("y_stored"), sem("rezeroed"), sem("node_step"), sem("first_ready"), sem("stored"),
        sem("out_ready"))
    NODE = 5

    def sync(sp):
        def edges(s):
            def load(h, par, first):
                if not first:
                    sp.wait_ge(same_ready, s * NH + h - 1)
                    sp.sem_inc(env["sp_passed"], 1)
                sp.dma_start(key_rows[:, par, :], dst_rows[bass.ds(h * HT, HT), :].rearrange("t e -> (t e)")
                             .partition_broadcast(TE)).then_inc(keys[par], 16)
            load(0, 0, True)
            load(1, 1, True)
            with sp.Fori(1, NB) as b:
                load(2 * b, 0, False)
                load(2 * b + 1, 1, False)

        def between(s):
            for q in range(4):
                sp.wait_ge(added[q], (s + 1) * (NH * 16 * QT))
                sp.sem_inc(env["sp_passed"], 1)
            for i in range(NTAB):
                if i >= 2:
                    sp.wait_ge(tab_read, s * NTAB + i - 1)
                    sp.sem_inc(env["sp_passed"], 1)
                sp.dma_start(tabs[:, i % 2, :, :], prop_acc[i][0:N, :].rearrange("(j p) f -> p j f", p=TE)
                             ).then_inc(tabs_in[i % 2], 16)
            for i in range(2):
                sp.wait_ge(tabs_in[i], (s + 1) * (16 * NTAB // 2))
                sp.sem_inc(env["sp_passed"], 1)
            for t in prop_acc:
                sp.dma_start(t.rearrange("(p r) f -> p (r f)", p=P), zeros[:, 0:ACC_ROWS // P * H]
                             ).then_inc(rezeroed, 16)
            sp.wait_ge(y_ready, s + 2)
            sp.sem_inc(env["sp_passed"], 1)
            sp.dma_start(y_tab.rearrange("(j p) f -> p j f", p=TE), yn[:, :, :]).then_inc(y_stored, 16)
            sp.wait_ge(rezeroed, (s + 1) * (16 * NTAB))
            sp.wait_ge(y_stored, s * 16 + 32)
            sp.sem_inc(env["sp_passed"], 1)
        sp.wait_ge(y_ready, 1)
        sp.dma_start(y_tab.rearrange("(j p) f -> p j f", p=TE), yn[:, :, :]).then_inc(y_stored, 16)
        edges(0)
        between(0)
        with sp.Fori(1, K + 1) as s:
            edges(s)
            between(s)
        sp.wait_ge(out_ready, 1)
        sp.dma_start(out.rearrange("(j p) f -> p j f", p=TE), xn[:, :, :]).then_inc(stored, 16)
        sp.wait_ge(stored, 16)

    def gpsimd(p):
        def edges(s):
            p.wait_ge(y_stored, s * 16 + 16)
            if not isinstance(s, int):
                p.wait_ge(rezeroed, s * (16 * NTAB))

            def gather(h, par, first):
                g = s * NH + h
                if not first:
                    p.wait_ge(sum_mm, g - 1)
                p.sem_inc(pool_passed, 1)
                p.tensor_copy(gat_idx[:, par, :], cols(src_i, h, P)).then_inc(idx_copied, 1)
                p.wait_ge(idx_copied, g + 1)
                p.sem_inc(pool_passed, 1)
                for i in range(HT):
                    p.indirect_dma_start(gat_y[:, par, i, :], None, y_tab,
                                         bass.IndirectOffsetOnAxis(ap=gat_idx[:, par, i:i + 1], axis=0)
                                         ).then_inc(gathered[par][i // QT], 16)

            def scatter(h, par, first):
                g = s * NH + h
                p.wait_ge(sum_sb, g + 2)
                p.wait_ge(target_ready, g + 1)
                for q in range(4):
                    if not first:
                        p.wait_ge(added[q], g * (16 * QT))
                    p.sem_inc(pool_passed, 1)
                    for i in range(QT * q, QT * (q + 1)):
                        p.indirect_dma_start(prop_acc[i], bass.IndirectOffsetOnAxis(ap=target[:, par, i:i + 1], axis=0),
                                             sums_y[:, par, i, :], None, compute_op=ALU.add
                                             ).then_inc(added[q], 16)
            gather(0, 0, True)
            gather(1, 1, True)
            scatter(0, 0, True)
            with p.Fori(1, NB) as b:
                gather(2 * b, 0, False)
                scatter(2 * b - 1, 1, False)
                gather(2 * b + 1, 1, False)
                scatter(2 * b, 0, False)
            scatter(NH - 1, 1, False)
        edges(0)
        with p.Fori(1, K + 1) as s:
            edges(s)

    def tensor(t):
        def edges(s):
            def combine(h, par, b, first):
                g = s * NH + h
                t.wait_ge(same_ready, g + 1)
                for q in range(4):
                    t.wait_ge(gathered[par][q], (s * NB + b + 1) * (16 * QT))
                if not first:
                    t.wait_ge(sum_sb, g)
                for i in range(HT):
                    m = t.matmul(ps_sum[0:TE, par, H * i:H * (i + 1)], same[:, par, i, :], gat_y[0:TE, par, i, :],
                                 start=True, stop=True)
                m.then_inc(sum_mm, 1)
            combine(0, 0, 0, True)
            combine(1, 1, 0, True)
            with t.Fori(1, NB) as b:
                combine(2 * b, 0, b, False)
                combine(2 * b + 1, 1, b, False)
        t.sem_inc(sum_sb, 1)
        edges(0)
        with t.Fori(1, K + 1) as s:
            edges(s)

    def scalar(a):
        def edges(s):
            def back(h, par):
                a.wait_ge(sum_mm, s * NH + h + 1)
                a.wait_ge(target_ready, s * NH + h + 1)
                a.activation(sums_y[0:TE, par, :, :], ps_sum[0:TE, par, 0:HT * H]
                             .rearrange("p (i f) -> p i f", f=H), ACT.Copy).then_inc(sum_sb, 1)
            with a.Fori(0, NB) as b:
                back(2 * b, 0)
                back(2 * b + 1, 1)
        edges(0)
        root(a, 5)
        with a.Fori(1, K + 1) as s:
            edges(s)

    def vector(v):
        def edges(s):
            def half(h, par, first):
                g = s * NH + h
                v.wait_ge(keys[par], (s * NH + (h - par)) * 8 + 16)
                if not first:
                    v.wait_ge(sum_mm, g - 1)
                for i in range(HT):
                    m = v.scalar_tensor_tensor(same[:, par, i, :], key_rows[:, par, TE * i:TE * i + TE],
                                               dst_c[:, bass.ds(h * HT + i, 1)], tri[0:TE, :], ALU.is_equal,
                                               ALU.mult, accum_out=count[:, par, i:i + 1])
                m.then_inc(same_ready, 1)
                v.wait_ge(same_ready, g + 1)
                v.scalar_tensor_tensor(firsts[:, par, :], count[:, par, :], 1.0, cols(dst_less, h), ALU.is_equal,
                                       ALU.mult).then_inc(first_ready, 1)
                v.wait_ge(first_ready, g + 1)
                if not first:
                    for q in range(4):
                        v.wait_ge(added[q], (g - 1) * (16 * QT))
                v.tensor_scalar(target[0:TE, par, :], firsts[:, par, :], trash[0:TE, :], None, ALU.add
                                ).then_inc(target_ready, 1)
            half(0, 0, True)
            half(1, 1, True)
            with v.Fori(1, NB) as b:
                half(2 * b, 0, False)
                half(2 * b + 1, 1, False)

        def collect(s):
            for i in range(NTAB):
                v.wait_ge(tabs_in[i % 2], s * (16 * NTAB // 2) + 16 * (i // 2 + 1))
                if i == 0:
                    m = v.tensor_copy(acc[:, :, :], tabs[:, 0, :, :])
                else:
                    v.wait_ge(tab_read, s * NTAB + i)
                    m = v.tensor_tensor(acc[:, :, :], acc[:, :, :], tabs[:, i % 2, :, :], ALU.add)
                m.then_inc(tab_read, 1)
            v.wait_ge(tab_read, s * NTAB + NTAB)

        v.memset(sums_y[:, :, :, :], 0.0)
        link(v.tensor_scalar(target[:, :, :].rearrange("p a i -> p (a i)"), zeros[:, 0:2 * HT], trash[:, :], None,
                             ALU.add))
        link(v.tensor_scalar(dst_less[:, :], dst_c[:, :], trash[0:TE, :], None, ALU.subtract))
        v.memset(yn[:, :, :], 1.0).then_inc(y_ready, 1)
        edges(0)
        collect(0)
        link(v.tensor_scalar(stat[:, 0, :].unsqueeze(2), acc[:, :, 0:1], 1.0, None, ALU.add))
        v.sem_inc(env["root_asked"], 1)
        v.wait_ge(env["root_done"], 5)
        link(v.reciprocal(dinv[:, :], stat[:, 1, :]))
        v.wait_ge(y_stored, 16)
        v.tensor_tensor(yn[:, :, :], hn[:, :, :], bc(dinv[:, :]), ALU.mult).then_inc(y_ready, 1)
        with v.Fori(1, K + 1) as s:
            edges(s)
            collect(s)
            n = [0]

            def step(ins):
                n[0] += 1
                ins.then_inc(node_step, 1)
                v.wait_ge(node_step, (s - 1) * NODE + n[0])
            step(v.tensor_tensor(acc[:, :, :], acc[:, :, :], yn[:, :, :], ALU.add))
            step(v.tensor_tensor(acc[:, :, :], acc[:, :, :], bc(dinv[:, :]), ALU.mult))
            step(v.tensor_scalar(acc[:, :, :], acc[:, :, :], 1.0 - ALPHA, None, ALU.mult))
            step(v.scalar_tensor_tensor(acc[:, :, :], hn[:, :, :], ALPHA, acc[:, :, :], ALU.mult, ALU.add))
            v.wait_ge(y_stored, s * 16 + 16)
            step(v.tensor_tensor(yn[:, :, :], acc[:, :, :], bc(dinv[:, :]), ALU.mult))
            v.sem_inc(y_ready, 1)
            assert n[0] == NODE
        v.tensor_tensor(xn[:, :, :], xn[:, :, :], acc[:, :, :], ALU.add).then_inc(out_ready, 1)
    mine.close()
    return {"sync": sync, "gpsimd": gpsimd, "tensor": tensor, "scalar": scalar, "vector": vector}


def propagate_counts(nc, env):
    sem, link, bc = env["sem"], env["link"], env["bc"]
    counts, xn, hn, dinv, out = (env[k] for k in ("counts", "xn", "hn", "dinv", "out"))
    mine = ExitStack()

    def sb(name, shape, dt=F32):
        return mine.enter_context(nc.sbuf_tensor(name, shape, dt))
    RING = 5
    PARTS = ((0, 3), (3, 5))
    IT = LO // RING
    CH = TE * LO
    chunk = sb("chunk", [TE, RING, TE, LO], F8)
    y3 = sb("y3", [TE, 2, LO, 3 * H], BF16)
    yn = sb("yn", [TE, LO, H])
    more = sb("more", [TE, LO, H])
    scale = sb("scale", [TE, 2, LO])
    t1, t2 = sb("t1", [TE, 3, H]), sb("t2", [TE, 3, H])
    ps = mine.enter_context(nc.psum_tensor("ps_prop", [P, RING, 512], F32))
    chunk_in = [sem(f"chunk_in{i}") for i in range(RING)]
    chunk_mm, ps_read, y_ready, c_step, out_ready, out_stored = (
        sem("chunk_mm"), sem("ps_read"), sem("c_y_ready"), sem("c_step"), sem("c_out_ready"), sem("c_out_stored"))
    NP = len(PARTS) * IT
    LINKS, LAST_LINKS = 8, 3

    def sync(sp):
        def load(step, it, first):
            for i in range(RING):
                if not first:
                    sp.wait_ge(chunk_mm, (step * IT + it - 1) * RING + i + 1)
                    sp.sem_inc(env["sp_passed"], 1)
                sp.dma_start(chunk[:, i, :, :].rearrange("p m j -> p (m j)").bitcast(I16),
                             counts[0:TE, bass.ds(it * (RING * CH // 2) + i * (CH // 2), CH // 2)]
                             ).then_inc(chunk_in[i], 16)
        load(0, 0, True)
        with sp.Fori(1, IT) as it:
            load(0, it, False)
        with sp.Fori(1, K) as step:
            with sp.Fori(0, IT) as it:
                load(step, it, False)
        sp.wait_ge(out_ready, NP)
        sp.dma_start(out.rearrange("(j p) f -> p j f", p=TE), yn[:, :, :]).then_inc(out_stored, 16)
        sp.wait_ge(out_stored, 16)

    def tensor(t):
        def chunks(step, par, it, first, start):
            n = step * IT + it
            for i in range(RING):
                part = 0 if i < PARTS[0][1] else 1
                t.wait_ge(chunk_in[i], n * 16 + 16)
                if not first:
                    t.wait_ge(ps_read, (n - 1) * 2 + part + 1)
                t.sem_inc(env["pe_passed"], 1)
                for j in range(LO):
                    if start and i == 0 and j % RING in (PARTS[0][0], PARTS[1][0]):
                        t.wait_ge(y_ready, step * NP + j // RING * 2 + (j % RING > 0) + 1)
                        t.sem_inc(env["pe_passed"], 1)
                    m = t.matmul(ps[0:TE, i, 0:3 * H], chunk[:, i, :, j], y3[:, par, j, :], start=(j == 0),
                                 stop=(j == LO - 1))
                m.then_inc(chunk_mm, 1)

        def one_step(step, par, first):
            chunks(step, par, 0, first, True)
            with t.Fori(1, IT) as it:
                chunks(step, par, it, False, False)
        one_step(0, 0, True)
        with t.Fori(0, (K - 1) // 2) as pair:
            one_step(2 * pair + 1, 1, False)
            one_step(2 * pair + 2, 0, False)

    def vector(v):
        def split(par, q, n, link_to):
            at = bass.ds(q, n)
            hi, mid, lo = (y3[:, par, at, H * k:H * k + H] for k in range(3))
            link_to(v.tensor_copy(hi, yn[:, at, :]))
            link_to(v.tensor_tensor(t1[:, 0:n, :], yn[:, at, :], hi, ALU.subtract))
            link_to(v.tensor_copy(mid, t1[:, 0:n, :]))
            link_to(v.tensor_tensor(t2[:, 0:n, :], t1[:, 0:n, :], mid, ALU.subtract))
            return v.tensor_copy(lo, t2[:, 0:n, :])

        def parts(step, par, it, last):
            for part, (a, b) in enumerate(PARTS):
                n, count = b - a, [0]
                number = (step * IT + it) * 2 + part
                q = it * RING + a
                at = bass.ds(q, n)

                def inner(ins):
                    count[0] += 1
                    ins.then_inc(c_step, 1)
                    v.wait_ge(c_step, (K - 1) * NP * LINKS + (it * 2 + part) * LAST_LINKS + count[0] if last
                              else number * LINKS + count[0])
                v.wait_ge(chunk_mm, (step * IT + it) * RING + b)
                inner(v.tensor_tensor(t1[:, 0:n, :], ps[0:TE, a:b, 0:H], yn[:, at, :], ALU.add))
                inner(v.tensor_tensor(t2[:, 0:n, :], ps[0:TE, a:b, H:2 * H], t1[:, 0:n, :], ALU.add))
                v.tensor_tensor(t1[:, 0:n, :], ps[0:TE, a:b, 2 * H:3 * H], t2[:, 0:n, :], ALU.add).then_inc(ps_read, 1)
                v.wait_ge(ps_read, number + 1)
                inner(v.tensor_tensor(t2[:, 0:n, :], t1[:, 0:n, :],
                                      scale[:, int(last), at].unsqueeze(2).to_broadcast([TE, n, H]), ALU.mult))
                if last:
                    v.tensor_tensor(yn[:, at, :], t2[:, 0:n, :], more[:, at, :], ALU.add).then_inc(out_ready, 1)
                    assert count[0] == LAST_LINKS
                else:
                    inner(v.tensor_tensor(yn[:, at, :], t2[:, 0:n, :], more[:, at, :], ALU.add))
                    split(1 - par, q, n, inner).then_inc(y_ready, 1)
                    v.wait_ge(y_ready, (step + 1) * NP + it * 2 + part + 1)
                    assert count[0] == LINKS

        link(v.tensor_tensor(scale[:, 0, :], dinv[:, :], dinv[:, :], ALU.mult))
        link(v.tensor_scalar(scale[:, 0, :], scale[:, 0, :], 1.0 - ALPHA, None, ALU.mult))
        link(v.tensor_scalar(scale[:, 1, :], dinv[:, :], 1.0 - ALPHA, None, ALU.mult))
        link(v.tensor_tensor(yn[:, :, :], hn[:, :, :], bc(dinv[:, :]), ALU.mult))
        for it in range(IT):
            for a, b in PARTS:
                split(0, RING * it + a, b - a, link).then_inc(y_ready, 1)
                v.wait_ge(y_ready, it * 2 + (a > 0) + 1)
        link(v.tensor_scalar(more[:, :, :], yn[:, :, :], ALPHA, None, ALU.mult))

        def one_step(step, par):
            with v.Fori(0, IT) as it:
                parts(step, par, it, False)
        with v.Fori(0, (K - 1) // 2) as pair:
            one_step(2 * pair, 0)
            one_step(2 * pair + 1, 1)
        link(v.scalar_tensor_tensor(more[:, :, :], hn[:, :, :], ALPHA, xn[:, :, :], ALU.mult, ALU.add))
        with v.Fori(0, IT) as it:
            parts(K - 1, 0, it, True)

    def scalar(a):
        pass

    def gpsimd(p):
        pass
    mine.close()
    return {"sync": sync, "gpsimd": gpsimd, "tensor": tensor, "scalar": scalar, "vector": vector}


_INS = ['x', 'src', 'dst', 'edge_attr_40', 'edge_weight', 'node_type_119', 'node_vec', 'L0_gnn_W1', 'L0_gnn_b1',
        'L0_gnn_W2', 'L0_gnn_b2', 'L0_gnn_emb', 'L0_gnn_adaptW', 'L0_gnn_gamma', 'L0_gnn_beta']
_OUTS = [((N, H), 'float32')]


def kernel(**inputs):
    import numpy as _np
    import concourse.bacc as _bacc
    from concourse import mybir as _mybir
    from concourse.bass_utils import run_bass_kernel_spmd as _run

    nc = _bacc.Bacc("TRN2", target_bir_lowering=False, num_devices=1)
    arrays, args = {}, []
    for name in _INS:
        a = _np.ascontiguousarray(inputs[name])
        arrays[f"in_{name}_dram"] = a
        args.append(nc.dram_tensor(f"in_{name}_dram", a.shape, _mybir.dt.from_np(a.dtype), kind="ExternalInput").ap())
    for i, (shape, dtype) in enumerate(_OUTS):
        dt = _mybir.dt.from_np(_np.dtype(dtype))
        args.append(nc.dram_tensor(f"out_{i}_dram", shape, dt, kind="ExternalOutput").ap())
    build(nc, *args)
    r = _run(nc, [arrays], core_ids=[0])
    got = tuple(r.results[0][f"out_{i}_dram"] for i in range(len(_OUTS)))
    return got[0]
```

```python
from contextlib import ExitStack

import concourse.bass as bass
from concourse import mybir

F32 = mybir.dt.float32
BF16 = mybir.dt.bfloat16
I32 = mybir.dt.int32
I16 = mybir.dt.int16
F16 = mybir.dt.float16
F8 = mybir.dt.float8e4
ALU = mybir.AluOpType
ACT = mybir.ActivationFunctionType
AX = mybir.AxisListType

P = 128
N = 6250
E = 200000
H = 48
R = 40
NEL = 119
G = 32
TE = 125
LO = N // TE
HT = 8
HE = HT * TE
BT = 2 * HT
NB = E // (BT * TE)
T = E // TE
GW = H + 1 + NEL
ACC_ROWS = 6400
NTAB = HT
K = 5
GN = 8
GT = 3
HG = 4
NG = HG * E // HE
QG = 7
FINE = 16
ALPHA = 0.8
CUTOFF = 6.0
LN_EPS = 1e-5
PI = 3.141592653589793
ROUND = 12582912.0


def build(nc, x, src, dst, edge_attr, edge_weight, node_type, node_vec, W1, b1, W2, b2, emb, adaptW,
          gamma, beta, out):
    node_parts = nc.dram_tensor("node_parts", (N + P, 3 * GW), BF16).ap()
    y_tab = nc.dram_tensor("y_tab", (N, H), F32).ap()
    logit_tab = nc.dram_tensor("logit_tab", (NEL, 3 * GW), BF16).ap()
    msg_acc = [nc.dram_tensor(f"msg_acc{i}", (ACC_ROWS, H + 1), F32).ap() for i in range(NTAB)]
    prop_acc = [nc.dram_tensor(f"prop_acc{i}", (ACC_ROWS, H), F32).ap() for i in range(NTAB)]
    src_rows = nc.dram_tensor("src_rows", (T, TE), I16).ap()
    dst_rows = nc.dram_tensor("dst_rows", (T, TE), I16).ap()
    hi_rows = nc.dram_tensor("hi_rows", (T, TE), BF16).ap()
    code_pairs = nc.dram_tensor("code_pairs", (E + GT * P, 2), F32).ap()
    first_edges = nc.dram_tensor("first_edges", (QG * P,), I32).ap()
    counts = nc.dram_tensor("counts", (TE + 1, NG * GN * LO // 2), I16).ap()
    sum_tab = nc.dram_tensor("sum_tab", (N, H + 1), F32).ap()

    with ExitStack() as ctx:
        def sb(name, shape, dt=F32):
            return ctx.enter_context(nc.sbuf_tensor(name, shape, dt))

        def sem(name):
            return ctx.enter_context(nc.semaphore(name))

        part_idx = sb("part_idx", [P, 1])
        free_idx = sb("free_idx", [P, P])
        ident = sb("ident", [P, P])
        tri = sb("tri", [P, TE])
        trash = sb("trash", [P, 1])
        zeros = sb("zeros", [P, ACC_ROWS // P * (H + 1)])
        half_pi = sb("half_pi", [P, 1])
        flags = sb("flags", [P, 4])
        flag_i = sb("flag_i", [1, 2], I32)
        flag_f = sb("flag_f", [1, 2])
        ones_col = sb("ones_col", [P, 1])
        window_row = sb("window_row", [1, NB], I32)
        window_col = sb("window_col", [P, NB])
        first_row = sb("first_row", [1, QG * P], I32)
        indeg = sb("indeg", [TE, LO])
        eps = sb("eps", [P, 1])
        w1_pair = sb("w1_pair", [2 * R, 2 * H])
        w2_pair = sb("w2_pair", [2 * H + 1, 2 * H])
        b1_pair = sb("b1_pair", [2 * H, 1])
        emb_t = sb("emb_t", [G, NEL])
        adapt_t = sb("adapt_t", [G, G])
        gamma_b = sb("gamma_b", [P, H])
        beta_b = sb("beta_b", [P, H])
        q_t = sb("q_t", [G, NEL])
        xn = sb("xn", [TE, LO, H])
        hn = sb("hn", [TE, LO, H])
        mult = sb("mult", [TE, LO])
        ntype = sb("ntype", [P, LO], I32)
        ntype_bf = sb("ntype_bf", [TE, LO], BF16)
        stat = sb("stat", [TE, 4, LO])
        dinv = sb("dinv", [TE, LO])
        src_i = sb("src_i", [P, T], I32)
        dst_i = sb("dst_i", [P, T], I32)
        src_c = sb("src_c", [TE, T])
        dst_c = sb("dst_c", [TE, T])
        lo_c = sb("lo_c", [TE, T])
        cw_c = sb("cw_c", [TE, T])

        dve_step = sem("dve_step")
        steps = [0]

        def link(ins):
            steps[0] += 1
            ins.then_inc(dve_step, 1)
            nc.vector.wait_ge(dve_step, steps[0])

        def layer_norm(v, xin, y, sq):
            def bc(a):
                return a.unsqueeze(2).to_broadcast([TE, LO, H])
            link(v.tensor_reduce(stat[:, 0, :], xin, AX.X, ALU.add))
            link(v.tensor_scalar(stat[:, 1, :], stat[:, 0, :], 1.0 / H, None, ALU.mult))
            link(v.tensor_tensor(y, xin, bc(stat[:, 1, :]), ALU.subtract))
            link(v.tensor_tensor(sq, y, y, ALU.mult))
            link(v.tensor_reduce(stat[:, 2, :], sq, AX.X, ALU.add))
            link(v.tensor_scalar(stat[:, 0, :], stat[:, 2, :], 1.0 / H, LN_EPS, ALU.mult, ALU.add))
            v.sem_inc(root_asked, 1)
            roots[0] += 1
            v.wait_ge(root_done, roots[0])
            link(v.reciprocal(stat[:, 3, :], stat[:, 1, :]))
            link(v.tensor_tensor(y, y, bc(stat[:, 3, :]), ALU.mult))

        root_asked, root_done, roots = sem("root_asked"), sem("root_done"), [0]

        def root(a, n):
            a.wait_ge(root_asked, n)
            a.activation(stat[:, 1, :], stat[:, 0, :], ACT.Sqrt).then_inc(root_done, 1)

        with ExitStack() as setup:
            def ssb(name, shape, dt=F32):
                return setup.enter_context(nc.sbuf_tensor(name, shape, dt))

            sq = ssb("sq", [TE, LO, H + 1])
            rest, logit_parts = ssb("rest", [NEL, 3, NEL]), ssb("logit_parts", [NEL, 3, GW], BF16)
            rows = ssb("rows", [TE, LO, H + 1])
            image = ssb("image", [TE, LO, 3, GW], BF16)
            window_end_i = ssb("window_end_i", [1, NB], I32)
            window_f = ssb("window_f", [1, 2, NB])
            hi_c = ssb("hi_c", [TE, T])
            pair = ssb("pair", [TE, T, 2])
            no_pair = ssb("no_pair", [P, 2 * GT])
            ones_row = ssb("ones_row", [1, P])
            dst_flat = ssb("dst_flat", [TE, T], I32)
            dst_next = ssb("dst_next", [TE, T], I32)
            below = ssb("below", [P, T], BF16)
            group_node = ssb("group_node", [P, QG + 1])
            tiles_below, tile_at = ssb("tiles_below", [P, QG + 1]), ssb("tile_at", [P, QG + 1])
            tile_at_i = ssb("tile_at_i", [P, QG + 1], I32)
            found = ssb("found", [P, QG + 1, TE], I32)
            edges_below, first_at = ssb("edges_below", [P, QG + 1]), ssb("first_at", [P, QG + 1])
            first_at_i = ssb("first_at_i", [P, QG + 1], I32)
            loaded_order, pair_ready, firsts_ready, firsts_mm = (sem("loaded_order"), sem("pair_ready"), sem("firsts_ready"),
                                                                 sem("firsts_mm"))
            windows_mm, flags_ready, flag_mm = sem("windows_mm"), sem("flags_ready"), sem("flag_mm")
            tile_known, tile_found, first_known, first_out = (sem("tile_known"), sem("tile_found"), sem("first_known"),
                                                              sem("first_out"))
            tile_first_i = rows[0:1, :, :].rearrange("o j f -> o (j f)").bitcast(I32)[:, 0:T]
            tile_first = sq[0:1, :, :].rearrange("o j f -> o (j f)")[:, 0:T]
            near = dst_flat[:, :].bitcast(F32)
            wt_c = ssb("wt_c", [TE, T])
            row_out = [ssb("src_out", [100, 16, TE], I16), ssb("dst_out", [100, 16, TE], I16),
                       ssb("hi_out", [100, 16, TE], BF16)]
            ps_row = setup.enter_context(nc.psum_tensor("ps_row", [P, 2, 4, P], F32))
            ps_q = setup.enter_context(nc.psum_tensor("ps_q", [P, 512], F32))
            ps_l = setup.enter_context(nc.psum_tensor("ps_l", [P, 512], F32))
            ps_first = setup.enter_context(nc.psum_tensor("ps_first", [P, 4, 512], F32))
            loaded_nodes, loaded_edges, loaded_weights = sem("loaded_nodes"), sem("loaded_edges"), sem("loaded_weights")
            consts, padded, qt_mm, qt_sb, logit_mm, logit_sb = (sem("consts"), sem("padded"), sem("qt_mm"), sem("qt_sb"),
                                                                sem("logit_mm"), sem("logit_sb"))
            logit_out, logit_rows, rows_ready, tables = sem("logit_out"), sem("logit_rows"), sem("rows_ready"), sem("tables")
            cols_ready, row_mm, row_copied, angle, sined = (sem("cols_ready"), sem("row_mm"), sem("row_copied"), sem("angle"),
                                                            sem("sined"))
            zeroed = sem("zeroed")
            rows_of = (src_c, dst_c, hi_c)
            WEIGHTS = 12
            with nc.allow_non_contiguous_dma(reason="weights of a few KB, transposed once"), nc.Block() as block:

                @block.sync
                def _(sp):
                    by_tile = "(b p i) -> p b i"
                    sp.wait_ge(padded, 3)
                    for a, t in ((dst, dst_i), (src, src_i)):
                        sp.dma_start(t[0:TE, :].rearrange("p (b i) -> p b i", i=BT),
                                     a.rearrange(by_tile, p=TE, i=BT)).then_inc(loaded_edges, 16)
                    sp.dma_start(wt_c[:, :].rearrange("p (b i) -> p b i", i=BT),
                                 edge_weight.rearrange(by_tile, p=TE, i=BT)).then_inc(loaded_edges, 16)
                    sp.wait_ge(padded, 4)
                    sp.dma_start(tile_first_i[:, :], dst.rearrange("(o t e) -> o t e", o=1, e=TE)[:, :, 0]
                                 ).then_inc(loaded_order, 16)
                    for t, e in ((window_row, 0), (window_end_i, BT * TE - 1)):
                        sp.dma_start(t[:, :], dst.rearrange("(o b e) -> o b e", o=1, b=NB)[:, :, e]
                                     ).then_inc(loaded_order, 16)
                    sp.dma_start(dst_flat[:, :], dst.rearrange("(p t) -> p t", t=T)).then_inc(loaded_order, 16)
                    sp.dma_start(dst_next[0:TE - 1, :], dst[1:1 + (TE - 1) * T].rearrange("(p t) -> p t", t=T)
                                 ).then_inc(loaded_order, 16)
                    sp.dma_start(dst_next[TE - 1:TE, 0:T - 1], dst[1 + (TE - 1) * T:E].unsqueeze(0)
                                 ).then_inc(loaded_order, 16)
                    sp.wait_ge(logit_sb, 1)
                    sp.dma_start(logit_tab, logit_parts[:, :, :].rearrange("p k f -> p (k f)")).then_inc(logit_out, 16)
                    sp.wait_ge(pair_ready, 1)
                    sp.dma_start(code_pairs[0:E, :].rearrange("(b p i) c -> p b (i c)", p=TE, i=BT),
                                 pair[:, :, :].rearrange("p (b i) c -> p b (i c)", i=BT)).then_inc(tables, 16)
                    sp.wait_ge(consts, 2)
                    sp.dma_start(code_pairs[E:E + GT * P, :].rearrange("(p i) c -> p (i c)", p=P), no_pair[:, :]
                                 ).then_inc(tables, 16)
                    for c in range(16):
                        sp.wait_ge(row_copied, 3 * (c + 1))
                        for d, t in zip((src_rows, dst_rows, hi_rows), row_out):
                            sp.dma_start(d[100 * c:100 * c + 100, :], t[:, c, :]).then_inc(tables, 16)
                    sp.wait_ge(first_known, 1)
                    sp.dma_start(first_edges.rearrange("(p c) -> p c", c=QG), first_at_i[:, 0:QG]).then_inc(first_out, 16)
                    sp.wait_ge(first_out, 16)
                    sp.dma_start(first_row[:, :], first_edges.unsqueeze(0)).then_inc(tables, 16)
                    for n, j in enumerate((0, LO // 2)):
                        sp.wait_ge(rows_ready, n + 1)
                        sp.dma_start(node_parts[TE * j:TE * (j + LO // 2), :].rearrange("(j p) f -> p j f", p=TE),
                                     image[:, j:j + LO // 2, :, :].rearrange("p j k f -> p j (k f)")
                                     ).then_inc(tables, 16)
                    sp.dma_start(node_parts[N:N + P, :], zeros[:, 0:3 * GW // 2].bitcast(BF16)).then_inc(tables, 16)
                    sp.wait_ge(tables, 16 * 54)
                    sp.wait_ge(zeroed, 16 * NTAB)

                @block.gpsimd
                def _(p):
                    p.memset(src_i[:, :], 0).then_inc(padded, 1)
                    p.memset(dst_i[:, :], 0).then_inc(padded, 1)
                    p.memset(ntype[:, :], 0).then_inc(padded, 1)
                    p.memset(dst_next[:, :], N).then_inc(padded, 1)
                    p.iota(group_node[:, :], [[GN, QG + 1]], 0, GN * QG, allow_small_or_imprecise_dtypes=True)
                    p.iota(part_idx[:, :], [[0, 1]], 0, 1, allow_small_or_imprecise_dtypes=True)
                    p.iota(trash[:, :], [[0, 1]], N, 1, allow_small_or_imprecise_dtypes=True)
                    p.iota(free_idx[:, :], [[1, P]], 0, 0, allow_small_or_imprecise_dtypes=True).then_inc(consts, 1)
                    def node_rows(a, b):
                        for j in range(a, b):
                            p.indirect_dma_start(image[:, j, :, :].rearrange("p k f -> p (k f)"), None, logit_tab,
                                                 bass.IndirectOffsetOnAxis(ap=ntype[0:TE, j:j + 1], axis=0)
                                                 ).then_inc(logit_rows, 16)
                    p.wait_ge(logit_out, 16)
                    p.wait_ge(loaded_nodes, 16 * 3)
                    node_rows(0, 2 * LO // 5)
                    p.wait_ge(tile_known, 1)
                    for c in range(QG + 1):
                        p.indirect_dma_start(found[:, c, :], None, dst.rearrange("(t e) -> t e", e=TE),
                                             bass.IndirectOffsetOnAxis(ap=tile_at_i[:, c:c + 1], axis=0)
                                             ).then_inc(tile_found, 16)
                    node_rows(2 * LO // 5, LO)

                @block.scalar
                def _(a):
                    a.wait_ge(padded, 3)
                    a.dma_start(xn[:, :, :], x.rearrange("(j p) f -> p j f", p=TE)).then_inc(loaded_nodes, 16)
                    a.dma_start(mult[:, :], node_vec.rearrange("(j p) -> p j", p=TE)).then_inc(loaded_nodes, 16)
                    a.dma_start(ntype[0:TE, :], node_type.rearrange("(j p) -> p j", p=TE)).then_inc(loaded_nodes, 16)
                    a.dma_start(emb_t[:, :], emb.rearrange("n g -> g n")).then_inc(loaded_weights, 16)
                    a.dma_start(adapt_t[:, :], adaptW.rearrange("i k -> k i")).then_inc(loaded_weights, 16)
                    a.wait_ge(consts, 2)
                    for s in range(2):
                        a.dma_start(w1_pair[R * s:R * s + R, H * s:H * s + H], W1.rearrange("h r -> r h")
                                    ).then_inc(loaded_weights, 16)
                        a.dma_start(w2_pair[H * s:H * s + H, H * s:H * s + H], W2.rearrange("o i -> i o")
                                    ).then_inc(loaded_weights, 16)
                        a.dma_start(w2_pair[2 * H:2 * H + 1, H * s:H * s + H], b2.unsqueeze(0)
                                    ).then_inc(loaded_weights, 16)
                        a.dma_start(b1_pair[H * s:H * s + H, :], b1.unsqueeze(1)).then_inc(loaded_weights, 16)
                    a.dma_start(gamma_b[:, :], gamma.partition_broadcast(P)).then_inc(loaded_weights, 16)
                    a.dma_start(beta_b[:, :], beta.partition_broadcast(P)).then_inc(loaded_weights, 16)
                    a.wait_ge(angle, 1)
                    a.activation(near[:, :], wt_c[:, :], ACT.Sin, bias=half_pi[0:TE, :],
                                 scale=-PI / CUTOFF).then_inc(sined, 1)
                    for t in msg_acc:
                        a.dma_start(t.rearrange("(p r) f -> p (r f)", p=P), zeros[:, :]).then_inc(zeroed, 16)
                    root(a, 1)
                    a.wait_ge(loaded_weights, 16 * WEIGHTS)
                    a.wait_ge(logit_out, 16)

                @block.tensor
                def _(t):
                    t.wait_ge(loaded_weights, 16 * WEIGHTS)
                    t.matmul(ps_q[0:G, 0:NEL], adapt_t[:, :], emb_t[:, :], start=True, stop=True).then_inc(qt_mm, 1)
                    t.wait_ge(qt_sb, 1)
                    t.matmul(ps_l[0:NEL, 0:NEL], q_t[:, :], emb_t[:, :], start=True, stop=True).then_inc(logit_mm, 1)
                    t.wait_ge(firsts_ready, 1)
                    for c in range(4):
                        m = t.matmul(ps_first[:, c, 0:T // 4], ones_row[:, :], tile_first[:, T // 4 * c:T // 4 * (c + 1)],
                                     start=True, stop=True)
                    m.then_inc(firsts_mm, 1)
                    t.matmul(ps_l[:, 128:128 + NB], ones_row[:, :], window_f[:, 0, :], start=True, stop=True
                             ).then_inc(windows_mm, 1)
                    t.wait_ge(cols_ready, 1)
                    for c in range(16):
                        if c >= 2:
                            t.wait_ge(row_copied, 3 * (c - 1))
                        for n, cols in enumerate(rows_of):
                            m = t.transpose(ps_row[0:100, c % 2, n, 0:TE], cols[:, 100 * c:100 * c + 100],
                                            ident[0:TE, 0:TE])
                        m.then_inc(row_mm, 1)
                    t.wait_ge(flags_ready, 1)
                    t.matmul(ps_l[0:1, 256:259], ones_col[:, :], flags[:, 0:3], start=True, stop=True
                             ).then_inc(flag_mm, 1)

                @block.vector
                def _(v):
                    def split(a, b, parts):
                        link(v.tensor_copy(parts[0], a))
                        link(v.tensor_tensor(b, a, parts[0], ALU.subtract))
                        link(v.tensor_copy(parts[1], b))
                        link(v.tensor_tensor(a, b, parts[1], ALU.subtract))
                        link(v.tensor_copy(parts[2], a))
                    v.memset(zeros[:, :], 0.0)
                    v.memset(flags[:, :], 0.0)
                    v.memset(ones_col[:, :], 1.0)
                    v.memset(ones_row[:, :], 1.0)
                    v.memset(no_pair[:, :], -1.0)
                    v.memset(logit_parts[:, :, :], 0.0)
                    v.memset(w1_pair[:, :], 0.0)
                    v.memset(w2_pair[:, :], 0.0)
                    v.memset(half_pi[:, :], PI / 2)
                    v.memset(eps[:, :], LN_EPS).then_inc(consts, 1)
                    v.wait_ge(consts, 2)
                    v.tensor_scalar(ident[:, :], free_idx[:, :], part_idx[:, 0:1], None, ALU.is_equal)
                    link(v.tensor_scalar(tri[:, :], free_idx[:, 0:TE], part_idx[:, 0:1], None, ALU.is_le))
                    v.wait_ge(loaded_edges, 16 * 3)
                    v.tensor_copy(src_c[:, :], src_i[0:TE, :])
                    link(v.tensor_copy(dst_c[:, :], dst_i[0:TE, :]))
                    link(v.tensor_scalar(hi_c[:, :], src_c[:, :], (TE - 1) / 2, 1.0 / TE, ALU.subtract, ALU.mult))
                    link(v.tensor_scalar(lo_c[:, :], hi_c[:, :], ROUND, ROUND, ALU.add, ALU.subtract))
                    link(v.scalar_tensor_tensor(hi_c[:, :], lo_c[:, :], -float(TE), src_c[:, :], ALU.mult, ALU.add))
                    v.sem_inc(cols_ready, 1)
                    v.tensor_copy(pair[:, :, 1], hi_c[:, :])
                    link(v.scalar_tensor_tensor(pair[:, :, 0], dst_c[:, :], float(LO), lo_c[:, :], ALU.mult, ALU.add))
                    v.sem_inc(pair_ready, 1)
                    v.wait_ge(qt_mm, 1)
                    v.tensor_copy(q_t[:, :], ps_q[0:G, 0:NEL]).then_inc(qt_sb, 1)
                    v.wait_ge(logit_mm, 1)
                    link(v.tensor_copy(rest[:, 0, :], ps_l[0:NEL, 0:NEL]))
                    split(rest[:, 0, :], rest[:, 1, :], [logit_parts[:, k, H + 1:GW] for k in range(3)])
                    v.sem_inc(logit_sb, 1)
                    v.wait_ge(loaded_order, 16 * 6)
                    v.tensor_copy(window_f[:, 0, :], window_row[:, :])
                    v.tensor_copy(window_f[:, 1, :], window_end_i[:, :])
                    link(v.tensor_copy(tile_first[:, :], tile_first_i[:, :]))
                    v.sem_inc(firsts_ready, 1)
                    v.tensor_tensor(below[0:TE, :], dst_flat[:, :], dst_next[:, :], ALU.is_gt).then_inc(dve_step, 1)
                    steps[0] += 1
                    v.wait_ge(dve_step, steps[0])
                    link(v.tensor_reduce(flags[0:TE, 0:1], below[0:TE, :], AX.X, ALU.max))
                    v.wait_ge(firsts_mm, 1)
                    for c in range(QG + 1):
                        link(v.tensor_scalar(below[:, :].rearrange("p (a b) -> p a b", a=4), ps_first[:, :, 0:T // 4],
                                             group_node[:, c:c + 1], 0.0, ALU.is_lt, ALU.add,
                                             accum_out=tiles_below[:, c:c + 1]))
                    link(v.tensor_scalar(tile_at[:, :], tiles_below[:, :], 1.0, 0.0, ALU.subtract, ALU.max))
                    link(v.tensor_copy(tile_at_i[:, :], tile_at[:, :]))
                    v.sem_inc(tile_known, 1)
                    link(v.tensor_scalar(cw_c[:, :], wt_c[:, :], CUTOFF, 0.5, ALU.is_lt, ALU.mult))
                    link(v.tensor_scalar(wt_c[:, :], wt_c[:, :], CUTOFF, None, ALU.min))
                    v.sem_inc(angle, 1)
                    v.wait_ge(windows_mm, 1)
                    v.tensor_scalar(window_col[:, :], ps_l[:, 128:128 + NB], part_idx[:, :], None, ALU.add)
                    link(v.tensor_tensor(window_f[:, 1, :], window_f[:, 1, :], window_f[:, 0, :], ALU.subtract))
                    link(v.tensor_reduce(window_f[:, 0, 0:1], window_f[:, 1, :], AX.X, ALU.max))
                    link(v.tensor_scalar(flags[0:1, 2:3], window_f[:, 0, 0:1], float(P), None, ALU.is_ge))
                    for c in range(16):
                        v.wait_ge(row_mm, c + 1)
                        for n, t in enumerate(row_out):
                            v.tensor_copy(t[:, c, :], ps_row[0:100, c % 2, n, 0:TE]).then_inc(row_copied, 1)
                    v.wait_ge(sined, 1)
                    link(v.scalar_tensor_tensor(cw_c[:, :], near[:, :], 1.0, cw_c[:, :], ALU.add, ALU.mult))
                    v.wait_ge(loaded_nodes, 16 * 3)
                    v.tensor_copy(ntype_bf[:, :], ntype[0:TE, :])
                    layer_norm(v, xn[:, :, :], hn[:, :, :], sq[:, :, 0:H])
                    link(v.tensor_scalar(hn[:, :, :], hn[:, :, :], 0.0, None, ALU.max))
                    v.tensor_copy(rows[:, :, H:H + 1], mult[:, :].unsqueeze(2))
                    link(v.tensor_tensor(rows[:, :, 0:H], hn[:, :, :], mult[:, :].unsqueeze(2).to_broadcast([TE, LO, H]),
                                         ALU.mult))
                    v.wait_ge(tile_found, 16 * (QG + 1))
                    for c in range(QG + 1):
                        link(v.tensor_scalar(below[:, 0:TE], found[:, c, :], group_node[:, c:c + 1], 0.0, ALU.is_lt,
                                             ALU.add, accum_out=edges_below[:, c:c + 1]))
                    link(v.scalar_tensor_tensor(first_at[:, :], tile_at[:, :], float(TE), edges_below[:, :], ALU.mult,
                                                ALU.add))
                    link(v.tensor_copy(first_at_i[:, :], first_at[:, :]))
                    v.sem_inc(first_known, 1)
                    link(v.tensor_tensor(below[:, 0:QG], first_at[:, 1:QG + 1], first_at[:, 0:QG], ALU.subtract))
                    link(v.tensor_reduce(tiles_below[:, 0:1], below[:, 0:QG], AX.X, ALU.max))
                    link(v.tensor_scalar(flags[:, 1:2], tiles_below[:, 0:1], float(GT * P), None, ALU.is_gt))
                    v.sem_inc(flags_ready, 1)
                    v.wait_ge(flag_mm, 1)
                    link(v.tensor_reduce(flag_f[:, 0:1], ps_l[0:1, 256:259], AX.X, ALU.add))
                    link(v.tensor_copy(flag_i[:, 0:1], flag_f[:, 0:1]))
                    v.wait_ge(logit_rows, 16 * LO)
                    for j in (0, LO // 2):
                        some = slice(j, j + LO // 2)
                        split(rows[:, some, :], sq[:, some, :], [image[:, some, k, 0:H + 1] for k in range(3)])
                        v.sem_inc(rows_ready, 1)

        def cols(a, h, parts=TE):
            return a[0:parts, bass.ds(h * HT, HT)]

        def bc(a):
            return a.unsqueeze(2).to_broadcast([TE, LO, H])

        def branches(flag_at, usual, other):
            with nc.Block() as block:
                for name, part in (("sync", block.sync), ("gpsimd", block.gpsimd), ("tensor", block.tensor),
                                   ("scalar", block.scalar), ("vector", block.vector)):
                    def program(eng, name=name):
                        flag = eng.value_load(flag_at, min_val=0, max_val=4 * P)
                        before = steps[0]
                        with eng.If(flag == 0):
                            usual[name](eng)
                        steps[0] = before
                        with eng.Else():
                            other[name](eng)
                    part(program)

        sp_passed, pe_passed = sem("sp_passed"), sem("pe_passed")
        env = locals()
        branches(flag_i[0:1, 0:1], layer1_windows(nc, env), layer1_edges(nc, env))

        with ExitStack() as nodes:
            tabs = nodes.enter_context(nc.sbuf_tensor("tabs", [TE, 4, LO * (H + 1)], F32))
            summed = nodes.enter_context(nc.sbuf_tensor("summed", [TE, LO * (H + 1)], F32))
            agg = nodes.enter_context(nc.sbuf_tensor("agg", [TE, LO, H + 1], F32))
            work = nodes.enter_context(nc.sbuf_tensor("work", [TE, LO, H], F32))
            sq1 = nodes.enter_context(nc.sbuf_tensor("sq1", [TE, LO, H], F32))
            last_row = nodes.enter_context(nc.sbuf_tensor("last_row", [TE, LO, LO], F8))
            last_row_f = nodes.enter_context(nc.sbuf_tensor("last_row_f", [TE, LO, LO], F32))
            biggest = nodes.enter_context(nc.sbuf_tensor("biggest", [TE, 1], F32))
            ps_flag = nodes.enter_context(nc.psum_tensor("ps_flag", [P, 512], F32))
            tabs_in = [sem(f"tabs_in{i}") for i in range(4)]
            tab_read, row_in, turned, flags_ready, flag_mm = (sem("tab_read"), sem("row_in"), sem("turned"),
                                                              sem("flags_ready2"), sem("flag_mm2"))
            with nc.Block() as block:

                @block.sync
                def _(sp):
                    for i in range(NTAB):
                        if i >= 4:
                            sp.wait_ge(tab_read, i - 3)
                        sp.dma_start(tabs[:, i % 4, :], msg_acc[i][0:N, :].rearrange("(p j) f -> p (j f)", j=LO)
                                     ).then_inc(tabs_in[i % 4], 16)
                    sp.dma_start(last_row[:, :, :].rearrange("p q j -> p (q j)").bitcast(I16)
                                 .rearrange("p (q j) -> p q j", q=LO),
                                 counts[TE, 0:N * LO // 2].rearrange("(q m j) -> m q j", m=TE, j=LO // 2)
                                 ).then_inc(row_in, 16)
                    sp.wait_ge(tab_read, NTAB)
                    sp.dma_start(sum_tab.rearrange("(p j) f -> p (j f)", j=LO), summed[:, :]).then_inc(turned, 16)
                    sp.wait_ge(turned, 16)
                    sp.dma_start(agg[:, :, :], sum_tab.rearrange("(j p) f -> p j f", p=TE)).then_inc(turned, 16)

                @block.scalar
                def _(a):
                    root(a, 2)
                    root(a, 3)
                    root(a, 4)

                @block.tensor
                def _(t):
                    t.wait_ge(flags_ready, 1)
                    t.matmul(ps_flag[0:1, 0:4], ones_col[:, :], flags[:, :], start=True, stop=True).then_inc(flag_mm, 1)

                @block.vector
                def _(v):
                    for i in range(NTAB):
                        v.wait_ge(tabs_in[i % 4], 16 * (i // 4 + 1))
                        if i >= 1:
                            v.wait_ge(tab_read, i)
                            m = v.tensor_tensor(summed[:, :], summed[:, :], tabs[:, i % 4, :], ALU.add)
                        else:
                            m = v.tensor_copy(summed[:, :], tabs[:, 0, :])
                        m.then_inc(tab_read, 1)
                    v.wait_ge(row_in, 16)
                    link(v.tensor_copy(last_row_f[:, :, :], last_row[:, :, :]))
                    link(v.tensor_reduce(indeg[:, :], last_row_f[:, :, :], AX.X, ALU.add))
                    link(v.tensor_reduce(biggest[:, :], last_row_f[:, :, :], AX.XY, ALU.max))
                    link(v.tensor_scalar(flags[0:TE, 3:4], biggest[:, :], float(FINE), None, ALU.is_ge))
                    v.sem_inc(flags_ready, 1)
                    v.wait_ge(flag_mm, 1)
                    link(v.tensor_reduce(flag_f[:, 1:2], ps_flag[0:1, 0:4], AX.X, ALU.add))
                    link(v.tensor_copy(flag_i[:, 1:2], flag_f[:, 1:2]))
                    link(v.tensor_scalar(stat[:, 0, :], indeg[:, :], 1.0, None, ALU.add))
                    v.sem_inc(root_asked, 1)
                    roots[0] += 1
                    v.wait_ge(root_done, roots[0])
                    link(v.reciprocal(dinv[:, :], stat[:, 1, :]))
                    v.wait_ge(turned, 32)
                    link(v.tensor_scalar(stat[:, 0, :].unsqueeze(2), agg[:, :, H:H + 1], 1e-8, None, ALU.max))
                    link(v.reciprocal(stat[:, 1, :], stat[:, 0, :]))
                    link(v.tensor_tensor(work[:, :, :], agg[:, :, 0:H], bc(stat[:, 1, :]), ALU.mult))
                    link(v.tensor_tensor(hn[:, :, :], hn[:, :, :], work[:, :, :], ALU.add))
                    layer_norm(v, hn[:, :, :], work[:, :, :], sq1[:, :, :])
                    link(v.tensor_tensor(work[:, :, :], work[:, :, :], gamma_b[0:TE, :].unsqueeze(1)
                                         .to_broadcast([TE, LO, H]), ALU.mult))
                    link(v.tensor_tensor(work[:, :, :], work[:, :, :], beta_b[0:TE, :].unsqueeze(1)
                                         .to_broadcast([TE, LO, H]), ALU.add))
                    link(v.tensor_tensor(xn[:, :, :], xn[:, :, :], work[:, :, :], ALU.add))
                    layer_norm(v, xn[:, :, :], hn[:, :, :], sq1[:, :, :])
                    link(v.tensor_scalar(hn[:, :, :], hn[:, :, :], 0.0, None, ALU.max))

        env = locals()
        branches(flag_i[0:1, 1:2], propagate_counts(nc, env), propagate_edges(nc, env))


def layer1_windows(nc, env):
    sem, link, cols = env["sem"], env["link"], env["cols"]
    (src_c, lo_c, cw_c, trash, tri, part_idx, free_idx, ident, zeros) = (
        env[k] for k in ("src_c", "lo_c", "cw_c", "trash", "tri", "part_idx", "free_idx", "ident", "zeros"))
    (w1_pair, w2_pair, b1_pair, ntype_bf, first_row, window_row, window_col) = (
        env[k] for k in ("w1_pair", "w2_pair", "b1_pair", "ntype_bf", "first_row", "window_row", "window_col"))
    (edge_attr, src_rows, hi_rows, dst_rows, node_parts, msg_acc, code_pairs, counts) = (
        env[k] for k in ("edge_attr", "src_rows", "hi_rows", "dst_rows", "node_parts", "msg_acc", "code_pairs", "counts"))
    mine = ExitStack()

    def sb(name, shape, dt=F32):
        return mine.enter_context(nc.sbuf_tensor(name, shape, dt))

    def psum(name, shape):
        return mine.enter_context(nc.psum_tensor(name, shape, F32))

    attr = sb("attr", [TE, 2, HT, R])
    src_keys = sb("src_keys", [TE, 2, HE], I16)
    hi_keys = sb("hi_keys", [TE, 2, HE], BF16)
    dst_keys = sb("dst_keys", [P, 2, HE], I16)
    hi_t = sb("hi_t", [TE, 2, HE], BF16)
    dst_t = sb("dst_t", [P, 2, HE], BF16)
    window = sb("window", [P, 2, 3, GW], BF16)
    attr_t = sb("attr_t", [2 * R, HT // 2 * TE])
    hid = sb("hid", [2 * H + 1, 2, HT // 2 * TE])
    same = sb("same", [TE, 2, HT, TE])
    junk_lo, junk_z = sb("junk_lo", [TE, HT, LO], BF16), sb("junk_z", [TE, HT, NEL], BF16)
    count, firsts = sb("count", [TE, 2, HT]), sb("firsts", [TE, 2, HT])
    target = sb("target", [P, 2, HT], I32)
    ztype, adapt, adapt_cw = sb("ztype", [TE, 2, HT]), sb("adapt", [TE, 2, HT]), sb("adapt_cw", [TE, 2, HT])
    gate = sb("gate", [TE, 2, HT, H])
    msg = sb("msg", [TE, 2, HT, H + 1])
    sums = sb("sums", [P, 2, HT, H + 1])
    src_less = sb("src_less", [TE, T])
    pair_in = sb("pair_in", [P, 2, HG, GT, 2])
    group_code = sb("group_code", [P, NG])
    code_in = sb("code_in", [P, 2, HG, GT])
    hi_in = sb("hi_in", [P, 2, HG, GT], BF16)
    hi_iota = sb("hi_iota", [P, TE, HG * GT], BF16)
    code_iota = sb("code_iota", [P, GN * LO], F16)
    hi_hot = sb("hi_hot", [P, 2, TE + 1, HG * GT], BF16)
    code_hot = sb("code_hot", [P, 2, HG * GT, GN * LO], BF16)
    off_code = sb("off_code", [P, GT, GN * LO], BF16)
    ones = env["ones_col"]
    slab = sb("slab", [TE + 1, 2, HG, GN * LO], F8)
    ps_mlp, ps_count, ps_gate, ps_z, ps_sum = (psum(n, [P, 512]) for n in
                                              ("ps_mlp", "ps_count", "ps_gate", "ps_z", "ps_sum"))
    ps_row = psum("ps_rows", [P, 3, 512])
    RB = 3
    assert HG == 4

    def ps_bank(k):
        return ps_mlp if k == 2 else ps_count

    loads = [sem("w_loads_even"), sem("w_loads_odd")]
    pairs_in = [sem("w_pairs_in_even"), sem("w_pairs_in_odd")]
    (attr_read, attr_sb, hid_mm, hid_sb, hi_ready, dst_ready, z_mm, z_read, rows_mm, adapt_ready, gate_mm, gate_sb,
     same_ready, msg_ready, sum_mm, sum_sb, target_ready, code_ready, hot_ready, count_mm, slab_sb, iotas,
     passed, dve_half, pool_half, off_ready, last_hot) = (sem("w_" + n) for n in (
         "attr_read", "attr_sb", "hid_mm", "hid_sb", "hi_ready", "dst_ready", "z_mm", "z_read", "rows_mm", "adapt_ready",
         "gate_mm", "gate_sb", "same_ready", "msg_ready", "sum_mm", "sum_sb", "target_ready", "code_ready", "hot_ready",
         "count_mm", "slab_sb", "iotas", "passed", "dve_half", "pool_half", "off_ready", "last_hot"))
    added = [sem("w_added_low"), sem("w_added_high")]
    slab_out = [sem("w_slab_out_even"), sem("w_slab_out_odd")]
    NH = 2 * NB
    ADDS = 16 * HT // 2
    LOADS = 16 * 5

    def sync(sp):
        def load(b, par, first):
            h = 2 * b + par
            if not first:
                for used in (attr_read, rows_mm, hi_ready, dst_ready, same_ready):
                    sp.wait_ge(used, h - 1)
                sp.sem_inc(passed, 1)
            sp.dma_start(attr[:, par, :, :],
                         edge_attr[bass.ds(b * 2 * HE, 2 * HE), :].rearrange("(p i) r -> p i r", i=BT)
                         [:, HT * par:HT * par + HT, :]).then_inc(loads[par], 16)
            for keys, rows_dram, parts in ((src_keys, src_rows, TE), (hi_keys, hi_rows, TE), (dst_keys, dst_rows, P)):
                sp.dma_start(keys[:, par, :], rows_dram[bass.ds(h * HT, HT), :].rearrange("t e -> (t e)")
                             .partition_broadcast(parts)).then_inc(loads[par], 16)
            at = sp.value_load(window_row[0:1, bass.ds(b, 1)], min_val=0, max_val=N - 1)
            sp.dma_start(window[:, par, :, :].rearrange("p k f -> p (k f)"), node_parts[bass.ds(at, P), :]
                         ).then_inc(loads[par], 16)
            if not first:
                sp.wait_ge(code_ready, h - 1)
                sp.sem_inc(passed, 1)
            for k in range(HG):
                at = sp.value_load(first_row[0:1, bass.ds(h * HG + k, 1)], min_val=0, max_val=E)
                sp.dma_start(pair_in[:, par, k, :, :].rearrange("p i c -> p (i c)"),
                             code_pairs[bass.ds(at, GT * P), :].rearrange("(p i) c -> p (i c)", p=P)
                             ).then_inc(pairs_in[par], 16)
        load(0, 0, True)
        load(0, 1, True)
        with sp.Fori(1, NB) as b:
            load(b, 0, False)
            load(b, 1, False)

    def gpsimd(p):
        def codes(b, par, first):
            h = 2 * b + par
            p.wait_ge(pairs_in[par], 16 * HG * b + 16 * HG)
            if not first:
                p.wait_ge(hot_ready, h - 1)
                p.wait_ge(last_hot, h - 1)
            p.sem_inc(passed, 1)
            p.tensor_tensor(code_in[:, par, :, :], pair_in[:, par, :, :, 0],
                            group_code[:, bass.ds(h * HG, HG)].unsqueeze(2).to_broadcast([P, HG, GT]), ALU.subtract)
            p.tensor_copy(hi_in[:, par, :, :], pair_in[:, par, :, :, 1]).then_inc(code_ready, 1)

        def scatter(h, par, first=False, fresh=False):
            p.wait_ge(same_ready, h + 1)
            if not fresh:
                for g in range(2):
                    p.wait_ge(added[g], (h - 1) * ADDS)
            p.sem_inc(passed, 1)
            p.tensor_scalar(firsts[:, par, :], count[:, par, :], 1.0, None, ALU.is_equal).then_inc(pool_half, 1)
            p.wait_ge(pool_half, 2 * h + 1)
            p.sem_inc(passed, 1)
            p.tensor_tensor(firsts[:, par, :], firsts[:, par, :], cols(src_less, h), ALU.mult).then_inc(pool_half, 1)
            p.wait_ge(pool_half, 2 * h + 2)
            p.sem_inc(passed, 1)
            p.tensor_scalar(target[0:TE, par, :], firsts[:, par, :], trash[0:TE, :], None, ALU.add
                            ).then_inc(target_ready, 1)
            p.wait_ge(sum_sb, h + 2)
            p.wait_ge(target_ready, h + 1)
            for g in range(2):
                if not first:
                    p.wait_ge(added[g], h * ADDS)
                p.sem_inc(passed, 1)
                for i in range(HT // 2 * g, HT // 2 * (g + 1)):
                    p.indirect_dma_start(msg_acc[i], bass.IndirectOffsetOnAxis(ap=target[:, par, i:i + 1], axis=0),
                                         sums[:, par, i, :], None, compute_op=ALU.add).then_inc(added[g], 16)
        p.iota(group_code[:, :], [[GN * LO, NG]], 0, 0, allow_small_or_imprecise_dtypes=True)
        p.iota(code_iota[:, :], [[1, GN * LO]], 0, 0, allow_small_or_imprecise_dtypes=True)
        p.iota(hi_iota[:, :, :], [[1, TE], [0, HG * GT]], 0, 0, allow_small_or_imprecise_dtypes=True
               ).then_inc(iotas, 1)
        p.wait_ge(iotas, 1)
        codes(0, 0, True)
        codes(0, 1, True)
        scatter(0, 0, True, True)
        codes(1, 0, False)
        scatter(1, 1, fresh=True)
        with p.Fori(1, NB - 1) as b:
            codes(b, 1, False)
            scatter(2 * b, 0)
            codes(b + 1, 0, False)
            scatter(2 * b + 1, 1)
        codes(NB - 1, 1, False)
        scatter(NH - 2, 0)
        scatter(NH - 1, 1)
        for g in range(2):
            p.wait_ge(added[g], NH * ADDS)

    def tensor(t):
        def transpose_attr(b, par, fresh=False):
            t.wait_ge(loads[par], LOADS * b + LOADS)
            if not fresh:
                t.wait_ge(slab_sb, (2 * b + par - 2) * HG - 1)
            for k in range(HT // 2):
                m = t.transpose(ps_mlp[0:2 * R, TE * k:TE * k + TE],
                                attr[:, par, 2 * k:2 * k + 2, :].rearrange("p a r -> p (a r)"), ident[0:TE, 0:TE])
            m.then_inc(attr_read, 1)

        def hidden(b, par):
            t.wait_ge(attr_sb, 2 * b + par + 1)
            t.matmul(ps_mlp[0:2 * H, 0:HE // 2], w1_pair[:, :], attr_t[:, :], start=True, stop=True).then_inc(hid_mm, 1)

        def types(b, par, fresh=False):
            t.wait_ge(hi_ready, 2 * b + par + 1)
            if not fresh:
                t.wait_ge(z_read, 2 * b + par)
            for i in range(HT):
                m = t.matmul(ps_z[0:TE, LO * i:LO * i + LO], hi_t[:, par, TE * i:TE * i + TE], ntype_bf[:, :],
                             start=True, stop=True)
            m.then_inc(z_mm, 1)

        def gates(b, par, fresh=False):
            t.wait_ge(hid_sb, 2 * b + par + 1)
            if not fresh:
                t.wait_ge(gate_sb, 2 * b + par)
            for k in range(HT // 2):
                m = t.matmul(ps_gate[0:TE, 2 * H * k:2 * H * k + 2 * H], hid[:, par, TE * k:TE * k + TE],
                             w2_pair[:, :], start=True, stop=True)
            m.then_inc(gate_mm, 1)

        def rows(b, par, fresh=False):
            t.wait_ge(dst_ready, 2 * b + par + 1)
            if not fresh:
                t.wait_ge(msg_ready, 2 * b + par)
            for i in range(HT):
                for k in range(3):
                    m = t.matmul(ps_row[0:TE, i // RB, GW * (i % RB):GW * (i % RB + 1)], dst_t[:, par, TE * i:TE * i + TE],
                                 window[:, par, k, :], start=(k == 0), stop=(k == 2))
            m.then_inc(rows_mm, 1)

        def combine(b, par):
            h = 2 * b + par
            t.wait_ge(same_ready, h + 1)
            t.wait_ge(msg_ready, h + 1)
            t.wait_ge(sum_sb, h + 1)
            for i in range(HT):
                m = t.matmul(ps_sum[0:TE, (H + 1) * i:(H + 1) * (i + 1)], same[:, par, i, :], msg[:, par, i, :],
                             start=True, stop=True)
            m.then_inc(sum_mm, 1)

        def count_group(b, par, k, soon, fresh=False):
            h = 2 * b + par
            t.wait_ge(last_hot if k == HG - 1 else hot_ready, h + 1)
            if k == 2 and soon:
                t.wait_ge(hid_sb, h + 3)
            elif k != 2 and not fresh:
                t.wait_ge(slab_sb, h * HG + (0, 1, None, 2)[k])
            for i in range(GT * k, GT * k + GT):
                m = t.matmul(ps_bank(k)[0:TE + 1, 0:GN * LO], hi_hot[:, par, :, i], code_hot[:, par, i, :],
                             start=(i % GT == 0), stop=(i % GT == GT - 1))
            m.then_inc(count_mm, 1)

        def half(b, par, fresh=False):
            soon = b + 1 < NB if isinstance(b, int) else True
            if soon or par == 0:
                rows(b + par, 1 - par)
            combine(b, par)
            if soon or par == 0:
                gates(b + par, 1 - par)
            if soon:
                transpose_attr(b + 1, par, fresh)
            count_group(b, par, 0, soon, fresh)
            if soon:
                hidden(b + 1, par)
            count_group(b, par, 1, soon)
            count_group(b, par, 2, soon)
            if soon:
                types(b + 1, par)
            count_group(b, par, 3, soon)
        t.sem_inc(sum_sb, 1)
        transpose_attr(0, 0, True)
        hidden(0, 0)
        types(0, 0, True)
        rows(0, 0, True)
        gates(0, 0, True)
        transpose_attr(0, 1, True)
        hidden(0, 1)
        types(0, 1)
        half(0, 0, True)
        half(0, 1)
        with t.Fori(1, NB - 1) as b:
            half(b, 0)
            half(b, 1)
        half(NB - 1, 0)
        half(NB - 1, 1)

    def scalar(a):
        def columns(b, par, fresh=False):
            a.wait_ge(attr_read, 2 * b + par + 1)
            if not fresh:
                a.wait_ge(hid_mm, 2 * b + par)
            a.activation(attr_t[:, :], ps_mlp[0:2 * R, 0:HE // 2], ACT.Copy).then_inc(attr_sb, 1)

        def hidden(b, par, fresh=False):
            a.wait_ge(hid_mm, 2 * b + par + 1)
            if not fresh:
                a.wait_ge(gate_mm, 2 * b + par - 1)
            a.activation(hid[0:2 * H, par, :], ps_mlp[0:2 * H, 0:HE // 2], ACT.Silu, bias=b1_pair[:, :]
                         ).then_inc(hid_sb, 1)

        def gates(b, par, i_from, i_to):
            h = 2 * b + par
            if i_from == 0:
                a.wait_ge(adapt_ready, h + 1)
                a.wait_ge(gate_mm, h + 1)
                for r in range(0, HT, RB):
                    n_r = min(RB, HT - r)
                    a.activation(msg[:, par, r:r + n_r, H:H + 1], ps_row[0:TE, r // RB, 0:GW * n_r]
                                 .rearrange("p (i f) -> p i f", f=GW)[:, :, H:H + 1], ACT.Copy)
            for i in range(i_from, i_to):
                m = a.activation(gate[:, par, i, :], ps_gate[0:TE, H * i:H * i + H], ACT.Identity,
                                 bias=adapt_cw[:, par, i:i + 1], scale=cw_c[:, bass.ds(h * HT + i, 1)])
            if i_to == HT:
                m.then_inc(gate_sb, 1)

        def combined(b, par):
            a.wait_ge(sum_mm, 2 * b + par + 1)
            a.wait_ge(target_ready, 2 * b + par + 1)
            a.activation(sums[0:TE, par, :, :], ps_sum[0:TE, 0:HT * (H + 1)]
                         .rearrange("p (i f) -> p i f", f=H + 1), ACT.Copy).then_inc(sum_sb, 1)

        def counted(b, par, k):
            a.wait_ge(count_mm, (2 * b + par) * HG + k + 1)
            a.sem_inc(passed, 1)
            a.activation(slab[:, par, k, :], ps_bank(k)[0:TE + 1, 0:GN * LO], ACT.Copy, saturate=False
                         ).then_inc(slab_sb, 1)

        def last_codes(b, par, fresh=False):
            h = 2 * b + par
            a.wait_ge(code_ready, h + 1)
            if not fresh:
                a.wait_ge(last_hot, h)
            a.sem_inc(passed, 1)
            for i in range(GT):
                m = a.activation(off_code[:, i, :], code_iota[:, :], ACT.Square, bias=code_in[:, par, HG - 1, i:i + 1],
                                 scale=-1.0)
            m.then_inc(off_ready, 1)
            a.wait_ge(off_ready, h + 1)
            a.sem_inc(passed, 1)
            for i in range(GT):
                m = a.activation(code_hot[:, par, (HG - 1) * GT + i, :], off_code[:, i, :], ACT.Relu, bias=ones[:, :],
                                 scale=-1.0)
            m.then_inc(last_hot, 1)

        def half(b, par, fresh=False):
            soon = b + 1 < NB if isinstance(b, int) else True
            if not fresh:
                a.wait_ge(slab_out[par], 16 * b + 16 * par)
            combined(b, par)
            if soon:
                columns(b + 1, par)
            counted(b, par, 0)
            if soon or par == 0:
                gates(b + par, 1 - par, 0, 3)
            if soon:
                hidden(b + 1, par)
            if soon or par == 0:
                gates(b + par, 1 - par, 3, HT)
            for k in range(1, HG):
                counted(b, par, k)
            if soon or par == 0:
                last_codes(b + par, 1 - par)
            h = 2 * b + par
            a.wait_ge(slab_sb, h * HG + HG)
            a.sem_inc(passed, 1)
            a.dma_start(counts[:, bass.ds(h * (HG * GN * LO // 2), HG * GN * LO // 2)],
                        slab[:, par, :, :].rearrange("p k c -> p (k c)").bitcast(I16)).then_inc(slab_out[par], 16)
        a.sem_inc(slab_out[1], 16)
        last_codes(0, 0, True)
        columns(0, 0, True)
        hidden(0, 0, True)
        columns(0, 1)
        hidden(0, 1, True)
        gates(0, 0, 0, HT)
        half(0, 0, True)
        half(0, 1)
        with a.Fori(1, NB - 1) as b:
            half(b, 0)
            half(b, 1)
        half(NB - 1, 0)
        half(NB - 1, 1)
        a.wait_ge(slab_out[0], 16 * NB)
        a.wait_ge(slab_out[1], 16 * NB + 16)

    def vector(v):
        v.memset(hid[2 * H:2 * H + 1, :, :], 1.0)
        v.memset(hi_hot[:, :, TE, :], 1.0)
        v.memset(sums[:, :, :, :], 0.0)
        link(v.tensor_scalar(target[:, :, :].rearrange("p a i -> p (a i)"), zeros[:, 0:2 * HT], trash[:, :], None,
                             ALU.add))
        link(v.tensor_scalar(src_less[:, :], src_c[:, :], trash[0:TE, :], None, ALU.subtract))

        def edge_columns(b, par):
            v.wait_ge(loads[par], LOADS * b + LOADS)
            v.tensor_scalar(hi_t[:, par, :], hi_keys[:, par, :], part_idx[0:TE, :], None, ALU.is_equal
                            ).then_inc(hi_ready, 1)
            v.tensor_scalar(dst_t[:, par, :], dst_keys[:, par, :], window_col[:, bass.ds(b, 1)], None, ALU.is_equal
                            ).then_inc(dst_ready, 1)

        def half(b, par, first):
            h = 2 * b + par
            if not first:
                v.wait_ge(sum_mm, h - 1)
                v.wait_ge(target_ready, h - 1)
            for i in range(HT):
                m = v.scalar_tensor_tensor(same[:, par, i, :], src_keys[:, par, TE * i:TE * i + TE],
                                           src_c[:, bass.ds(h * HT + i, 1)], tri[0:TE, :], ALU.is_equal,
                                           ALU.mult, accum_out=count[:, par, i:i + 1])
            m.then_inc(same_ready, 1)
            v.wait_ge(z_mm, h + 1)
            for i in range(HT):
                m = v.scalar_tensor_tensor(junk_lo[:, i, :], free_idx[0:TE, 0:LO], lo_c[:, bass.ds(h * HT + i, 1)],
                                           ps_z[0:TE, LO * i:LO * i + LO], ALU.is_equal, ALU.mult,
                                           accum_out=ztype[:, par, i:i + 1])
            m.then_inc(z_read, 1)
            v.wait_ge(code_ready, h + 1)
            if not first:
                v.wait_ge(count_mm, (h - 1) * HG)

            def code_rows(i):
                return v.tensor_scalar(code_hot[:, par, i, :], code_iota[:, :],
                                       code_in[:, par, i // GT, i % GT:i % GT + 1], None, ALU.is_equal)
            code_rows(0)
            v.wait_ge(z_read, h + 1)
            v.wait_ge(rows_mm, h + 1)
            for i in range(HT):
                m = v.scalar_tensor_tensor(junk_z[:, i, :], free_idx[0:TE, 0:NEL], ztype[:, par, i:i + 1],
                                           ps_row[0:TE, i // RB, GW * (i % RB) + H + 1:GW * (i % RB + 1)],
                                           ALU.is_equal, ALU.mult, accum_out=adapt[:, par, i:i + 1])
            m.then_inc(dve_half, 1)
            code_rows(1)
            v.wait_ge(dve_half, h + 1)
            v.tensor_tensor(adapt_cw[:, par, :], adapt[:, par, :], cols(cw_c, h), ALU.mult).then_inc(adapt_ready, 1)
            if par == 0 or not isinstance(b, int) or b + 1 < NB:
                edge_columns(b + par, 1 - par)
            v.tensor_tensor(hi_hot[:, par, 0:TE, :], hi_iota[:, :, :],
                            hi_in[:, par, :, :].rearrange("p k i -> p (k i)").unsqueeze(1)
                            .to_broadcast([P, TE, HG * GT]), ALU.is_equal)
            for i in range(2, (HG - 1) * GT):
                m = code_rows(i)
            m.then_inc(hot_ready, 1)
            v.wait_ge(gate_sb, h + 1)
            for r in range(0, HT, RB):
                n_r = min(RB, HT - r)
                rows_r = ps_row[0:TE, r // RB, 0:GW * n_r].rearrange("p (i f) -> p i f", f=GW)
                m = v.tensor_tensor(msg[:, par, r:r + n_r, 0:H], gate[:, par, r:r + n_r, :], rows_r[:, :, 0:H], ALU.mult)
            m.then_inc(msg_ready, 1)
        edge_columns(0, 0)
        half(0, 0, True)
        half(0, 1, True)
        with v.Fori(1, NB - 1) as b:
            half(b, 0, False)
            half(b, 1, False)
        half(NB - 1, 0, False)
        half(NB - 1, 1, False)
    mine.close()
    return {"sync": sync, "gpsimd": gpsimd, "tensor": tensor, "scalar": scalar, "vector": vector}


def layer1_edges(nc, env):
    sem, link, cols, sp_passed = (env[k] for k in ("sem", "link", "cols", "sp_passed"))
    (src_c, lo_c, cw_c, dst_i, trash, tri, part_idx, free_idx, ident, zeros) = (
        env[k] for k in ("src_c", "lo_c", "cw_c", "dst_i", "trash", "tri", "part_idx", "free_idx", "ident", "zeros"))
    (w1_pair, w2_pair, b1_pair, ntype_bf, edge_attr, src_rows, hi_rows, node_parts, msg_acc, counts) = (
        env[k] for k in ("w1_pair", "w2_pair", "b1_pair", "ntype_bf", "edge_attr", "src_rows", "hi_rows", "node_parts",
                         "msg_acc", "counts"))
    mine = ExitStack()

    def sb(name, shape, dt=F32):
        return mine.enter_context(nc.sbuf_tensor(name, shape, dt))

    attr = sb("g_attr", [TE, 2, HT, R])
    key_rows = sb("g_key_rows", [TE, 2, HE], I16)
    hib = sb("g_hib", [TE, 2, HE], BF16)
    hi_t = sb("g_hi_t", [TE, 2, HE], BF16)
    attr_t = sb("g_attr_t", [2 * R, HT // 2 * TE])
    hid = sb("g_hid", [2 * H + 1, 2, HT // 2 * TE])
    gat_parts = sb("g_gat_parts", [P, 2, HT, 3, GW], BF16)
    gat = sb("g_gat", [TE, 2, HT, GW])
    gat_idx = sb("g_gat_idx", [P, 2, HT], I32)
    same = sb("g_same", [TE, 2, HT, TE])
    junk_lo = sb("g_junk_lo", [TE, HT, LO], BF16)
    junk_z = sb("g_junk_z", [TE, HT, NEL], BF16)
    count = sb("g_count", [TE, 2, HT])
    sel = sb("g_sel", [TE, 2, HT])
    firsts = sb("g_firsts", [TE, 2, HT])
    target = sb("g_target", [P, 2, HT], I32)
    ztype = sb("g_ztype", [TE, 2, HT])
    adapt = sb("g_adapt", [TE, 2, HT])
    raw = sb("g_raw", [TE, HT, H])
    msg = sb("g_msg", [TE, 2, HT, H + 1])
    sums = sb("g_sums", [P, 2, HT, H + 1])
    src_less = sb("g_src_less", [TE, T])

    ps_attr = mine.enter_context(nc.psum_tensor("g_ps_attr", [P, 512], F32))
    ps_hid = mine.enter_context(nc.psum_tensor("g_ps_hid", [P, 512], F32))
    ps_gate = mine.enter_context(nc.psum_tensor("g_ps_gate", [P, 2, 512], F32))
    ps_z = mine.enter_context(nc.psum_tensor("g_ps_z", [P, 2, 512], F32))
    ps_sum = mine.enter_context(nc.psum_tensor("g_ps_sum", [P, 2, 512], F32))

    loads = [sem("g_loads_even"), sem("g_loads_odd")]
    attr_read, attr_sb, hid_mm, hid_sb = sem("g_attr_read"), sem("g_attr_sb"), sem("g_hid_mm"), sem("g_hid_sb")
    hi_onehot, z_mm, z_read, gate_mm, gate_read = (sem("g_hi_onehot"), sem("g_z_mm"), sem("g_z_read"), sem("g_gate_mm"),
                                                   sem("g_gate_read"))
    same_ready, msg_ready, sum_mm, sum_sb = sem("g_same_ready"), sem("g_msg_ready"), sem("g_sum_mm"), sem("g_sum_sb")
    gathered = [sem("g_gathered_even"), sem("g_gathered_odd")]
    idx_copied, target_ready = sem("g_idx_copied"), sem("g_target_ready")
    added = [sem("g_added_low"), sem("g_added_high")]
    pool_passed, cleared = sem("g_pool_passed"), sem("g_cleared")
    dve_half = sem("g_dve_half")
    NH = 2 * NB
    ADDS = 16 * HT // 2
    LINKS = 5

    def sync(sp):
        def load(h, par, first):
            if not first:
                sp.wait_ge(attr_read, h - 1)
                sp.wait_ge(same_ready, h - 1)
                sp.wait_ge(hi_onehot, h - 1)
                sp.sem_inc(sp_passed, 1)
            sp.dma_start(attr[:, par, :, :],
                         edge_attr[bass.ds((h - par) * HE, 2 * HE), :].rearrange("(p i) r -> p i r", i=BT)
                         [:, HT * par:HT * par + HT, :]).then_inc(loads[par], 16)
            for rows_sb, rows_dram in ((key_rows, src_rows), (hib, hi_rows)):
                sp.dma_start(rows_sb[:, par, :], rows_dram[bass.ds(h * HT, HT), :].rearrange("t e -> (t e)")
                             .partition_broadcast(TE)).then_inc(loads[par], 16)
        sp.dma_start(counts[TE, 0:P * (N * LO // P // 2)].rearrange("(p c) -> p c", p=P),
                     zeros[:, 0:N * LO // P // 4 + 1].bitcast(I16)[:, 0:N * LO // P // 2]).then_inc(cleared, 16)
        left = P * (N * LO // P // 2)
        sp.dma_start(counts[TE, left:N * LO // 2].unsqueeze(0), zeros[0:1, 0:P].bitcast(I16)[:, 0:N * LO // 2 - left]
                     ).then_inc(cleared, 16)
        load(0, 0, True)
        load(1, 1, True)
        with sp.Fori(1, NB) as b:
            load(2 * b, 0, False)
            load(2 * b + 1, 1, False)

        sp.wait_ge(cleared, 16 * 2)

    def gpsimd(p):
        def gather(h, par, first):
            if not first:
                p.wait_ge(msg_ready, h - 1)
            p.sem_inc(pool_passed, 1)
            p.tensor_copy(gat_idx[:, par, :], cols(dst_i, h, P)).then_inc(idx_copied, 1)
            p.wait_ge(idx_copied, h + 1)
            p.sem_inc(pool_passed, 1)
            for i in range(HT):
                p.indirect_dma_start(gat_parts[:, par, i, :, :].rearrange("p k f -> p (k f)"), None, node_parts,
                                     bass.IndirectOffsetOnAxis(ap=gat_idx[:, par, i:i + 1], axis=0)
                                     ).then_inc(gathered[par], 16)

        def scatter(h, par, first):
            p.wait_ge(sum_sb, h + 2)
            p.wait_ge(target_ready, h + 1)
            for g in range(2):
                if not first:
                    p.wait_ge(added[g], h * ADDS)
                p.sem_inc(pool_passed, 1)
                for i in range(HT // 2 * g, HT // 2 * (g + 1)):
                    p.indirect_dma_start(msg_acc[i], bass.IndirectOffsetOnAxis(ap=target[:, par, i:i + 1], axis=0),
                                         sums[:, par, i, :], None, compute_op=ALU.add
                                         ).then_inc(added[g], 16)
        gather(0, 0, True)
        gather(1, 1, True)
        scatter(0, 0, True)
        with p.Fori(1, NB) as b:
            gather(2 * b, 0, False)
            scatter(2 * b - 1, 1, False)
            gather(2 * b + 1, 1, False)
            scatter(2 * b, 0, False)
        scatter(NH - 1, 1, False)
        for g in range(2):
            p.wait_ge(added[g], NH * ADDS)

    def tensor(t):
        def front(h, par, first, b):
            t.wait_ge(loads[par], 48 * b + 48)
            if not (first and par == 0):
                t.wait_ge(attr_sb, h)
            for k in range(HT // 2):
                m = t.transpose(ps_attr[0:2 * R, TE * k:TE * k + TE],
                                attr[:, par, 2 * k:2 * k + 2, :].rearrange("p a r -> p (a r)"), ident[0:TE, 0:TE])
            m.then_inc(attr_read, 1)
            t.wait_ge(attr_sb, h + 1)
            if not (first and par == 0):
                t.wait_ge(hid_sb, h)
            t.matmul(ps_hid[0:2 * H, 0:HE // 2], w1_pair[:, :], attr_t[:, :], start=True, stop=True
                     ).then_inc(hid_mm, 1)
            t.wait_ge(hi_onehot, h + 1)
            if not first:
                t.wait_ge(z_read, h - 1)
            for i in range(HT):
                m = t.matmul(ps_z[0:TE, par, LO * i:LO * i + LO], hi_t[:, par, TE * i:TE * i + TE], ntype_bf[:, :],
                             start=True, stop=True)
            m.then_inc(z_mm, 1)
            t.wait_ge(hid_sb, h + 1)
            if not first:
                t.wait_ge(gate_read, h - 1)
            for k in range(HT // 2):
                m = t.matmul(ps_gate[0:TE, par, 2 * H * k:2 * H * k + 2 * H], hid[:, par, TE * k:TE * k + TE],
                             w2_pair[:, :], start=True, stop=True)
            m.then_inc(gate_mm, 1)

        def combine(h, par, first):
            t.wait_ge(same_ready, h + 1)
            t.wait_ge(msg_ready, h + 1)
            if not first:
                t.wait_ge(sum_sb, h)
            for i in range(HT):
                m = t.matmul(ps_sum[0:TE, par, (H + 1) * i:(H + 1) * (i + 1)], same[:, par, i, :],
                             msg[:, par, i, :], start=True, stop=True)
            m.then_inc(sum_mm, 1)
        t.sem_inc(sum_sb, 1)
        front(0, 0, True, 0)
        front(1, 1, True, 0)
        combine(0, 0, True)
        with t.Fori(1, NB) as b:
            front(2 * b, 0, False, b)
            combine(2 * b - 1, 1, False)
            front(2 * b + 1, 1, False, b)
            combine(2 * b, 0, False)
        combine(NH - 1, 1, False)

    def scalar(a):
        def front(h, par, first):
            a.wait_ge(attr_read, h + 1)
            if not (first and par == 0):
                a.wait_ge(hid_mm, h)
            a.activation(attr_t[:, :], ps_attr[0:2 * R, 0:HE // 2], ACT.Copy).then_inc(attr_sb, 1)
            a.wait_ge(hid_mm, h + 1)
            if not first:
                a.wait_ge(gate_mm, h - 1)
            a.activation(hid[0:2 * H, par, :], ps_hid[0:2 * H, 0:HE // 2], ACT.Silu, bias=b1_pair[:, :]
                         ).then_inc(hid_sb, 1)

        def back(h, par):
            a.wait_ge(sum_mm, h + 1)
            a.wait_ge(target_ready, h + 1)
            a.activation(sums[0:TE, par, :, :], ps_sum[0:TE, par, 0:HT * (H + 1)]
                         .rearrange("p (i f) -> p i f", f=H + 1), ACT.Copy).then_inc(sum_sb, 1)
        front(0, 0, True)
        front(1, 1, True)
        back(0, 0)
        with a.Fori(1, NB) as b:
            front(2 * b, 0, False)
            back(2 * b - 1, 1)
            front(2 * b + 1, 1, False)
            back(2 * b, 0)
        back(NH - 1, 1)

    def vector(v):
        v.memset(hid[2 * H:2 * H + 1, :, :], 1.0)
        v.memset(sums[:, :, :, :], 0.0)
        link(v.tensor_scalar(target[:, :, :].rearrange("p a i -> p (a i)"), zeros[:, 0:2 * HT], trash[:, :], None, ALU.add))
        link(v.tensor_scalar(src_less[:, :], src_c[:, :], trash[0:TE, :], None, ALU.subtract))

        def half(h, par, first, b):
            n = [0]

            def inner(ins):
                n[0] += 1
                ins.then_inc(dve_half, 1)
                v.wait_ge(dve_half, h * LINKS + n[0])
            v.wait_ge(loads[par], 48 * b + 48)
            if not first:
                v.wait_ge(z_mm, h - 1)
            v.tensor_scalar(hi_t[:, par, :], hib[:, par, :], part_idx[0:TE, :], None, ALU.is_equal
                            ).then_inc(hi_onehot, 1)
            if not first:
                v.wait_ge(sum_mm, h - 1)
            for i in range(HT):
                m = v.scalar_tensor_tensor(same[:, par, i, :], key_rows[:, par, TE * i:TE * i + TE],
                                           src_c[:, bass.ds(h * HT + i, 1)], tri[0:TE, :], ALU.is_equal,
                                           ALU.mult, accum_out=count[:, par, i:i + 1])
            m.then_inc(same_ready, 1)
            v.wait_ge(same_ready, h + 1)
            inner(v.scalar_tensor_tensor(firsts[:, par, :], count[:, par, :], 1.0, cols(src_less, h), ALU.is_equal,
                                         ALU.mult))
            if not first:
                for g in range(2):
                    v.wait_ge(added[g], (h - 1) * ADDS)
            v.tensor_scalar(target[0:TE, par, :], firsts[:, par, :], trash[0:TE, :], None, ALU.add
                            ).then_inc(target_ready, 1)
            v.wait_ge(z_mm, h + 1)
            for i in range(HT):
                m = v.scalar_tensor_tensor(junk_lo[:, i, :], free_idx[0:TE, 0:LO], lo_c[:, bass.ds(h * HT + i, 1)],
                                           ps_z[0:TE, par, LO * i:LO * i + LO], ALU.is_equal, ALU.mult,
                                           accum_out=ztype[:, par, i:i + 1])
            m.then_inc(z_read, 1)
            v.wait_ge(z_read, h + 1)
            v.wait_ge(gathered[par], 16 * HT * b + 16 * HT)
            inner(v.tensor_tensor(gat[:, par, :, :], gat_parts[0:TE, par, :, 0, :], gat_parts[0:TE, par, :, 1, :], ALU.add))
            inner(v.tensor_tensor(gat[:, par, :, :], gat[:, par, :, :], gat_parts[0:TE, par, :, 2, :], ALU.add))
            for i in range(HT):
                m = v.scalar_tensor_tensor(junk_z[:, i, :], free_idx[0:TE, 0:NEL], ztype[:, par, i:i + 1],
                                           gat[0:TE, par, i, H + 1:GW], ALU.is_equal, ALU.mult,
                                           accum_out=adapt[:, par, i:i + 1])
            inner(m)
            v.wait_ge(gate_mm, h + 1)
            for i in range(HT):
                m = v.scalar_tensor_tensor(raw[:, i, :], ps_gate[0:TE, par, H * i:H * i + H], adapt[:, par, i:i + 1],
                                           gat[0:TE, par, i, 0:H], ALU.add, ALU.mult)
            m.then_inc(gate_read, 1)
            v.wait_ge(gate_read, h + 1)
            v.tensor_copy(msg[:, par, :, H:H + 1], gat[0:TE, par, :, H:H + 1])
            inner(v.tensor_tensor(msg[:, par, :, 0:H], raw[:, :, :],
                                  cols(cw_c, h).unsqueeze(2).to_broadcast([TE, HT, H]), ALU.mult))
            v.sem_inc(msg_ready, 1)
            assert n[0] == LINKS
        half(0, 0, True, 0)
        half(1, 1, True, 0)
        with v.Fori(1, NB) as b:
            half(2 * b, 0, False, b)
            half(2 * b + 1, 1, False, b)
    mine.close()
    return {"sync": sync, "gpsimd": gpsimd, "tensor": tensor, "scalar": scalar, "vector": vector}


def propagate_edges(nc, env):
    (sem, root, link, bc, cols) = (env[k] for k in ("sem", "root", "link", "bc", "cols"))
    (dst_c, dst_rows, src_i, prop_acc, y_tab, zeros, tri, trash, xn, hn, dinv, stat, out) = (
        env[k] for k in ("dst_c", "dst_rows", "src_i", "prop_acc", "y_tab", "zeros", "tri", "trash", "xn",
                         "hn", "dinv", "stat", "out"))
    NH = 2 * NB
    QT = HT // 4
    mine = ExitStack()

    def sb(name, shape, dt=F32):
        return mine.enter_context(nc.sbuf_tensor(name, shape, dt))
    key_rows = sb("e_key_rows", [TE, 2, HE], I16)
    same = sb("e_same", [TE, 2, HT, TE])
    count, firsts = sb("e_count", [TE, 2, HT]), sb("e_firsts", [TE, 2, HT])
    target, gat_idx = sb("e_target", [P, 2, HT], I32), sb("e_gat_idx", [P, 2, HT], I32)
    gat_y, sums_y = sb("e_gat_y", [P, 2, HT, H]), sb("e_sums_y", [P, 2, HT, H])
    dst_less = sb("e_dst_less", [TE, T])
    ps_sum = mine.enter_context(nc.psum_tensor("e_ps_sum", [P, 2, 512], F32))
    yn = mine.enter_context(nc.sbuf_tensor("yn_e", [TE, LO, H], F32))
    acc = mine.enter_context(nc.sbuf_tensor("acc_e", [TE, LO, H], F32))
    tabs = mine.enter_context(nc.sbuf_tensor("tabs_e", [TE, 2, LO, H], F32))
    keys = [sem("keys_even"), sem("keys_odd")]
    same_ready, sum_mm, sum_sb = sem("p_same_ready"), sem("p_sum_mm"), sem("p_sum_sb")
    gathered = [[sem(f"p_gathered_{x}{q}") for q in range(4)] for x in ("even", "odd")]
    idx_copied, target_ready, pool_passed = sem("p_idx_copied"), sem("p_target_ready"), sem("p_pool_passed")
    added = [sem(f"p_added{q}") for q in range(4)]
    tabs_in, tab_read = [sem("p_tabs_even"), sem("p_tabs_odd")], sem("p_tab_read")
    y_ready, y_stored, rezeroed, node_step, first_ready, stored, out_ready = (
        sem("y_ready"), sem("y_stored"), sem("rezeroed"), sem("node_step"), sem("first_ready"), sem("stored"),
        sem("out_ready"))
    NODE = 5

    def sync(sp):
        def edges(s):
            def load(h, par, first):
                if not first:
                    sp.wait_ge(same_ready, s * NH + h - 1)
                    sp.sem_inc(env["sp_passed"], 1)
                sp.dma_start(key_rows[:, par, :], dst_rows[bass.ds(h * HT, HT), :].rearrange("t e -> (t e)")
                             .partition_broadcast(TE)).then_inc(keys[par], 16)
            load(0, 0, True)
            load(1, 1, True)
            with sp.Fori(1, NB) as b:
                load(2 * b, 0, False)
                load(2 * b + 1, 1, False)

        def between(s):
            for q in range(4):
                sp.wait_ge(added[q], (s + 1) * (NH * 16 * QT))
                sp.sem_inc(env["sp_passed"], 1)
            for i in range(NTAB):
                if i >= 2:
                    sp.wait_ge(tab_read, s * NTAB + i - 1)
                    sp.sem_inc(env["sp_passed"], 1)
                sp.dma_start(tabs[:, i % 2, :, :], prop_acc[i][0:N, :].rearrange("(j p) f -> p j f", p=TE)
                             ).then_inc(tabs_in[i % 2], 16)
            for i in range(2):
                sp.wait_ge(tabs_in[i], (s + 1) * (16 * NTAB // 2))
                sp.sem_inc(env["sp_passed"], 1)
            for t in prop_acc:
                sp.dma_start(t.rearrange("(p r) f -> p (r f)", p=P), zeros[:, 0:ACC_ROWS // P * H]
                             ).then_inc(rezeroed, 16)
            sp.wait_ge(y_ready, s + 2)
            sp.sem_inc(env["sp_passed"], 1)
            sp.dma_start(y_tab.rearrange("(j p) f -> p j f", p=TE), yn[:, :, :]).then_inc(y_stored, 16)
            sp.wait_ge(rezeroed, (s + 2) * (16 * NTAB))
            sp.wait_ge(y_stored, s * 16 + 32)
            sp.sem_inc(env["sp_passed"], 1)
        for t in prop_acc:
            sp.dma_start(t.rearrange("(p r) f -> p (r f)", p=P), zeros[:, 0:ACC_ROWS // P * H]).then_inc(rezeroed, 16)
        sp.wait_ge(y_ready, 1)
        sp.dma_start(y_tab.rearrange("(j p) f -> p j f", p=TE), yn[:, :, :]).then_inc(y_stored, 16)
        edges(0)
        between(0)
        with sp.Fori(1, K + 1) as s:
            edges(s)
            between(s)
        sp.wait_ge(out_ready, 1)
        sp.dma_start(out.rearrange("(j p) f -> p j f", p=TE), xn[:, :, :]).then_inc(stored, 16)
        sp.wait_ge(stored, 16)

    def gpsimd(p):
        def edges(s):
            p.wait_ge(y_stored, s * 16 + 16)
            p.wait_ge(rezeroed, (s + 1) * (16 * NTAB))

            def gather(h, par, first):
                g = s * NH + h
                if not first:
                    p.wait_ge(sum_mm, g - 1)
                p.sem_inc(pool_passed, 1)
                p.tensor_copy(gat_idx[:, par, :], cols(src_i, h, P)).then_inc(idx_copied, 1)
                p.wait_ge(idx_copied, g + 1)
                p.sem_inc(pool_passed, 1)
                for i in range(HT):
                    p.indirect_dma_start(gat_y[:, par, i, :], None, y_tab,
                                         bass.IndirectOffsetOnAxis(ap=gat_idx[:, par, i:i + 1], axis=0)
                                         ).then_inc(gathered[par][i // QT], 16)

            def scatter(h, par, first):
                g = s * NH + h
                p.wait_ge(sum_sb, g + 2)
                p.wait_ge(target_ready, g + 1)
                for q in range(4):
                    if not first:
                        p.wait_ge(added[q], g * (16 * QT))
                    p.sem_inc(pool_passed, 1)
                    for i in range(QT * q, QT * (q + 1)):
                        p.indirect_dma_start(prop_acc[i], bass.IndirectOffsetOnAxis(ap=target[:, par, i:i + 1], axis=0),
                                             sums_y[:, par, i, :], None, compute_op=ALU.add
                                             ).then_inc(added[q], 16)
            gather(0, 0, True)
            gather(1, 1, True)
            scatter(0, 0, True)
            with p.Fori(1, NB) as b:
                gather(2 * b, 0, False)
                scatter(2 * b - 1, 1, False)
                gather(2 * b + 1, 1, False)
                scatter(2 * b, 0, False)
            scatter(NH - 1, 1, False)
        edges(0)
        with p.Fori(1, K + 1) as s:
            edges(s)

    def tensor(t):
        def edges(s):
            def combine(h, par, b, first):
                g = s * NH + h
                t.wait_ge(same_ready, g + 1)
                for q in range(4):
                    t.wait_ge(gathered[par][q], (s * NB + b + 1) * (16 * QT))
                if not first:
                    t.wait_ge(sum_sb, g)
                for i in range(HT):
                    m = t.matmul(ps_sum[0:TE, par, H * i:H * (i + 1)], same[:, par, i, :], gat_y[0:TE, par, i, :],
                                 start=True, stop=True)
                m.then_inc(sum_mm, 1)
            combine(0, 0, 0, True)
            combine(1, 1, 0, True)
            with t.Fori(1, NB) as b:
                combine(2 * b, 0, b, False)
                combine(2 * b + 1, 1, b, False)
        t.sem_inc(sum_sb, 1)
        edges(0)
        with t.Fori(1, K + 1) as s:
            edges(s)

    def scalar(a):
        def edges(s):
            def back(h, par):
                a.wait_ge(sum_mm, s * NH + h + 1)
                a.wait_ge(target_ready, s * NH + h + 1)
                a.activation(sums_y[0:TE, par, :, :], ps_sum[0:TE, par, 0:HT * H]
                             .rearrange("p (i f) -> p i f", f=H), ACT.Copy).then_inc(sum_sb, 1)
            with a.Fori(0, NB) as b:
                back(2 * b, 0)
                back(2 * b + 1, 1)
        edges(0)
        root(a, 5)
        with a.Fori(1, K + 1) as s:
            edges(s)

    def vector(v):
        def edges(s):
            def half(h, par, first):
                g = s * NH + h
                v.wait_ge(keys[par], (s * NH + (h - par)) * 8 + 16)
                if not first:
                    v.wait_ge(sum_mm, g - 1)
                for i in range(HT):
                    m = v.scalar_tensor_tensor(same[:, par, i, :], key_rows[:, par, TE * i:TE * i + TE],
                                               dst_c[:, bass.ds(h * HT + i, 1)], tri[0:TE, :], ALU.is_equal,
                                               ALU.mult, accum_out=count[:, par, i:i + 1])
                m.then_inc(same_ready, 1)
                v.wait_ge(same_ready, g + 1)
                v.scalar_tensor_tensor(firsts[:, par, :], count[:, par, :], 1.0, cols(dst_less, h), ALU.is_equal,
                                       ALU.mult).then_inc(first_ready, 1)
                v.wait_ge(first_ready, g + 1)
                if not first:
                    for q in range(4):
                        v.wait_ge(added[q], (g - 1) * (16 * QT))
                v.tensor_scalar(target[0:TE, par, :], firsts[:, par, :], trash[0:TE, :], None, ALU.add
                                ).then_inc(target_ready, 1)
            half(0, 0, True)
            half(1, 1, True)
            with v.Fori(1, NB) as b:
                half(2 * b, 0, False)
                half(2 * b + 1, 1, False)

        def collect(s):
            for i in range(NTAB):
                v.wait_ge(tabs_in[i % 2], s * (16 * NTAB // 2) + 16 * (i // 2 + 1))
                if i == 0:
                    m = v.tensor_copy(acc[:, :, :], tabs[:, 0, :, :])
                else:
                    v.wait_ge(tab_read, s * NTAB + i)
                    m = v.tensor_tensor(acc[:, :, :], acc[:, :, :], tabs[:, i % 2, :, :], ALU.add)
                m.then_inc(tab_read, 1)
            v.wait_ge(tab_read, s * NTAB + NTAB)

        v.memset(sums_y[:, :, :, :], 0.0)
        link(v.tensor_scalar(target[:, :, :].rearrange("p a i -> p (a i)"), zeros[:, 0:2 * HT], trash[:, :], None,
                             ALU.add))
        link(v.tensor_scalar(dst_less[:, :], dst_c[:, :], trash[0:TE, :], None, ALU.subtract))
        v.memset(yn[:, :, :], 1.0).then_inc(y_ready, 1)
        edges(0)
        collect(0)
        link(v.tensor_scalar(stat[:, 0, :].unsqueeze(2), acc[:, :, 0:1], 1.0, None, ALU.add))
        v.sem_inc(env["root_asked"], 1)
        v.wait_ge(env["root_done"], 5)
        link(v.reciprocal(dinv[:, :], stat[:, 1, :]))
        v.wait_ge(y_stored, 16)
        v.tensor_tensor(yn[:, :, :], hn[:, :, :], bc(dinv[:, :]), ALU.mult).then_inc(y_ready, 1)
        with v.Fori(1, K + 1) as s:
            edges(s)
            collect(s)
            n = [0]

            def step(ins):
                n[0] += 1
                ins.then_inc(node_step, 1)
                v.wait_ge(node_step, (s - 1) * NODE + n[0])
            step(v.tensor_tensor(acc[:, :, :], acc[:, :, :], yn[:, :, :], ALU.add))
            step(v.tensor_tensor(acc[:, :, :], acc[:, :, :], bc(dinv[:, :]), ALU.mult))
            step(v.tensor_scalar(acc[:, :, :], acc[:, :, :], 1.0 - ALPHA, None, ALU.mult))
            step(v.scalar_tensor_tensor(acc[:, :, :], hn[:, :, :], ALPHA, acc[:, :, :], ALU.mult, ALU.add))
            v.wait_ge(y_stored, s * 16 + 16)
            step(v.tensor_tensor(yn[:, :, :], acc[:, :, :], bc(dinv[:, :]), ALU.mult))
            v.sem_inc(y_ready, 1)
            assert n[0] == NODE
        v.tensor_tensor(xn[:, :, :], xn[:, :, :], acc[:, :, :], ALU.add).then_inc(out_ready, 1)
    mine.close()
    return {"sync": sync, "gpsimd": gpsimd, "tensor": tensor, "scalar": scalar, "vector": vector}


def propagate_counts(nc, env):
    sem, link, bc = env["sem"], env["link"], env["bc"]
    counts, xn, hn, dinv, out = (env[k] for k in ("counts", "xn", "hn", "dinv", "out"))
    mine = ExitStack()

    def sb(name, shape, dt=F32):
        return mine.enter_context(nc.sbuf_tensor(name, shape, dt))
    RING = 5
    PARTS = ((0, 3), (3, 5))
    IT = LO // RING
    CH = TE * LO
    KEPT = 2
    chunk = sb("chunk", [TE, RING, TE, LO], F8)
    kept = sb("kept", [TE, KEPT * RING, TE, LO], F8)
    HI, LOW = 16.0, 1024.0
    y_parts = sb("y_parts", [TE, 2, LO, 2 * H], F16)
    yn = sb("yn", [TE, LO, H])
    more = sb("more", [TE, LO, H])
    scale = sb("scale", [TE, 2, LO])
    t1, t2 = sb("t1", [TE, 3, H]), sb("t2", [TE, 3, H])
    ps = mine.enter_context(nc.psum_tensor("ps_prop", [P, RING, 512], F32))
    kept_in = [sem(f"kept_in{i}") for i in range(KEPT)]
    chunk_in = [sem(f"chunk_in{i}") for i in range(RING)]
    chunk_mm, ps_read, y_ready, c_step, out_ready, out_stored = (
        sem("chunk_mm"), sem("ps_read"), sem("c_y_ready"), sem("c_step"), sem("c_out_ready"), sem("c_out_stored"))
    NP = len(PARTS) * IT
    LINKS, LAST_LINKS = 5, 2

    def sync(sp):
        def load(step, it, last_use):
            for i in range(RING):
                if last_use is not None:
                    sp.wait_ge(chunk_mm, (last_use - 1) * RING + i + 1)
                    sp.sem_inc(env["sp_passed"], 1)
                sp.dma_start(chunk[:, i, :, :].rearrange("p m j -> p (m j)").bitcast(I16),
                             counts[0:TE, bass.ds(it * (RING * CH // 2) + i * (CH // 2), CH // 2)]
                             ).then_inc(chunk_in[i], 16)
        for it in range(KEPT):
            for i in range(RING * it, RING * it + RING):
                sp.dma_start(kept[:, i, :, :].rearrange("p m j -> p (m j)").bitcast(I16),
                             counts[0:TE, i * (CH // 2):(i + 1) * (CH // 2)]).then_inc(kept_in[it], 16)
        load(0, KEPT, None)
        with sp.Fori(KEPT + 1, IT) as it:
            load(0, it, it)
        with sp.Fori(1, K) as step:
            load(step, KEPT, step * IT)
            with sp.Fori(KEPT + 1, IT) as it:
                load(step, it, step * IT + it)
        sp.wait_ge(out_ready, NP)
        sp.dma_start(out.rearrange("(j p) f -> p j f", p=TE), yn[:, :, :]).then_inc(out_stored, 16)
        sp.wait_ge(out_stored, 16)

    def tensor(t):
        def chunks(step, par, it, first, start, stay=False):
            n = step * IT + it
            for i in range(RING):
                part = 0 if i < PARTS[0][1] else 1
                if stay:
                    t.wait_ge(kept_in[it], 16 * RING)
                else:
                    t.wait_ge(chunk_in[i], (step * (IT - KEPT) + it - KEPT) * 16 + 16)
                if not first:
                    t.wait_ge(ps_read, (n - 1) * 2 + part + 1)
                t.sem_inc(env["pe_passed"], 1)
                for j in range(LO):
                    if start and i == 0 and j % RING in (PARTS[0][0], PARTS[1][0]):
                        t.wait_ge(y_ready, step * NP + j // RING * 2 + (j % RING > 0) + 1)
                        t.sem_inc(env["pe_passed"], 1)
                    a = kept[:, it * RING + i, :, j] if stay else chunk[:, i, :, j]
                    m = t.matmul(ps[0:TE, i, 0:2 * H], a, y_parts[:, par, j, :], start=(j == 0),
                                 stop=(j == LO - 1))
                m.then_inc(chunk_mm, 1)

        def one_step(step, par, first):
            for it in range(KEPT):
                chunks(step, par, it, first and it == 0, it == 0, True)
            with t.Fori(KEPT, IT) as it:
                chunks(step, par, it, False, False)
        one_step(0, 0, True)
        with t.Fori(0, (K - 1) // 2) as pair:
            one_step(2 * pair + 1, 1, False)
            one_step(2 * pair + 2, 0, False)

    def vector(v):
        def split(par, q, n, link_to):
            at = bass.ds(q, n)
            hi, lo = (y_parts[:, par, at, H * k:H * k + H] for k in range(2))
            link_to(v.tensor_copy(hi, yn[:, at, :]))
            link_to(v.tensor_tensor(t1[:, 0:n, :], yn[:, at, :], hi, ALU.subtract))
            return v.tensor_scalar(lo, t1[:, 0:n, :], LOW, None, ALU.mult)

        def parts(step, par, it, last):
            for part, (a, b) in enumerate(PARTS):
                n, count = b - a, [0]
                number = (step * IT + it) * 2 + part
                q = it * RING + a
                at = bass.ds(q, n)

                def inner(ins):
                    count[0] += 1
                    ins.then_inc(c_step, 1)
                    v.wait_ge(c_step, (K - 1) * NP * LINKS + (it * 2 + part) * LAST_LINKS + count[0] if last
                              else number * LINKS + count[0])
                v.wait_ge(chunk_mm, (step * IT + it) * RING + b)
                inner(v.tensor_tensor(t1[:, 0:n, :], ps[0:TE, a:b, 0:H], yn[:, at, :], ALU.add))
                v.scalar_tensor_tensor(t2[:, 0:n, :], ps[0:TE, a:b, H:2 * H], 1.0 / LOW, t1[:, 0:n, :], ALU.mult, ALU.add
                                       ).then_inc(ps_read, 1)
                v.wait_ge(ps_read, number + 1)
                inner(v.tensor_tensor(t1[:, 0:n, :], t2[:, 0:n, :],
                                      scale[:, int(last), at].unsqueeze(2).to_broadcast([TE, n, H]), ALU.mult))
                if last:
                    v.tensor_tensor(yn[:, at, :], t1[:, 0:n, :], more[:, at, :], ALU.add).then_inc(out_ready, 1)
                    v.wait_ge(out_ready, it * 2 + part + 1)
                    assert count[0] == LAST_LINKS
                else:
                    inner(v.tensor_tensor(yn[:, at, :], t1[:, 0:n, :], more[:, at, :], ALU.add))
                    split(1 - par, q, n, inner).then_inc(y_ready, 1)
                    v.wait_ge(y_ready, (step + 1) * NP + it * 2 + part + 1)
                    assert count[0] == LINKS

        link(v.tensor_tensor(scale[:, 0, :], dinv[:, :], dinv[:, :], ALU.mult))
        link(v.tensor_scalar(scale[:, 0, :], scale[:, 0, :], 1.0 - ALPHA, None, ALU.mult))
        link(v.tensor_scalar(scale[:, 1, :], dinv[:, :], (1.0 - ALPHA) / HI, None, ALU.mult))
        link(v.tensor_tensor(yn[:, :, :], hn[:, :, :], bc(dinv[:, :]), ALU.mult))
        link(v.tensor_scalar(yn[:, :, :], yn[:, :, :], HI, None, ALU.mult))
        for it in range(IT):
            for a, b in PARTS:
                split(0, RING * it + a, b - a, link).then_inc(y_ready, 1)
                v.wait_ge(y_ready, it * 2 + (a > 0) + 1)
        link(v.tensor_scalar(more[:, :, :], yn[:, :, :], ALPHA, None, ALU.mult))

        def one_step(step, par):
            with v.Fori(0, IT) as it:
                parts(step, par, it, False)
        with v.Fori(0, (K - 1) // 2) as pair:
            one_step(2 * pair, 0)
            one_step(2 * pair + 1, 1)
        link(v.scalar_tensor_tensor(more[:, :, :], hn[:, :, :], ALPHA, xn[:, :, :], ALU.mult, ALU.add))
        with v.Fori(0, IT) as it:
            parts(K - 1, 0, it, True)

    def scalar(a):
        pass

    def gpsimd(p):
        pass
    mine.close()
    return {"sync": sync, "gpsimd": gpsimd, "tensor": tensor, "scalar": scalar, "vector": vector}


_INS = ['x', 'src', 'dst', 'edge_attr_40', 'edge_weight', 'node_type_119', 'node_vec', 'L0_gnn_W1', 'L0_gnn_b1',
        'L0_gnn_W2', 'L0_gnn_b2', 'L0_gnn_emb', 'L0_gnn_adaptW', 'L0_gnn_gamma', 'L0_gnn_beta']
_OUTS = [((N, H), 'float32')]


def kernel(**inputs):
    import numpy as _np
    import concourse.bacc as _bacc
    from concourse import mybir as _mybir
    from concourse.bass_utils import run_bass_kernel_spmd as _run

    nc = _bacc.Bacc("TRN2", target_bir_lowering=False, num_devices=1)
    arrays, args = {}, []
    for name in _INS:
        a = _np.ascontiguousarray(inputs[name])
        arrays[f"in_{name}_dram"] = a
        args.append(nc.dram_tensor(f"in_{name}_dram", a.shape, _mybir.dt.from_np(a.dtype), kind="ExternalInput").ap())
    for i, (shape, dtype) in enumerate(_OUTS):
        dt = _mybir.dt.from_np(_np.dtype(dtype))
        args.append(nc.dram_tensor(f"out_{i}_dram", shape, dt, kind="ExternalOutput").ap())
    build(nc, *args)
    r = _run(nc, [arrays], core_ids=[0])
    got = tuple(r.results[0][f"out_{i}_dram"] for i in range(len(_OUTS)))
    return got[0]
```
